# Optimizing a Trainium2 kernel written in Bass

```python
import numpy as np
import jax
import jax.numpy as jnp

def _softmax(x, axis=-1):
    return jax.nn.softmax(x, axis=axis)

def _gelu(x):
    return jax.nn.gelu(x, approximate=True)

def _silu(x):
    return jax.nn.silu(x)

def _sigmoid(x):
    return jax.nn.sigmoid(x)

def _layernorm(x, axis=-1, eps=1e-05):
    m = jnp.mean(x, axis=axis, keepdims=True)
    v = jnp.var(x, axis=axis, keepdims=True)
    return (x - m) / jnp.sqrt(v + eps)

def _scatter_add(tgt, idx, src, axis=0):
    return tgt.at[idx].add(src)

def _segment_sum(src, seg, n):
    return jax.ops.segment_sum(src, seg, n)
kernel_name = 'mk_prb_d2_jaxref_r8_e49c5f'

def setup_inputs(seed: int=0):
    np.random.seed(seed)
    _w = jnp.asarray

    def _L0_attn_setup():
        import jax, jax.numpy as jnp
        import numpy as np
        DIM = 128
        N_HEADS = 16
        HEAD_DIM = DIM // N_HEADS
        SCALE = HEAD_DIM ** (-0.5)
        key = jax.random.key(seed)
        k1, k2, k3 = jax.random.split(key, 3)
        x = jax.random.normal(k1, (4, 256, DIM), dtype=jnp.float32)
        w_qkv = jax.random.normal(k2, (DIM, 3 * DIM), dtype=jnp.float32) * DIM ** (-0.5)
        w_proj = jax.random.normal(k3, (DIM, DIM), dtype=jnp.float32) * DIM ** (-0.5)
        b_proj = jnp.zeros((DIM,), dtype=jnp.float32)
        return {'x': x, 'w_qkv': w_qkv, 'w_proj': w_proj, 'b_proj': b_proj}
    _L0_attn_in = _L0_attn_setup()

    def _L0_ffn_setup():
        import jax, jax.numpy as jnp
        import numpy as np
        TAU = 1.0
        K_ROUTE = 3
        EPS = 1e-08

        def _route_combine_weights(x_addr, U, k, tau):
            z = x_addr @ U.T
            topv, topi = jax.lax.top_k(z, k)
            w = jax.nn.softmax(topv / (tau + EPS), axis=1)
            N, L = z.shape
            rows = jnp.arange(N)[:, None]
            return jnp.zeros((N, L), z.dtype).at[rows, topi].add(w)

        def _mixture(inp, C, W):
            L = W.shape[0]
            y = jnp.zeros((inp.shape[0], W.shape[1]), inp.dtype)
            for e in range(L):
                y = y + C[:, e:e + 1] * (inp @ W[e].T)
            return y
        key = jax.random.key(seed)
        ks = jax.random.split(key, 8)
        B, T, D_in, H, D_out, L, d_addr = (8, 1024, 128, 128, 128, 12, 64)

        def unit_rows(k, L_, d_):
            U = jax.random.normal(k, (L_, d_), dtype=jnp.float32)
            U = U - U.mean(axis=1, keepdims=True)
            return U / (jnp.linalg.norm(U, axis=1, keepdims=True) + EPS)

        def norm_tape(k, shape):
            W = jax.random.normal(k, shape, dtype=jnp.float32)
            n = jnp.sqrt(jnp.sum(W * W, axis=tuple(range(1, W.ndim)), keepdims=True)) + 1e-12
            return W / n
        x = jax.random.normal(ks[0], (B, T, D_in), dtype=jnp.float32)
        P_w = jax.random.normal(ks[1], (d_addr, D_in), dtype=jnp.float32) / np.sqrt(D_in)
        U1 = unit_rows(ks[2], L, d_addr)
        U2 = unit_rows(ks[3], L, d_addr)
        U3 = unit_rows(ks[4], L, d_addr)
        W1 = norm_tape(ks[5], (L, H, D_in))
        W2 = norm_tape(ks[6], (L, D_out, H))
        b2 = norm_tape(ks[7], (L, D_out))
        return {'x': x, 'P_w': P_w, 'U1': U1, 'U2': U2, 'U3': U3, 'W1': W1, 'W2': W2, 'b2': b2}
    _L0_ffn_in = _L0_ffn_setup()

    def _L1_attn_setup():
        import jax, jax.numpy as jnp
        import numpy as np
        D_MODEL = 128
        NHEAD = 16
        HEAD_DIM = D_MODEL // NHEAD
        NPOS_MAX = 125
        SEQ = 128
        BATCH = 4

        def _cope(query, attn_logits, pos_emb):
            gates = jax.nn.sigmoid(attn_logits)
            pos = jnp.cumsum(gates[..., ::-1], axis=-1)[..., ::-1]
            pos = jnp.minimum(pos, NPOS_MAX - 1)
            pos_ceil = jnp.ceil(pos).astype(jnp.int32)
            pos_floor = jnp.floor(pos).astype(jnp.int32)
            logits_int = jnp.einsum('hbsd,dn->hbsn', query, pos_emb[0])
            logits_ceil = jnp.take_along_axis(logits_int, pos_ceil, axis=-1)
            logits_floor = jnp.take_along_axis(logits_int, pos_floor, axis=-1)
            w = pos - pos_floor.astype(pos.dtype)
            return logits_ceil * w + logits_floor * (1.0 - w)
        key = jax.random.key(seed)
        ks = jax.random.split(key, 10)
        s = 0.02
        return {'x': jax.random.normal(ks[0], (SEQ, BATCH, D_MODEL), dtype=jnp.float32), 'Wq': jax.random.normal(ks[1], (D_MODEL, D_MODEL), dtype=jnp.float32) * s, 'bq': jnp.zeros((D_MODEL,), dtype=jnp.float32), 'Wk': jax.random.normal(ks[2], (D_MODEL, D_MODEL), dtype=jnp.float32) * s, 'bk': jnp.zeros((D_MODEL,), dtype=jnp.float32), 'Wv': jax.random.normal(ks[3], (D_MODEL, D_MODEL), dtype=jnp.float32) * s, 'bv': jnp.zeros((D_MODEL,), dtype=jnp.float32), 'Wo': jax.random.normal(ks[4], (D_MODEL, D_MODEL), dtype=jnp.float32) * s, 'bo': jnp.zeros((D_MODEL,), dtype=jnp.float32), 'pos_emb': jax.random.normal(ks[5], (1, HEAD_DIM, NPOS_MAX), dtype=jnp.float32) * s}
    _L1_attn_in = _L1_attn_setup()

    def _L1_ffn_setup():
        import jax, jax.numpy as jnp
        import numpy as np
        D_MODEL = 128
        HIDDEN = 256
        E_ROUTED = 14
        E_SHARED = 2
        TOP_K = 2
        EPS = 1e-09
        RMS_EPS = 1.1920929e-07

        def _ffn(xn, rw, W1, W2):
            ms = jnp.mean(xn * xn, axis=-1, keepdims=True)
            h = xn * jax.lax.rsqrt(ms + RMS_EPS) * rw
            return jax.nn.silu(h @ W1) @ W2
        key = jax.random.key(seed)
        ks = jax.random.split(key, 9)
        B, T = (2, 128)
        x = jax.random.normal(ks[0], (B, T, D_MODEL), dtype=jnp.float32)
        router_w = jax.random.normal(ks[1], (D_MODEL, E_ROUTED), dtype=jnp.float32) * 0.006
        rms_w = jnp.ones((E_ROUTED, D_MODEL), dtype=jnp.float32)
        w1 = jax.random.normal(ks[2], (E_ROUTED, D_MODEL, HIDDEN), dtype=jnp.float32) * 0.02
        w2 = jax.random.normal(ks[3], (E_ROUTED, HIDDEN, D_MODEL), dtype=jnp.float32) * 0.02
        rms_w_s = jnp.ones((E_SHARED, D_MODEL), dtype=jnp.float32)
        w1_s = jax.random.normal(ks[4], (E_SHARED, D_MODEL, HIDDEN), dtype=jnp.float32) * 0.02
        w2_s = jax.random.normal(ks[5], (E_SHARED, HIDDEN, D_MODEL), dtype=jnp.float32) * 0.02
        return {'x': x, 'router_w': router_w, 'rms_w': rms_w, 'w1': w1, 'w2': w2, 'rms_w_s': rms_w_s, 'w1_s': w1_s, 'w2_s': w2_s}
    _L1_ffn_in = _L1_ffn_setup()
    _d = {'L0_attn_x': _L0_attn_in['x'], 'L0_attn_w_qkv': _L0_attn_in['w_qkv'], 'L0_attn_w_proj': _L0_attn_in['w_proj'], 'L0_attn_b_proj': _L0_attn_in['b_proj'], 'L0_ffn_P_w': _L0_ffn_in['P_w'], 'L0_ffn_U1': _L0_ffn_in['U1'], 'L0_ffn_U2': _L0_ffn_in['U2'], 'L0_ffn_U3': _L0_ffn_in['U3'], 'L0_ffn_W1': _L0_ffn_in['W1'], 'L0_ffn_W2': _L0_ffn_in['W2'], 'L0_ffn_b2': _L0_ffn_in['b2'], 'L1_attn_Wq': _L1_attn_in['Wq'], 'L1_attn_bq': _L1_attn_in['bq'], 'L1_attn_Wk': _L1_attn_in['Wk'], 'L1_attn_bk': _L1_attn_in['bk'], 'L1_attn_Wv': _L1_attn_in['Wv'], 'L1_attn_bv': _L1_attn_in['bv'], 'L1_attn_Wo': _L1_attn_in['Wo'], 'L1_attn_bo': _L1_attn_in['bo'], 'L1_attn_pos_emb': _L1_attn_in['pos_emb'], 'L1_ffn_router_w': _L1_ffn_in['router_w'], 'L1_ffn_rms_w': _L1_ffn_in['rms_w'], 'L1_ffn_w1': _L1_ffn_in['w1'], 'L1_ffn_w2': _L1_ffn_in['w2'], 'L1_ffn_rms_w_s': _L1_ffn_in['rms_w_s'], 'L1_ffn_w1_s': _L1_ffn_in['w1_s'], 'L1_ffn_w2_s': _L1_ffn_in['w2_s']}
    _x0 = _d['L0_attn_x']
    _d['L0_attn_x'] = jax.random.normal(jax.random.fold_in(jax.random.key(seed), 1), (8, 512, 128), dtype=_x0.dtype)
    del _x0
    return _d

def reference(L0_attn_x, L0_attn_w_qkv, L0_attn_w_proj, L0_attn_b_proj, L0_ffn_P_w, L0_ffn_U1, L0_ffn_U2, L0_ffn_U3, L0_ffn_W1, L0_ffn_W2, L0_ffn_b2, L1_attn_Wq, L1_attn_bq, L1_attn_Wk, L1_attn_bk, L1_attn_Wv, L1_attn_bv, L1_attn_Wo, L1_attn_bo, L1_attn_pos_emb, L1_ffn_router_w, L1_ffn_rms_w, L1_ffn_w1, L1_ffn_w2, L1_ffn_rms_w_s, L1_ffn_w1_s, L1_ffn_w2_s):

    def _L0_attn_ref(x, w_qkv, w_proj, b_proj):
        import jax, jax.numpy as jnp
        import numpy as np
        DIM = 128
        N_HEADS = 16
        HEAD_DIM = DIM // N_HEADS
        SCALE = HEAD_DIM ** (-0.5)
        b, s, d = x.shape
        qkv = (x @ w_qkv).reshape(b, s, 3, N_HEADS, HEAD_DIM)
        q, k, v = jnp.moveaxis(qkv, 2, 0)
        scores = jnp.einsum('bqhd,bkhd->bhqk', q, k) * SCALE
        attn = jax.nn.softmax(scores, axis=-1)
        out = jnp.einsum('bhqk,bkhd->bqhd', attn, v).reshape(b, s, d)
        return out @ w_proj + b_proj

    def _L0_ffn_ref(x, P_w, U1, U2, U3, W1, W2, b2):
        import jax, jax.numpy as jnp
        import numpy as np
        TAU = 1.0
        K_ROUTE = 3
        EPS = 1e-08

        def _route_combine_weights(x_addr, U, k, tau):
            z = x_addr @ U.T
            topv, topi = jax.lax.top_k(z, k)
            w = jax.nn.softmax(topv / (tau + EPS), axis=1)
            N, L = z.shape
            rows = jnp.arange(N)[:, None]
            return jnp.zeros((N, L), z.dtype).at[rows, topi].add(w)

        def _mixture(inp, C, W):
            L = W.shape[0]
            y = jnp.zeros((inp.shape[0], W.shape[1]), inp.dtype)
            for e in range(L):
                y = y + C[:, e:e + 1] * (inp @ W[e].T)
            return y
        B, T, D = x.shape
        xf = x.reshape(B * T, D)
        xa = xf @ P_w.T
        C1 = _route_combine_weights(xa, U1, K_ROUTE, TAU)
        C2 = _route_combine_weights(xa, U2, K_ROUTE, TAU)
        C3 = _route_combine_weights(xa, U3, K_ROUTE, TAU)
        h = jax.nn.gelu(_mixture(xf, C1, W1), approximate=False)
        y = _mixture(h, C2, W2) + C3 @ b2
        return y.reshape(B, T, -1)

    def _L1_attn_ref(x, Wq, bq, Wk, bk, Wv, bv, Wo, bo, pos_emb):
        import jax, jax.numpy as jnp
        import numpy as np
        D_MODEL = 128
        NHEAD = 16
        HEAD_DIM = D_MODEL // NHEAD
        NPOS_MAX = 125
        SEQ = 128
        BATCH = 4

        def _cope(query, attn_logits, pos_emb):
            gates = jax.nn.sigmoid(attn_logits)
            pos = jnp.cumsum(gates[..., ::-1], axis=-1)[..., ::-1]
            pos = jnp.minimum(pos, NPOS_MAX - 1)
            pos_ceil = jnp.ceil(pos).astype(jnp.int32)
            pos_floor = jnp.floor(pos).astype(jnp.int32)
            logits_int = jnp.einsum('hbsd,dn->hbsn', query, pos_emb[0])
            logits_ceil = jnp.take_along_axis(logits_int, pos_ceil, axis=-1)
            logits_floor = jnp.take_along_axis(logits_int, pos_floor, axis=-1)
            w = pos - pos_floor.astype(pos.dtype)
            return logits_ceil * w + logits_floor * (1.0 - w)
        S, B, _ = x.shape

        def split_heads(t):
            return t.reshape(S, B, NHEAD, HEAD_DIM).transpose(2, 1, 0, 3)
        q = split_heads(x @ Wq + bq)
        k = split_heads(x @ Wk + bk)
        v = split_heads(x @ Wv + bv)
        scale = 1.0 / HEAD_DIM ** 0.5
        attn_logits = jnp.einsum('hbsd,hbtd->hbst', q, k) * scale
        attn_logits = attn_logits + _cope(q, attn_logits, pos_emb)
        attn = jax.nn.softmax(attn_logits, axis=-1)
        out = jnp.einsum('hbst,hbtd->hbsd', attn, v)
        out = out.transpose(2, 1, 0, 3).reshape(S, B, D_MODEL)
        return out @ Wo + bo

    def _L1_ffn_ref(x, router_w, rms_w, w1, w2, rms_w_s, w1_s, w2_s):
        import jax, jax.numpy as jnp
        import numpy as np
        D_MODEL = 128
        HIDDEN = 256
        E_ROUTED = 14
        E_SHARED = 2
        TOP_K = 2
        EPS = 1e-09
        RMS_EPS = 1.1920929e-07

        def _ffn(xn, rw, W1, W2):
            ms = jnp.mean(xn * xn, axis=-1, keepdims=True)
            h = xn * jax.lax.rsqrt(ms + RMS_EPS) * rw
            return jax.nn.silu(h @ W1) @ W2
        B, T, D = x.shape
        N = B * T
        xf = x.reshape(N, D)
        gates = jax.nn.softmax(xf @ router_w, axis=-1)
        top_v, top_i = jax.lax.top_k(gates, TOP_K)
        masked = jnp.zeros_like(gates).at[jnp.arange(N)[:, None], top_i].set(top_v)
        masked = masked / (masked.sum(axis=-1, keepdims=True) + EPS)
        routed = jax.vmap(lambda rw_, W1_, W2_: _ffn(xf, rw_, W1_, W2_))(rms_w, w1, w2)
        routed_out = jnp.einsum('end,ne->nd', routed, masked)
        shared = jax.vmap(lambda rw_, W1_, W2_: _ffn(xf, rw_, W1_, W2_))(rms_w_s, w1_s, w2_s).sum(0)
        return (routed_out + shared).reshape(B, T, D)
    x = L0_attn_x
    xn = _layernorm(x, axis=-1)
    x = x + _L0_attn_ref(xn, L0_attn_w_qkv, L0_attn_w_proj, L0_attn_b_proj) + _L0_ffn_ref(xn, L0_ffn_P_w, L0_ffn_U1, L0_ffn_U2, L0_ffn_U3, L0_ffn_W1, L0_ffn_W2, L0_ffn_b2)
    xn = _layernorm(x, axis=-1)
    x = x + _L1_attn_ref(xn, L1_attn_Wq, L1_attn_bq, L1_attn_Wk, L1_attn_bk, L1_attn_Wv, L1_attn_bv, L1_attn_Wo, L1_attn_bo, L1_attn_pos_emb) + _L1_ffn_ref(xn, L1_ffn_router_w, L1_ffn_rms_w, L1_ffn_w1, L1_ffn_w2, L1_ffn_rms_w_s, L1_ffn_w1_s, L1_ffn_w2_s)
    return x

_drawn_inputs = setup_inputs


def setup_inputs(seed=0):
    import zlib

    import numpy as np

    out = dict(_drawn_inputs(seed))
    spreads = {'L0_attn_b_proj': (0.0, 0.1),
     'L1_attn_bq': (0.0, 0.8),
     'L1_attn_bk': (0.0, 2.0),
     'L1_attn_bv': (0.0, 0.332),
     'L1_attn_bo': (0.0, 0.1),
     'L1_ffn_rms_w': (1.0, 0.6),
     'L1_ffn_rms_w_s': (1.0, 0.6)}
    factors = {'L0_ffn_U1': 8.0,
     'L0_ffn_U2': 8.0,
     'L0_ffn_W1': 8.0,
     'L0_ffn_W2': 8.0,
     'L1_attn_Wq': 8.0,
     'L1_attn_Wk': 8.0,
     'L1_attn_Wv': 3.015,
     'L1_attn_pos_emb': 8.0}
    for name, (base, spread) in spreads.items():
        noise = np.random.default_rng([zlib.crc32(name.encode()), seed]).standard_normal(out[name].shape)
        drawn = base * np.exp(spread * noise) if base else spread * noise
        out[name] = jnp.asarray(drawn.astype(out[name].dtype))
    for name, factor in factors.items():
        out[name] = (out[name] * factor).astype(out[name].dtype)
    return out
```

```python
import concourse.bass as bass
from concourse import mybir
from contextlib import ExitStack

F32 = mybir.dt.float32
BF16 = mybir.dt.bfloat16
ALU = mybir.AluOpType
ACT = mybir.ActivationFunctionType
AX = mybir.AxisListType

P = 128
NB = 8
NTOK = 512
NT = NTOK // P
NTILE = NB * NT
H = 16
HD = P // H
L = 12
NR = 3
DA = 64
VW = 32
PARTS = 3
E1 = 16
LN_EPS = 1e-5
RMS_EPS = 1.1920929e-07
SCALE = float(HD) ** -0.5
LARGE = 3.0e38


def wait_apart(eng, sem, value, passed):
    eng.wait_ge(sem, value)
    eng.sem_inc(passed, 1)


class Chain:

    def __init__(self, eng, sem, per):
        self.eng, self.sem, self.per = eng, sem, per

    def round(self, b):
        self.base, self.k = b * self.per, 0

    def mark(self, ins):
        self.k += 1
        assert self.k <= self.per
        ins.then_inc(self.sem, 1)
        return self.base + self.k

    def wait(self, value):
        self.eng.wait_ge(self.sem, value)

    def link_apart(self, ins, passed):
        wait_apart(self.eng, self.sem, self.mark(ins), passed)

    def link(self, ins):
        self.wait(self.mark(ins))

    def end(self):
        assert self.k == self.per, (self.k, self.per)


def prepare_and_mix(nc, ctx, m):
    sb = lambda n, s, d=F32: ctx.enter_context(nc.sbuf_tensor(n, s, d))
    sem = lambda n: ctx.enter_context(nc.semaphore(n))
    x_all, v_all, yT_all, ident = m["x_all"], m["v_all"], m["yT_all"], m["ident"]
    qk_parts = m["qk_parts"]

    wqkv = sb("wqkv0", [P, 3 * P])
    PwT = sb("PwT", [P, DA])
    UT = sb("UT", [DA, NR * L])
    W1T = m["w2"][:, 0:L * P].rearrange("p (e d) -> p e d", e=L)
    W2T = m["w2"][:, L * P:2 * L * P].rearrange("p (e d) -> p e d", e=L)
    b2 = sb("b2", [L, P])
    selcol = sb("selcol", [P, 2 * L])
    sel = sb("sel", [P, 2 * L, P], BF16)
    identb = sb("identb", [P, P], BF16)

    stats = sb("stats", [P, NT, 6])
    mv = sb("mv", [P, NT, 2])
    ve = sb("ve", [P, NT])
    sd = sb("sd", [P, NT])
    r0 = sb("r0", [P, NT])
    nt_ = sb("nt_", [P, NT])
    rstd = sb("rstd", [P, NT])
    xn = sb("xn", [P, NT, P])
    xnT = sb("xnT", [P, 2, NTOK])
    split = sb("split", [P, 2, PARTS, NTOK], BF16)
    resid = sb("resid", [P, 2, NTOK])
    xa = sb("xa", [DA, NTOK])
    Z = sb("Z", [P, NT * NR, L])
    Zr = sb("Zr", [P, NT * NR, L])
    mx = sb("mx", [P, NT * NR, 8])
    Zd = sb("Zd", [P, NT * NR, L])
    Ex = sb("Ex", [P, NT * NR, L])
    Mk = sb("Mk", [P, NT * NR, L])
    Sm = sb("Sm", [P, NT * NR])
    C = sb("C", [P, NT * NR, L])
    Cs = sb("Cs", [P, NT, PARTS, 2, L], BF16)
    Cr = sb("Cr", [P, NT, 2, L])
    CsT = sb("CsT", [P, 2, NTOK], BF16)
    C3T = sb("C3T", [L, 2, NTOK])
    xs = sb("xs", [P, 3, NTOK])
    hT = m["w2"][:, 2 * L * P:2 * L * P + NTOK]

    banks = ctx.enter_context(nc.psum_tensor("banks0", [P, 8, NTOK], F32))
    prep_bank = [banks[:, 0, :], banks[:, 1, :]]
    bc_bank = [banks[:, 2 + i, :] for i in range(3)]
    h_bank, y_bank = banks[:, 5, :], banks[:, 6, :]

    x_loaded, w_loaded, passed = sem("x_loaded"), sem("w_loaded"), sem("passed0")
    consts_ready, vw_clear, w1_loaded = sem("consts_ready"), sem("vw_clear"), sem("w1_loaded")
    stats_ready, sd_ready, xn_ready, dve_prep = sem("stats_ready"), sem("sd_ready"), sem("xn_ready"), sem("dve_prep")
    bank_full, bank_free = [sem("bank_full0"), sem("bank_full1")], [sem("bank_free0"), sem("bank_free1")]
    xnT_ready, high_ready, resid_ready, parts_ready, parts_stored = (sem("xnT_ready"), sem("high_ready"), sem("resid_ready"),
                                                      sem("parts_ready"), sem("parts_stored"))
    xa_ready, zd_ready, ex_ready, cs_ready, cT_ready = (sem("xa_ready"), sem("zd_ready"), sem("ex_ready"),
                                                        sem("cs_ready"), sem("cT_ready"))
    bc_ready, xs_ready, xs_used = sem("bc_ready"), sem("xs_ready"), sem("xs_used")
    gelu_done, y_done = sem("gelu_done"), sem("y_done")
    USES = 4
    NW = 8
    STORES = 16 * 2 * PARTS

    def tok(t, b, at=0, n=NTOK):
        return t[:, bass.ds(b * NTOK + at, n)]

    def rounds(eng, first, both):
        first()
        both(1, 1, 0, 0)
        with eng.Fori(1, NB // 2) as i:
            both(2 * i, 0, 2 * i - 1, 1)
            both(2 * i + 1, 1, 2 * i, 0)
        both(None, None, NB - 1, 1)

    with nc.Block() as block:
        @block.sync
        def _(sp):
            sp.dma_start(tok(x_all, 0).rearrange("p (t d) -> p t d", t=NT), m["x"][0]).then_inc(x_loaded, 16)
            sp.dma_start(ident[:, :], m["ident_d"]).then_inc(w_loaded, 16)
            sp.dma_start(wqkv[:, :], m["wqkv0_d"]).then_inc(w_loaded, 16)
            sp.dma_start(PwT[:, :], m["PwT_d"]).then_inc(w_loaded, 16)
            sp.dma_start(UT[:, :], m["UT_d"]).then_inc(w_loaded, 16)
            sp.dma_start(selcol[:, :], m["selcol_d"]).then_inc(w_loaded, 16)
            sp.dma_start(W1T[:, :, :], m["W1T_d"]).then_inc(w_loaded, 16)
            sp.dma_start(W2T[:, :, :], m["W2T_d"]).then_inc(w_loaded, 16)
            sp.dma_start(b2[:, :], m["b2_d"]).then_inc(w_loaded, 16)
            sp.dma_start(m["rms"][:, :], m["rms_d"]).then_inc(w1_loaded, 16)
            sp.dma_start(m["w1"][:, :], m["w1_d"]).then_inc(w1_loaded, 16)
            with sp.Fori(1, NB) as b:
                sp.wait_ge(x_loaded, 16 * b)
                sp.dma_start(tok(x_all, b).rearrange("p (t d) -> p t d", t=NT),
                             m["x"][bass.ds(b, 1)].rearrange("a p t d -> p (a t) d")).then_inc(x_loaded, 16)
                for w in range(2):
                    sp.wait_ge(parts_ready, 2 * b - 1 + w)
                    for c in range(PARTS):
                        sp.dma_start(qk_parts[bass.ds(b - 1, 1), w, :, c].rearrange("a h d n -> (a h) d n"), split[:, w, c, :])\
                            .then_inc(parts_stored, 16)
            for w in range(2):
                sp.wait_ge(parts_ready, 2 * NB - 1 + w)
                for c in range(PARTS):
                    sp.dma_start(qk_parts[NB - 1, w, :, c], split[:, w, c, :]).then_inc(parts_stored, 16)
            sp.wait_ge(parts_stored, STORES * NB)

        @block.gpsimd
        def _(pool):
            pool.memset(CsT[:, :, :], 0.0).then_inc(consts_ready, 1)
            pool.memset(m["qs"][:, :, :, :].bitcast(F32), 0.0)
            pool.memset(m["ks"][:, :, :, :].bitcast(F32), 0.0)
            pool.memset(m["zero"][:, :], 0.0)
            pool.memset(m["one"][:, :], 1.0)
            pool.memset(m["vw"][:, :, :, :, :], 0.0).then_inc(vw_clear, 1)
            pool.wait_ge(vw_clear, 1)
            pool.memset(m["vw"][:, :, :, :, HD:HD + 1], 1.0)
            pool.wait_ge(w1_loaded, 32)
            for e in range(E1):
                w = m["w1"][:, e * 2 * P:(e + 1) * 2 * P]
                pool.tensor_scalar(w, w, m["rms"][:, e:e + 1], None, ALU.mult)

        @block.vector
        def _(v):
            own = Chain(v, dve_prep, 13 + 2 + 26 + 7)

            def norm(b):
                own.round(b)
                v.wait_ge(x_loaded, 16 * (b + 1))
                for t in range(NT):
                    done = own.mark(v.bn_stats(stats[:, t, :], tok(x_all, b, t * P, P)))
                wait_apart(v, dve_prep, done, passed)
                for t in range(NT):
                    done = own.mark(v.bn_aggr(mv[:, t, :], stats[:, t, :]))
                own.wait(done)
                v.tensor_scalar(ve[:, :], mv[:, :, 1], LN_EPS, None, ALU.add).then_inc(stats_ready, 1)
                v.wait_ge(sd_ready, b + 1)
                own.link(v.reciprocal(r0[:, :], sd[:, :]))
                own.link(v.tensor_tensor(nt_[:, :], r0[:, :], r0[:, :], ALU.mult))
                own.link(v.tensor_tensor(nt_[:, :], nt_[:, :], ve[:, :], ALU.mult))
                own.link(v.tensor_scalar(nt_[:, :], nt_[:, :], -0.5, 1.5, ALU.mult, ALU.add))
                own.link(v.tensor_tensor(rstd[:, :], r0[:, :], nt_[:, :], ALU.mult))
                if not isinstance(b, int) or b > 0:
                    v.wait_ge(bank_full[0], USES * (b - 1) + 1)
                for t in range(NT):
                    ins = v.tensor_scalar(xn[:, t, :], tok(x_all, b, t * P, P), mv[:, t, 0:1], rstd[:, t:t + 1],
                                          ALU.subtract, ALU.mult)
                ins.then_inc(xn_ready, 1)

            def residual(b, w):
                v.wait_ge(high_ready, 2 * b + w + 1)
                v.tensor_tensor(resid[:, w, :], prep_bank[1 - w], split[:, w, 0, :], ALU.subtract).then_inc(bank_free[1 - w], 1)
                v.wait_ge(bank_free[1 - w], USES * b + (1 if w == 0 else 2))
                own.link(v.tensor_copy(split[:, w, 1, :], resid[:, w, :]))
                v.tensor_tensor(split[:, w, 2, :], resid[:, w, :], split[:, w, 1, :], ALU.subtract).then_inc(parts_ready, 1)

            def choose(b):
                v.wait_ge(bank_full[1], USES * b + 3)
                v.tensor_copy(Z[:, :, :].rearrange("p a e -> p (a e)"), prep_bank[1][:, 0:NT * NR * L]).then_inc(bank_free[1], 1)
                wait_apart(v, bank_free[1], USES * b + 3, passed)
                for i in range(NT * NR):
                    done = own.mark(v.max(mx[:, i, :], Z[:, i, :]))
                own.wait(done)
                v.tensor_tensor(Zd[:, :, :], Z[:, :, :], mx[:, :, 0:1].broadcast_to([P, NT * NR, L]), ALU.subtract).then_inc(zd_ready, 1)
                own.link_apart(v.memset(mx[:, :, 3:8], LARGE), passed)
                for i in range(NT * NR):
                    done = own.mark(v.match_replace(Zr[:, i, :], mx[:, i, :], Z[:, i, :], -LARGE))
                own.wait(done)
                own.link(v.tensor_tensor(Mk[:, :, :], Zr[:, :, :], Z[:, :, :], ALU.not_equal))

            def weigh(b):
                v.wait_ge(ex_ready, b + 1)
                own.link(v.tensor_tensor(Mk[:, :, :], Mk[:, :, :], Ex[:, :, :], ALU.mult))
                own.link(v.tensor_reduce(Sm[:, :], Mk[:, :, :], AX.X, ALU.add))
                own.link(v.reciprocal(Sm[:, :], Sm[:, :]))
                own.link(v.tensor_tensor(C[:, :, :], Mk[:, :, :], Sm[:, :, None].broadcast_to([P, NT * NR, L]), ALU.mult))
                C12 = C[:, :, :].rearrange("p (t r) e -> p t r e", r=NR)[:, :, 0:2, :]
                own.link(v.tensor_copy(Cs[:, :, 0, :, :], C12))
                own.link(v.tensor_tensor(Cr[:, :, :, :], C12, Cs[:, :, 0, :, :], ALU.subtract))
                own.link(v.tensor_copy(Cs[:, :, 1, :, :], Cr[:, :, :, :]))
                v.tensor_tensor(Cs[:, :, 2, :, :], Cr[:, :, :, :], Cs[:, :, 1, :, :], ALU.subtract).then_inc(cs_ready, 1)
                own.end()

            def scale_inputs(b, par, e):
                n = 2 * L * b + e
                src = xnT[:, par, :] if e < L else hT[:, :]
                if e == L:
                    v.wait_ge(gelu_done, b + 1)
                v.wait_ge(bc_ready, n + 1)
                if not isinstance(b, int) or b > 0 or e >= 3:
                    v.wait_ge(xs_used, n - 2)
                v.tensor_tensor(xs[:, e % 3, :], bc_bank[e % 3], src, ALU.mult).then_inc(xs_ready, 1)

            v.wait_ge(w_loaded, 16 * NW)
            v.tensor_copy(identb[:, :], ident[:, :]).then_inc(consts_ready, 1)
            v.tensor_copy(sel[:, :, :], selcol[:, :, None].broadcast_to([P, 2 * L, P])).then_inc(consts_ready, 1)

            def first():
                norm(0)
                residual(0, 0)
                residual(0, 1)
                choose(0)
                weigh(0)

            def both(b, par, a, apar):
                for e in range(2 * L):
                    if b is not None:
                        if e == 1:
                            norm(b)
                        if e == 7:
                            residual(b, 0)
                        if e == 8:
                            residual(b, 1)
                        if e == 12:
                            choose(b)
                        if e == 17:
                            weigh(b)
                    scale_inputs(a, apar, e)

            rounds(v, first, both)

        @block.scalar
        def _(act):
            def deviation(b):
                act.wait_ge(stats_ready, b + 1)
                act.activation(sd[:, :], ve[:, :], ACT.Sqrt).then_inc(sd_ready, 1)

            def evacuate_norm(b, par):
                act.wait_ge(bank_full[0], USES * b + 1)
                if not isinstance(b, int) or b > 1:
                    act.wait_ge(xs_ready, 2 * L * (b - 1))
                act.activation(xnT[:, par, :], prep_bank[0], ACT.Copy).then_inc(bank_free[0], 1)

            def high_parts(b):
                for w in range(2):
                    act.wait_ge(bank_full[1 - w], USES * b + (1 if w == 0 else 2))
                    if not isinstance(b, int) or b > 0:
                        act.wait_ge(parts_stored, STORES * b)
                    act.activation(split[:, w, 0, :], prep_bank[1 - w], ACT.Copy).then_inc(high_ready, 1)

            def values_and_address(b):
                act.wait_ge(bank_full[1], USES * b + 2)
                act.activation(tok(v_all, b), prep_bank[1], ACT.Copy).then_inc(bank_free[1], 1)
                act.wait_ge(bank_full[0], USES * b + 3)
                act.activation(xa[:, :], prep_bank[0][0:DA, :], ACT.Copy).then_inc(bank_free[0], 1)

            def exponentials(b):
                act.wait_ge(zd_ready, b + 1)
                act.activation(Ex[:, :, :], Zd[:, :, :], ACT.Exp).then_inc(ex_ready, 1)

            def weights_transposed(b, par):
                act.wait_ge(bank_full[0], USES * b + 4)
                act.activation(CsT[0:PARTS * 2 * L, par, :], prep_bank[0].bitcast(BF16)[0:PARTS * 2 * L, 0:NTOK], ACT.Copy)\
                    .then_inc(bank_free[0], 1)
                act.wait_ge(bank_full[1], USES * b + 4)
                act.activation(C3T[:, par, :], prep_bank[1][0:L, :], ACT.Copy).then_inc(bank_free[1], 1)

            def gelu(b):
                act.wait_ge(xs_used, 2 * L * b + L)
                act.activation(hT[:, :], h_bank, ACT.Gelu).then_inc(gelu_done, 1)

            def keep_mixture(b):
                act.wait_ge(xs_used, 2 * L * (b + 1))
                act.activation(tok(yT_all, b), y_bank, ACT.Copy).then_inc(y_done, 1)

            act.wait_ge(consts_ready, 3)

            def first():
                deviation(0)
                evacuate_norm(0, 0)
                high_parts(0)
                values_and_address(0)
                exponentials(0)
                weights_transposed(0, 0)

            def both(b, par, a, apar):
                if b is not None:
                    deviation(b)
                    evacuate_norm(b, par)
                    high_parts(b)
                    values_and_address(b)
                gelu(a)
                if b is not None:
                    exponentials(b)
                    weights_transposed(b, par)
                keep_mixture(a)

            rounds(act, first, both)

        @block.tensor
        def _(pe):
            def claim(b, k):
                if not isinstance(b, int) or b > 0 or k >= 2:
                    pe.wait_ge(bank_free[k % 2], USES * b + k // 2)
                return prep_bank[k % 2]

            def mm(out, lhsT, rhs, start=True, stop=True):
                return nc.tensor.matmul(out, lhsT, rhs, start=start, stop=stop)

            def transpose_norm(b):
                pe.wait_ge(xn_ready, b + 1)
                o = claim(b, 0)
                for t in range(NT):
                    last = nc.tensor.transpose(o[:, t * P:(t + 1) * P], xn[:, t, :], ident[:, :])
                last.then_inc(bank_full[0], 1)

            def queries_keys(b, par):
                pe.wait_ge(bank_free[0], USES * b + 1)
                mm(claim(b, 1), wqkv[:, 0:P], xnT[:, par, :]).then_inc(bank_full[1], 1)
                mm(claim(b, 2), wqkv[:, P:2 * P], xnT[:, par, :]).then_inc(bank_full[0], 1)

            def values_and_address(b, par):
                o = claim(b, 3)
                for t in range(NT):
                    last = mm(o[:, t * P:(t + 1) * P], xnT[:, par, t * P:(t + 1) * P], wqkv[:, 2 * P:3 * P])
                last.then_inc(bank_full[1], 1)
                mm(claim(b, 4)[0:DA, :], PwT[:, :], xnT[:, par, :]).then_inc(bank_full[0], 1)

            def scores(b):
                pe.wait_ge(bank_free[0], USES * b + 3)
                o = claim(b, 5)
                for t in range(NT):
                    last = mm(o[:, t * NR * L:(t + 1) * NR * L], xa[:, t * P:(t + 1) * P], UT[:, :])
                last.then_inc(bank_full[1], 1)

            def transpose_weights(b):
                pe.wait_ge(cs_ready, b + 1)
                o = claim(b, 6).bitcast(BF16)
                for t in range(NT):
                    last = nc.tensor.transpose(o[0:PARTS * 2 * L, t * P:(t + 1) * P], Cs[:, t, :, :, :].rearrange("p c r e -> p (c r e)"), identb[:, :])
                last.then_inc(bank_full[0], 1)
                o = claim(b, 7)
                for t in range(NT):
                    last = nc.tensor.transpose(o[0:L, t * P:(t + 1) * P], C[:, t * NR + 2, :], ident[:, :])
                last.then_inc(bank_full[1], 1)

            def broadcast_weight(b, par, e):
                n = 2 * L * b + e
                if not isinstance(b, int) or b > 0 or e >= 3:
                    pe.wait_ge(xs_ready, n - 2)
                if e == 0:
                    pe.wait_ge(bank_free[0], USES * (b + 1))
                mm(bc_bank[e % 3], sel[:, e, :], CsT[:, par, :]).then_inc(bc_ready, 1)

            def accumulate(b, par, e):
                n = 2 * L * b + e
                if e == 0 and (not isinstance(b, int) or b > 0):
                    pe.wait_ge(gelu_done, b)
                if e == L:
                    if not isinstance(b, int) or b > 0:
                        pe.wait_ge(y_done, b)
                    pe.wait_ge(bank_free[1], USES * (b + 1))
                    mm(y_bank, b2[:, :], C3T[:, par, :], stop=False)
                pe.wait_ge(xs_ready, n + 1)
                w = (W1T if e < L else W2T)[:, e % L, :]
                mm(h_bank if e < L else y_bank, w, xs[:, e % 3, :], start=(e == 0), stop=(e % L == L - 1))\
                    .then_inc(xs_used, 1)

            pe.wait_ge(w_loaded, 16 * NW)
            pe.wait_ge(consts_ready, 3)

            def first():
                transpose_norm(0)
                queries_keys(0, 0)
                values_and_address(0, 0)
                scores(0)
                transpose_weights(0)

            def both(b, par, a, apar):
                broadcast_weight(a, apar, 0)
                broadcast_weight(a, apar, 1)
                for e in range(2 * L):
                    if e + 2 < 2 * L:
                        broadcast_weight(a, apar, e + 2)
                    accumulate(a, apar, e)
                    if b is not None:
                        if e == 3:
                            transpose_norm(b)
                        if e == 5:
                            queries_keys(b, par)
                        if e == 7:
                            values_and_address(b, par)
                        if e == 9:
                            scores(b)
                        if e == 21:
                            transpose_weights(b)

            rounds(pe, first, both)


def attend(nc, ctx, m):
    sb = lambda n, s, d=F32: ctx.enter_context(nc.sbuf_tensor(n, s, d))
    sem = lambda n: ctx.enter_context(nc.semaphore(n))
    x_all, v_all, yT_all, ident = m["x_all"], m["v_all"], m["yT_all"], m["ident"]
    qk_parts = m["qk_parts"]
    NPROD = PARTS * PARTS
    ROWS = NPROD * HD
    OCT, QUAD = 8, 4
    UNITS = OCT * NT
    STEPS = UNITS // QUAD
    LEAD = 3

    qs, ks, vw, zero, one = m["qs"], m["ks"], m["vw"], m["zero"], m["one"]
    wproj = sb("wproj", [P, P])
    bproj = sb("bproj", [P, 1])
    identb = sb("identb1", [P, P], BF16)
    probs = sb("probs", [P, 2, QUAD, NTOK])
    mx = sb("mx1", [P, 2, OCT * NT])
    mhl = sb("mhl", [P, 2, 4, OCT * NT], BF16)
    mT = sb("mT", [2 * OCT * NT, 2, P], BF16)
    oT = sb("oT", [P, 2, NTOK])
    rden = sb("rden", [P, NT, QUAD])
    att = sb("att", [P, NT, P])
    attT = sb("attT", [P, NTOK])
    x1T = sb("x1T", [P, NTOK])

    banks = ctx.enter_context(nc.psum_tensor("banks1", [P, 8, NTOK], F32))
    e_bank = [banks[:, i, :] for i in range(4)]
    s_bank = [banks[:, 4 + i, :] for i in range(2)]
    o_bank, misc = banks[:, 6, :], banks[:, 7, :]

    w_loaded, w2_loaded, filled = sem("w_loaded1"), sem("w2_loaded"), sem("filled1")
    stack_loaded = [[sem(f"stack_loaded{p}{o}") for o in range(2)] for p in range(2)]
    m_loaded = [sem("m_loaded0"), sem("m_loaded1")]
    v_ready = sem("v_ready")
    s_full, s_free, e_full, exp_done, av_done = sem("s_full"), sem("s_free"), sem("e_full"), sem("exp_done"), sem("av_done")
    m_hi, m_split, mt_full, mt_free = sem("m_hi"), sem("m_split"), sem("mt_full"), sem("mt_free")
    o_kept, ot_full, rden_ready, ot_free = sem("o_kept"), sem("ot_full"), sem("rden_ready"), sem("ot_free")
    at_full, at_free, pj_full, pj_free, xt_full, xt_free = (sem("at_full"), sem("at_free"), sem("pj_full"),
                                                            sem("pj_free"), sem("xt_full"), sem("xt_free"))
    LOADS = PARTS * PARTS + PARTS + 1

    def tok(t, b, at=0, n=NTOK):
        return t[:, bass.ds(b * NTOK + at, n)]

    def ge(eng, s, value):
        if not isinstance(value, int) or value > 0:
            eng.wait_ge(s, value)

    def rounds(eng, first, octet, last):
        first()
        def pair(b, end):
            for r in range(4):
                octet(b + r // 2, r // 2, r % 2, not end or r < 3, not end or r < 2)
        pair(0, False)
        with eng.Fori(1, NB // 2 - 1) as i:
            pair(2 * i, False)
        pair(NB - 2, True)
        last()

    with nc.Block() as block:
        @block.sync
        def _(sp):
            def gather(b, par, o):
                s = stack_loaded[par][o]
                heads = slice(o * OCT, (o + 1) * OCT)
                for a in range(PARTS):
                    lo = a * PARTS * HD
                    sp.dma_start(ks[lo:lo + PARTS * HD, par, heads, :],
                                 qk_parts[b, 1, heads].rearrange("h c d n -> (c d) h n") if isinstance(b, int) else
                                 qk_parts[bass.ds(b, 1), 1, heads].rearrange("a h c d n -> (a c d) h n")).then_inc(s, 16)
                    for c in range(PARTS):
                        at = lo + c * HD
                        sp.dma_start(qs[at:at + HD, par, heads, :],
                                     qk_parts[b, 0, heads, a].rearrange("h d n -> d h n") if isinstance(b, int) else
                                     qk_parts[bass.ds(b, 1), 0, heads, a].rearrange("a h d n -> (a d) h n")).then_inc(s, 16)
                sp.dma_start(qs[ROWS:ROWS + 2, par, heads, :], zero[:, None, :].broadcast_to([2, OCT, NTOK])).then_inc(s, 16)

            def put_maxima(b, par, o):
                n = 2 * b + o
                sp.wait_ge(mt_free, n + 1)
                sp.dma_start(qs[ROWS:ROWS + 2, par, o * OCT:(o + 1) * OCT, :], mT[:, o, :]).then_inc(m_loaded[o], 16)

            sp.dma_start(wproj[:, :], m["wproj_d"]).then_inc(w_loaded, 16)
            sp.dma_start(bproj[:, :], m["bproj_d"]).then_inc(w_loaded, 16)
            for par in range(2):
                sp.dma_start(ks[ROWS:ROWS + 2, par, :, :], one[:, None, :].broadcast_to([2, H, NTOK])).then_inc(filled, 16)

            def first():
                gather(0, 0, 0)
                gather(0, 0, 1)
                put_maxima(0, 0, 0)

            def octet(b, pb, o, more1, more2):
                if more2:
                    ge(sp, e_full, 2 * UNITS * b)
                    gather(b + 1, 1 - pb, o)
                if more1:
                    put_maxima(b + o, (pb + o) % 2, 1 - o)

            sp.dma_start(m["w2"][:, :], m["w2_d"]).then_inc(w2_loaded, 16)
            rounds(sp, first, octet, lambda: None)
            sp.wait_ge(w2_loaded, 16)
            for o in range(2):
                sp.wait_ge(m_loaded[o], 16 * NB)

        @block.gpsimd
        def _(pool):
            def spread(b, par):
                pool.tensor_copy(vw[:, par, :, :, 0:HD], tok(v_all, b).rearrange("p (t h d) -> p t h d", t=NT, h=H))\
                    .then_inc(v_ready, 1)

            def octet(b, pb, o, more1, more2):
                if o == 0 and more2:
                    ge(pool, av_done, 2 * STEPS * b)
                    spread(b + 1, 1 - pb)

            rounds(pool, lambda: spread(0, 0), octet, lambda: None)

        @block.vector
        def _(v):
            v.memset(mhl[:, :, 2:4, :], 0.0)
            v.tensor_copy(identb[:, :], ident[:, :]).then_inc(filled, 1)

            def maxima(b, o, s, js=range(QUAD)):
                for j in js:
                    u = s * QUAD + j
                    n = (2 * b + o) * UNITS + u
                    v.wait_ge(s_full, n + 1)
                    if u == 0:
                        ge(v, m_split, 2 * b + o - 1)
                    v.tensor_reduce(mx[:, o, u:u + 1], s_bank[u % 2], AX.X, ALU.max).then_inc(s_free, 1)

            def split_maxima(b, o):
                n = 2 * b + o
                v.wait_ge(s_free, UNITS * (n + 1))
                ge(v, mt_full, n - 1)
                v.tensor_scalar(mhl[:, o, 0, :], mx[:, o, :], -1.0, None, ALU.mult).then_inc(m_hi, 1)
                v.wait_ge(m_hi, n + 1)
                v.scalar_tensor_tensor(mhl[:, o, 1, :], mx[:, o, :], -1.0, mhl[:, o, 0, :], ALU.mult, ALU.subtract)\
                    .then_inc(m_split, 1)

            def normalize(b, quad):
                g = QUAD * b + quad
                v.wait_ge(ot_full, g + 1)
                o = misc.rearrange("p (t j c) -> p t j c", t=NT, j=QUAD)
                v.reciprocal(rden[:, :, :], o[:, :, :, HD]).then_inc(rden_ready, 1)
                v.wait_ge(rden_ready, g + 1)
                if quad == 0:
                    ge(v, at_full, b)
                v.tensor_tensor(att[:, :, quad * QUAD * HD:(quad + 1) * QUAD * HD].rearrange("p t (j d) -> p t j d", d=HD),
                                o[:, :, :, 0:HD], rden[:, :, :, None].broadcast_to([P, NT, QUAD, HD]), ALU.mult)\
                    .then_inc(ot_free, 1)

            def add_mixture(b):
                v.wait_ge(pj_full, b + 1)
                ge(v, xt_full, b)
                v.scalar_tensor_tensor(x1T[:, :], misc, bproj[:, 0:1], tok(yT_all, b), ALU.add, ALU.add).then_inc(pj_free, 1)

            def add_input(b):
                v.wait_ge(xt_full, b + 1)
                v.tensor_tensor(tok(x_all, b), misc, tok(x_all, b), ALU.add).then_inc(xt_free, 1)

            def first():
                v.wait_ge(w_loaded, 32)
                for s in range(STEPS):
                    maxima(0, 0, s)
                split_maxima(0, 0)
                for s in range(LEAD):
                    maxima(0, 1, s)

            def octet(b, pb, o, more1, more2):
                begin = isinstance(b, int) and b == 0 and o == 0
                for s in range(STEPS):
                    for js in ((0, 1), (2, 3)):
                        if s < STEPS - LEAD:
                            if more1:
                                maxima(b + o, 1 - o, s + LEAD, js)
                        elif more2:
                            maxima(b + 1, o, s + LEAD - STEPS, js)
                        if js[0] == 0:
                            if s == 2 and not begin:
                                normalize(b - 1 + o, 3 if o == 0 else 1)
                            if o == 0 and not begin:
                                if s == 4:
                                    add_mixture(b - 1)
                                if s == 5:
                                    add_input(b - 1)
                            if s == 7:
                                normalize(b, 2 * o)
                    if s == STEPS - LEAD - 1 and more1:
                        split_maxima(b + o, 1 - o)

            def last():
                normalize(NB - 1, 3)
                add_mixture(NB - 1)
                add_input(NB - 1)

            rounds(v, first, octet, last)

        @block.scalar
        def _(act):
            def exponentiate(b, o, s, js):
                g = (2 * b + o) * STEPS + s
                for j in js:
                    act.wait_ge(e_full, g * QUAD + j + 1)
                    if j == 0:
                        ge(act, av_done, g - 1)
                    act.activation(probs[:, s % 2, j, :], e_bank[j], ACT.Exp, scale=SCALE).then_inc(exp_done, 1)

            def keep_products(b, quad):
                g = QUAD * b + quad
                act.wait_ge(av_done, NT * (g + 1))
                ge(act, ot_full, g - 1)
                act.activation(oT[:, quad % 2, :], o_bank, ACT.Copy).then_inc(o_kept, 1)

            def keep_maxima(b, o):
                n = 2 * b + o
                act.wait_ge(mt_full, n + 1)
                ge(act, m_loaded[o], 16 * b)
                act.activation(mT[:, o, :], misc.bitcast(BF16)[0:2 * OCT * NT, 0:P], ACT.Copy).then_inc(mt_free, 1)

            def keep_attention(b):
                act.wait_ge(at_full, b + 1)
                act.activation(attT[:, :], misc, ACT.Copy).then_inc(at_free, 1)

            def octet(b, pb, o, more1, more2):
                begin = isinstance(b, int) and b == 0 and o == 0
                for s in range(STEPS):
                    exponentiate(b, o, s, (0, 1))
                    if s == 3 and o == 0 and not begin:
                        keep_attention(b - 1)
                    if s == 6 and more1:
                        keep_maxima(b + o, 1 - o)
                    exponentiate(b, o, s, (2, 3))
                    if s == 0 and not begin:
                        keep_products(b - 1 + o, 3 if o == 0 else 1)
                    if s == 4:
                        keep_products(b, 2 * o)

            def last():
                keep_products(NB - 1, 3)
                keep_attention(NB - 1)

            rounds(act, lambda: keep_maxima(0, 0), octet, last)

        @block.tensor
        def _(pe):
            def mm(out, lhsT, rhs, start=True, stop=True):
                return nc.tensor.matmul(out, lhsT, rhs, start=start, stop=stop)

            def score(b, par, o, s, js=range(QUAD)):
                if s == 0 and js[0] == 0:
                    pe.wait_ge(stack_loaded[par][o], 16 * LOADS * (b // 2 + 1) if isinstance(b, int) else 8 * LOADS * (b - par + 2))
                for j in js:
                    u = s * QUAD + j
                    h, t = o * OCT + u // NT, u % NT
                    ge(pe, s_free, (2 * b + o) * UNITS + u - 1)
                    mm(s_bank[u % 2], qs[:, par, h, t * P:(t + 1) * P], ks[:, par, h, :]).then_inc(s_full, 1)

            def shifted(b, par, o, s, js):
                if s == 0 and js[0] == 0:
                    pe.wait_ge(m_loaded[o], 16 * (b + 1))
                t = s % NT
                for j in js:
                    h = o * OCT + s // NT * QUAD + j
                    ge(pe, exp_done, ((2 * b + o) * STEPS + s - 1) * QUAD + j + 1)
                    mm(e_bank[j], ks[:, par, h, t * P:(t + 1) * P], qs[:, par, h, :]).then_inc(e_full, 1)

            def values(b, par, o, s):
                g = (2 * b + o) * STEPS + s
                t = s % NT
                if o == 0 and s == 0:
                    pe.wait_ge(v_ready, b + 1)
                if t == 0:
                    ge(pe, o_kept, (2 * b + o) * 2 + s // NT)
                pe.wait_ge(exp_done, (g + 1) * QUAD)
                for j in range(QUAD):
                    h = o * OCT + s // NT * QUAD + j
                    last = mm(o_bank[j * VW:(j + 1) * VW, :], vw[:, par, t, h, :], probs[:, s % 2, j, :],
                              start=(t == 0), stop=(t == NT - 1))
                last.then_inc(av_done, 1)

            def transposes(src, full):
                for t in range(NT):
                    last = nc.tensor.transpose(misc[:, t * P:(t + 1) * P], src(t), ident[:, :])
                last.then_inc(full, 1)

            def transpose_maxima(b, o, before, count):
                n = 2 * b + o
                ge(pe, before, count)
                pe.wait_ge(m_split, n + 1)
                nc.tensor.transpose(misc.bitcast(BF16)[:, 0:P], mhl[:, o, :, :].rearrange("p c u -> p (c u)"),
                                    identb[:, :]).then_inc(mt_full, 1)

            def transpose_products(b, quad, before, count):
                ge(pe, before, count)
                pe.wait_ge(o_kept, QUAD * b + quad + 1)
                transposes(lambda t: oT[:, quad % 2, t * P:(t + 1) * P], ot_full)

            def transpose_attention(b):
                pe.wait_ge(ot_free, QUAD * (b + 1))
                transposes(lambda t: att[:, t, :], at_full)

            def project(b):
                pe.wait_ge(at_free, b + 1)
                mm(misc, wproj[:, :], attT[:, :]).then_inc(pj_full, 1)

            def transpose_sum(b):
                pe.wait_ge(pj_free, b + 1)
                transposes(lambda t: x1T[:, t * P:(t + 1) * P], xt_full)

            pe.wait_ge(filled, 33)
            pe.wait_ge(w_loaded, 32)

            def first():
                for s in range(STEPS):
                    score(0, 0, 0, s)
                transpose_maxima(0, 0, mt_free, 0)
                for s in range(LEAD):
                    score(0, 0, 1, s)

            def octet(b, pb, o, more1, more2):
                begin = isinstance(b, int) and b == 0 and o == 0
                n = 2 * b + o
                for s in range(STEPS):
                    for j in range(QUAD):
                        if s < STEPS - LEAD:
                            if more1:
                                score(b + o, (pb + o) % 2, 1 - o, s + LEAD, [j])
                        elif more2:
                            score(b + 1, 1 - pb, o, s + LEAD - STEPS, [j])
                        shifted(b, pb, o, s, [j])
                        if j == 1:
                            if s > 0:
                                values(b, pb, o, s - 1)
                            elif not begin:
                                values(b - 1 + o, (pb + 1 + o) % 2, 1 - o, STEPS - 1)
                    if s == 1 and not begin:
                        transpose_products(b - 1 + o, 3 if o == 0 else 1, ot_free, 2 * n - 1)
                    if o == 0 and not begin:
                        if s == 2:
                            transpose_attention(b - 1)
                        if s == 3:
                            project(b - 1)
                        if s == 4:
                            transpose_sum(b - 1)
                    if s == 5 and more1:
                        if o == 1:
                            transpose_maxima(b + o, 1 - o, ot_free, 2 * n)
                        elif begin:
                            transpose_maxima(b, 1, mt_free, 1)
                        else:
                            transpose_maxima(b, 1, xt_free, b)
                    if s == 6:
                        if more1:
                            transpose_products(b, 2 * o, mt_free, n + 2)
                        else:
                            transpose_products(b, 2 * o, ot_free, 2 * n)

            def last():
                values(NB - 1, 1, 1, STEPS - 1)
                transpose_products(NB - 1, 3, ot_free, QUAD * NB - 1)
                transpose_attention(NB - 1)
                project(NB - 1)
                transpose_sum(NB - 1)

            rounds(pe, first, octet, last)


def second_layer(nc, ctx, m):
    sb = lambda n, s, d=F32: ctx.enter_context(nc.sbuf_tensor(n, s, d))
    sem = lambda n: ctx.enter_context(nc.semaphore(n))
    x_all, ident, w1, w2, rms = m["x_all"], m["ident"], m["w1"], m["w2"], m["rms"]
    out = m["out"]
    NE, NSH = 16, 2
    NRT = NE - NSH
    HID = 2
    NKNOT = NB + 1
    ND = H * NKNOT
    SD = ND + NRT
    HT = H * NB

    hT_all = sb("hT_all", [P, NTILE * P])
    qkv = sb("qkv_all", [P, NTILE, 3 * P])
    dl = sb("dl_all", [P, NTILE, SD])
    gate = sb("gate_all", [P, NTILE, NRT])
    wqkv = sb("wqkv1", [P, 3 * P])
    wside = sb("wside", [P, SD])
    bqkv = sb("bqkv", [P, 3 * P])
    bside = sb("bside", [P, SD])
    wqT = sb("wqT", [P, P])
    bqc = sb("bqc", [P, 1])
    bqw = sb("bqw", [P, P])
    pe_rows = sb("pe_rows", [P, NKNOT])
    knots = sb("knots", [P, NKNOT])
    blockm = sb("blockm", [P, H])
    pe_blk = sb("pe_blk", [P, H, NKNOT])
    wo = sb("wo", [P, P])
    bo = sb("bo", [P, P])
    stats, mv = sb("stats2", [P, NT, 6]), sb("mv2", [P, NT, 2])
    ve, sd, r0, nt_, rstd = (sb(n, [P, NT]) for n in ("ve2", "sd2", "r02", "nt2", "rstd2"))
    xn, xh, xnT, sq = sb("xn2", [P, NT, P]), sb("xh", [P, NT, P]), sb("xnT2", [P, NTOK]), sb("sq", [P, P])
    ms = sb("ms", [P, NT])
    lmax, ld, lex, lsum = sb("lmax", [P, NT]), sb("ld", [P, NT, NRT]), sb("lex", [P, NT, NRT]), sb("lsum", [P, NT])
    top, rest = sb("top", [P, NT, 8]), sb("rest", [P, NT, NRT])
    hid = sb("hid", [P, 2, HID, NTOK])
    scaled = sb("scaled", [P, 2, NTOK])
    prod = sb("prod", [P, 3, HT * HD])
    prodv = sb("prodv", [P, HT * HD])
    sc, pos, lg, term = (sb(n, [P, NB, H, NB]) for n in ("sc", "pos", "lg", "term"))
    smx = sb("smx", [P, NB, H])
    ao = sb("ao", [P, NB, P])
    aoT = sb("aoT", [P, NTOK])

    banks = ctx.enter_context(nc.psum_tensor("banks2", [P, 8, NTOK], F32))
    a_bank = [banks[:, 0:2, :], banks[:, 2:4, :]]
    w_bank = [banks[:, 4, :], banks[:, 5, :]]
    misc = [banks[:, 6, :], banks[:, 7, :]]

    w_loaded, knots_done, blk_ready = sem("w_loaded2"), sem("knots_done"), sem("blk_ready")
    passed, pool_passed = sem("passed2"), sem("pool_passed")
    side_full, side_ready = sem("side_full"), sem("side_ready")
    stats_ready, sd_ready, xn_ready, ms_ready, ve2_ready, sd2_ready, xh_ready, dve_prep = (
        sem(n) for n in ("stats_ready2", "sd_ready2", "xn_ready2", "ms_ready", "msv_ready", "sdr_ready", "xh_ready", "dve_prep2"))
    misc_full, misc_free = [sem("misc_full0"), sem("misc_full1")], [sem("misc_free0"), sem("misc_free1")]
    ld_ready, lex_ready, gate_ready = sem("ld_ready"), sem("lex_ready"), sem("gate_ready")
    a_full, hid_ready, w_full, added = sem("a_full"), sem("hid_ready"), sem("w_full"), sem("added")
    scaled_ready, shared_added = sem("scaled_ready"), sem("shared_added")
    sprod_ready, sprod_free = sem("sprod_ready"), sem("sprod_free")
    sc_ready, pos_ready, lgm_ready, ex_ready, pr_ready, ao_ready, dve_att = (
        sem(n) for n in ("sc_ready", "sig_ready", "lgm_ready", "ex_ready2", "pr_ready", "ao_ready", "dve_att"))
    att_done, sum_ready, out_done = sem("att_done"), sem("sum_ready"), sem("out_done")
    NW = 9
    PUSES = 1 + NT
    AUSES = 2
    POOL_MUL = 6

    def tok(t, b, at=0, n=NTOK):
        return t[:, bass.ds(b * NTOK + at, n)]

    def ge(eng, s, value):
        if not isinstance(value, int) or value > 0:
            eng.wait_ge(s, value)

    def rounds(eng, first, left, right, last):
        first()
        left(0, 1, 2)
        with eng.Fori(1, NB // 2 - 1) as c:
            left(c, 2 * c + 1, 2 * c + 2)
        left(NB // 2 - 1, NB - 1, None)
        right(NB // 2, 0)
        with eng.Fori(1, NB // 2) as g:
            right(g + NB // 2, g)
        last()

    def group(t, g, lo, hi):
        v = t[:, :, :].rearrange("p (s g) c -> p g s c", g=NT)
        return v[:, bass.ds(g, 1), :, lo:hi].rearrange("p a s c -> p (a s) c")

    def factors(g, s, kind):
        if kind == 0:
            q = group(qkv, g, 0, P)[:, s, :].rearrange("p (h d) -> p h d", h=H)[:, :, None, :].broadcast_to([P, H, NB, HD])
            k = group(qkv, g, P, 2 * P).rearrange("p t (h d) -> p h t d", h=H)
            return q, k
        w = lg[:, s, :, None, :].broadcast_to([P, H, HD, NB])
        v = group(qkv, g, 2 * P, 3 * P).rearrange("p t (h d) -> p h d t", h=H)
        return w, v

    with nc.Block() as block:
        @block.sync
        def _(sp):
            for dst, name in ((wqT, "wqT"), (bqc, "bqc"), (pe_rows, "pe_rows"), (blockm, "blockm"), (wqkv, "wqkv1"), (wo, "wo")):
                sp.dma_start(dst[:, :], m[name + "_d"]).then_inc(w_loaded, 16)
            sp.dma_start(wside[:, ND:SD], m["router_d"]).then_inc(w_loaded, 16)
            sp.dma_start(bqkv[:, :], m["bqkv_d"].broadcast_to([P, 3 * P])).then_inc(w_loaded, 16)
            sp.dma_start(bo[:, :], m["bo_d"].broadcast_to([P, P])).then_inc(w_loaded, 16)
            for s in range(NB):
                sp.wait_ge(sum_ready, s + 1)
                sp.dma_start(out[s], x_all[:, s * NTOK:(s + 1) * NTOK].rearrange("p (g d) -> p g d", g=NT)).then_inc(out_done, 16)
            sp.wait_ge(out_done, 16 * NB)

        @block.gpsimd
        def _(pool):
            def add(c, i):
                n = c * NRT + i - NSH
                wait_apart(pool, scaled_ready, n + 1, pool_passed)
                pool.tensor_tensor(tok(x_all, c), tok(x_all, c), scaled[:, i % 2, :], ALU.add).then_inc(added, 1)
                wait_apart(pool, added, n + 1, pool_passed)

            def multiply(g, s, kind):
                n = (2 * g + kind) * POOL_MUL + s
                if not isinstance(n, int) or n > 2:
                    wait_apart(pool, sprod_free, n - 2, pool_passed)
                o = prod[:, s % 3, :].rearrange("p (h a b) -> p h a b", h=H, a=NB)
                pool.tensor_tensor(o, *factors(g, s, kind), ALU.mult).then_inc(sprod_ready, 1)

            def left(c, b1, b2):
                for i in range(NSH, NE):
                    add(c, i)

            def right(c, g):
                wait_apart(pool, misc_free[0], PUSES * NB + AUSES * g, pool_passed)
                for i in range(NE):
                    if i < POOL_MUL:
                        multiply(g, i, 0)
                    if 10 <= i:
                        if i == 10:
                            wait_apart(pool, pr_ready, g + 1, pool_passed)
                        multiply(g, i - 10, 1)
                    if i >= NSH:
                        add(c, i)

            rounds(pool, lambda: None, left, right, lambda: None)

        @block.vector
        def _(v):
            own = Chain(v, dve_prep, 13 + 5 + 1 + 17)
            att = Chain(v, dve_att, 2 * (NB - POOL_MUL) + (NB - 1) + 3 + 3 * (NB - 1) + 1 + 2)

            def inverse_root(src, done):
                v.wait_ge(*done)
                own.link(v.reciprocal(r0[:, :], sd[:, :]))
                own.link(v.tensor_tensor(nt_[:, :], r0[:, :], r0[:, :], ALU.mult))
                own.link(v.tensor_tensor(nt_[:, :], nt_[:, :], src[:, :], ALU.mult))
                own.link(v.tensor_scalar(nt_[:, :], nt_[:, :], -0.5, 1.5, ALU.mult, ALU.add))
                own.link(v.tensor_tensor(rstd[:, :], r0[:, :], nt_[:, :], ALU.mult))

            def norm(b):
                own.round(b)
                for t in range(NT):
                    done = own.mark(v.bn_stats(stats[:, t, :], tok(x_all, b, t * P, P)))
                wait_apart(v, dve_prep, done, passed)
                for t in range(NT):
                    done = own.mark(v.bn_aggr(mv[:, t, :], stats[:, t, :]))
                own.wait(done)
                v.tensor_scalar(ve[:, :], mv[:, :, 1], LN_EPS, None, ALU.add).then_inc(stats_ready, 1)
                inverse_root(ve, (sd_ready, b + 1))
                ge(v, misc_full[0], PUSES * (b - 1) + 1)
                for t in range(NT):
                    ins = v.tensor_scalar(xn[:, t, :], tok(x_all, b, t * P, P), mv[:, t, 0:1], rstd[:, t:t + 1],
                                          ALU.subtract, ALU.mult)
                ins.then_inc(xn_ready, 1)

            def root_mean_square(b):
                v.wait_ge(ms_ready, NT * (b + 1))
                v.tensor_scalar(ve[:, :], ms[:, :], 1.0 / P, RMS_EPS, ALU.mult, ALU.add).then_inc(ve2_ready, 1)
                inverse_root(ve, (sd2_ready, b + 1))
                ge(v, misc_full[1], PUSES * (b - 1) + 1)
                for t in range(NT):
                    ins = v.tensor_scalar(xh[:, t, :], xn[:, t, :], rstd[:, t:t + 1], None, ALU.mult)
                ins.then_inc(xh_ready, 1)

            def keep_projections(b, t):
                v.wait_ge(misc_full[0], PUSES * b + 2 + t)
                v.tensor_tensor(qkv[:, bass.ds(b * NT + t, 1), :].rearrange("p a c -> p (a c)"), misc[0][:, 0:3 * P], bqkv[:, :], ALU.add)\
                    .then_inc(misc_free[0], 1)
                v.wait_ge(misc_full[1], PUSES * b + 2 + t)
                v.tensor_tensor(dl[:, bass.ds(b * NT + t, 1), :].rearrange("p a c -> p (a c)"), misc[1][:, 0:SD], bside[:, :], ALU.add)\
                    .then_inc(misc_free[1], 1)

            def logits(b):
                v.wait_ge(misc_free[1], PUSES * (b + 1))
                l = dl[:, bass.ds(b * NT, NT), ND:SD]
                own.link(v.tensor_reduce(lmax[:, :], l, AX.X, ALU.max))
                v.tensor_tensor(ld[:, :, :], l, lmax[:, :, None].broadcast_to([P, NT, NRT]), ALU.subtract).then_inc(ld_ready, 1)

            def choose(b):
                v.wait_ge(lex_ready, b + 1)
                wide = lambda t: t[:, :, None].broadcast_to([P, NT, NRT])
                own.link(v.tensor_reduce(lsum[:, :], lex[:, :, :], AX.X, ALU.add))
                own.link(v.reciprocal(lsum[:, :], lsum[:, :]))
                own.link_apart(v.tensor_tensor(lex[:, :, :], lex[:, :, :], wide(lsum), ALU.mult), passed)
                for t in range(NT):
                    done = own.mark(v.max(top[:, t, :], lex[:, t, :]))
                own.wait(done)
                own.link_apart(v.memset(top[:, :, 2:8], LARGE), passed)
                for t in range(NT):
                    done = own.mark(v.match_replace(rest[:, t, :], top[:, t, :], lex[:, t, :], -LARGE))
                own.wait(done)
                own.link(v.tensor_tensor(rest[:, :, :], rest[:, :, :], lex[:, :, :], ALU.not_equal))
                own.link(v.tensor_tensor(lex[:, :, :], lex[:, :, :], rest[:, :, :], ALU.mult))
                own.link(v.tensor_reduce(lsum[:, :], lex[:, :, :], AX.X, ALU.add))
                own.link(v.tensor_scalar(lsum[:, :], lsum[:, :], 1e-9, None, ALU.add))
                own.link(v.reciprocal(lsum[:, :], lsum[:, :]))
                v.tensor_tensor(gate[:, bass.ds(b * NT, NT), :], lex[:, :, :], wide(lsum), ALU.mult).then_inc(gate_ready, 1)
                own.end()

            def combine(c, i):
                n = c * NE + i
                v.wait_ge(w_full, n + 1)
                if i < NSH:
                    if i == 1:
                        v.wait_ge(shared_added, NSH * c + 1)
                    v.tensor_tensor(tok(x_all, c), w_bank[i % 2], tok(x_all, c), ALU.add).then_inc(shared_added, 1)
                    return
                e = i - NSH
                if i == NSH:
                    v.wait_ge(gate_ready, c + 1)
                ge(v, added, c * NRT + e - 1)
                g = gate[:, bass.ds(c * NT, NT), e:e + 1].broadcast_to([P, NT, P])
                v.tensor_tensor(scaled[:, i % 2, :].rearrange("p (t d) -> p t d", t=NT),
                                w_bank[i % 2].rearrange("p (t d) -> p t d", t=NT), g, ALU.mult).then_inc(scaled_ready, 1)

            v.wait_ge(w_loaded, 16 * NW)
            def setup(k, ins):
                ins.then_inc(knots_done, 1)
                v.wait_ge(knots_done, k)
            setup(1, v.tensor_copy(knots[:, 0:1], pe_rows[:, 0:1]))
            setup(2, v.tensor_tensor(knots[:, 1:], pe_rows[:, 1:], pe_rows[:, 0:NKNOT - 1], ALU.subtract))
            setup(3, v.tensor_copy(pe_rows[:, 1:], knots[:, 1:]))
            setup(4, v.tensor_tensor(knots[:, 2:], pe_rows[:, 2:], pe_rows[:, 1:NKNOT - 1], ALU.subtract))
            setup(5, v.tensor_scalar(knots[:, :], knots[:, :], 1.0 / SCALE, None, ALU.mult))
            v.tensor_tensor(pe_blk[:, :, :], knots[:, None, :].broadcast_to([P, H, NKNOT]), blockm[:, :, None].broadcast_to([P, H, NKNOT]),
                            ALU.mult).then_inc(blk_ready, 1)
            v.memset(bside[:, ND:SD], 0.0)
            v.tensor_copy(bqw[:, :], bqc[:, 0:1].broadcast_to([P, P])).then_inc(blk_ready, 1)
            v.wait_ge(side_full, 2)
            v.tensor_copy(wside[:, 0:ND], misc[0][:, 0:ND]).then_inc(side_ready, 1)
            v.tensor_copy(bside[:, 0:ND], misc[1][:, 0:ND]).then_inc(side_ready, 1)

            def multiply(g, s, kind):
                o = prodv[:, :].rearrange("p (h a b) -> p h a b", h=H, a=NB)
                a, b = factors(g, s, kind)
                att.link(v.tensor_tensor(o, a, b, ALU.mult))

            def reduce_products(g, s, kind):
                n = (2 * g + kind) * POOL_MUL + s
                o = sc[:, s, :, :] if kind == 0 else ao[:, s, :].rearrange("p (h d) -> p h d", h=H)
                if s < POOL_MUL:
                    v.wait_ge(sprod_ready, n + 1)
                    v.tensor_reduce(o, prod[:, s % 3, :].rearrange("p (h a b) -> p h a b", h=H, a=NB), AX.X, ALU.add)\
                        .then_inc(sprod_free, 1)
                else:
                    multiply(g, s, kind)
                    v.tensor_reduce(o, prodv[:, :].rearrange("p (h a b) -> p h a b", h=H, a=NB), AX.X, ALU.add)\
                        .then_inc(sc_ready if kind == 0 else ao_ready, 1)

            def positions(g):
                v.wait_ge(pos_ready, g + 1)
                for t in range(NB - 2, -1, -1):
                    att.link(v.tensor_tensor(pos[:, :, :, t], pos[:, :, :, t], pos[:, :, :, t + 1], ALU.add))
                L0 = group_knots(g, 0)
                att.link(v.tensor_tensor(lg[:, :, :, :], sc[:, :, :, :], L0[:, :, :, None].broadcast_to([P, NB, H, NB]), ALU.add))
                D0 = group_knots(g, 1)
                att.link(v.tensor_tensor(term[:, :, :, :], pos[:, :, :, :], D0[:, :, :, None].broadcast_to([P, NB, H, NB]), ALU.mult))
                att.link(v.tensor_tensor(lg[:, :, :, :], lg[:, :, :, :], term[:, :, :, :], ALU.add))

            def group_knots(g, n):
                return group(dl, g, 0, ND).rearrange("p s (h n) -> p s h n", n=NKNOT)[:, :, :, n]

            def knot(g, n):
                w = NB - n
                r = term[:, :, :, 0:w]
                D = group_knots(g, n + 1)[:, :, :, None].broadcast_to([P, NB, H, w])
                att.link(v.tensor_scalar(r, pos[:, :, :, 0:w], float(n), 0.0, ALU.subtract, ALU.max))
                att.link(v.tensor_tensor(r, r, D, ALU.mult))
                att.link(v.tensor_tensor(lg[:, :, :, 0:w], lg[:, :, :, 0:w], r, ALU.add))

            def subtract_maximum(g):
                att.link(v.tensor_reduce(smx[:, :, :], lg[:, :, :, :], AX.X, ALU.max))
                v.tensor_tensor(lg[:, :, :, :], lg[:, :, :, :], smx[:, :, :, None].broadcast_to([P, NB, H, NB]), ALU.subtract)\
                    .then_inc(lgm_ready, 1)

            def normalize(g):
                v.wait_ge(ex_ready, g + 1)
                att.link(v.tensor_reduce(smx[:, :, :], lg[:, :, :, :], AX.X, ALU.add))
                att.link(v.reciprocal(smx[:, :, :], smx[:, :, :]))
                v.tensor_tensor(lg[:, :, :, :], lg[:, :, :, :], smx[:, :, :, None].broadcast_to([P, NB, H, NB]), ALU.mult)\
                    .then_inc(pr_ready, 1)
                v.wait_ge(pr_ready, g + 1)

            def keep_attention(g):
                for half in range(2):
                    v.wait_ge(misc_full[half], PUSES * NB + AUSES * (g + 1))
                    o = group(qkv, g, 0, P)[:, half * NT:(half + 1) * NT, :]
                    v.tensor_tensor(o, misc[half].rearrange("p (s d) -> p s d", s=NT), bo[:, None, :].broadcast_to([P, NT, P]), ALU.add)\
                        .then_inc(misc_free[half], 1)

            def prepare(b, i):
                if i == 0:
                    norm(b)
                elif i == 1:
                    root_mean_square(b)
                elif 2 <= i < 2 + NT:
                    keep_projections(b, i - 2)
                    if i == 1 + NT:
                        logits(b)
                elif i == 7:
                    choose(b)

            def first():
                for i in range(8):
                    prepare(0, i)

            def left(c, b1, b2):
                for i in range(NE):
                    if i < 8:
                        prepare(b1, i)
                    elif b2 is not None:
                        prepare(b2, i - 8)
                    combine(c, i)

            def right(c, g):
                att.round(g)
                for i in range(NE):
                    combine(c, i)
                    if i < 6:
                        reduce_products(g, i, 0)
                    if i in (2, 4):
                        reduce_products(g, 5 + i // 2, 0)
                    if i == 6:
                        positions(g)
                    if i == 7:
                        for n in (1, 2, 3):
                            knot(g, n)
                    if i == 8:
                        for n in range(4, NB):
                            knot(g, n)
                        subtract_maximum(g)
                    if i == 9:
                        normalize(g)
                    if i >= 10:
                        reduce_products(g, i - 10, 1)
                    if i in (11, 13):
                        reduce_products(g, 6 + (i - 11) // 2, 1)
                keep_attention(g)
                att.end()

            def last():
                v.wait_ge(added, NRT * NB)
                v.wait_ge(misc_free[0], PUSES * NB + AUSES * NT)
                v.wait_ge(misc_free[1], PUSES * NB + AUSES * NT)
                for s in range(NB):
                    x = x_all[:, s * NTOK:(s + 1) * NTOK].rearrange("p (g d) -> p g d", g=NT)
                    v.tensor_tensor(x, x, qkv[:, s * NT:(s + 1) * NT, 0:P], ALU.add).then_inc(sum_ready, 1)

            rounds(v, first, left, right, last)

        @block.scalar
        def _(act):
            def norm(b):
                act.wait_ge(stats_ready, b + 1)
                act.activation(sd[:, :], ve[:, :], ACT.Sqrt).then_inc(sd_ready, 1)
                act.wait_ge(xn_ready, b + 1)
                for t in range(NT):
                    ge(act, ms_ready, NT * b + t)
                    act.activation(sq[:, :], xn[:, t, :], ACT.Square, accum_out=ms[:, t:t + 1]).then_inc(ms_ready, 1)

            def keep_transposes(b):
                act.wait_ge(ve2_ready, b + 1)
                act.activation(sd[:, :], ve[:, :], ACT.Sqrt).then_inc(sd2_ready, 1)
                act.wait_ge(misc_full[0], PUSES * b + 1)
                act.activation(xnT[:, :], misc[0], ACT.Copy).then_inc(misc_free[0], 1)
                act.wait_ge(misc_full[1], PUSES * b + 1)
                act.activation(tok(hT_all, b), misc[1], ACT.Copy).then_inc(misc_free[1], 1)

            def exponentials(b):
                act.wait_ge(ld_ready, b + 1)
                act.activation(lex[:, :, :], ld[:, :, :], ACT.Exp).then_inc(lex_ready, 1)

            def silu(c, i):
                n = c * NE + i
                act.wait_ge(a_full, n + 1)
                ge(act, w_full, n - 1)
                act.activation(hid[:, i % 2, :, :], a_bank[i % 2], ACT.Silu).then_inc(hid_ready, 1)

            def prepare(b, i):
                if i == 0:
                    norm(b)
                elif i == 1:
                    keep_transposes(b)
                elif i == 6:
                    exponentials(b)

            def first():
                for i in range(8):
                    prepare(0, i)

            def left(c, b1, b2):
                for i in range(NE):
                    if i < 8:
                        prepare(b1, i)
                    elif b2 is not None:
                        prepare(b2, i - 8)
                    silu(c, i)

            def right(c, g):
                for i in range(NE):
                    silu(c, i)
                    if i == 6:
                        act.wait_ge(sc_ready, (NB - POOL_MUL) * (g + 1))
                        act.wait_ge(sprod_free, POOL_MUL * (2 * g + 1))
                        act.activation(pos[:, :, :, :], sc[:, :, :, :], ACT.Sigmoid, scale=SCALE).then_inc(pos_ready, 1)
                    if i == 9:
                        act.wait_ge(lgm_ready, g + 1)
                        act.activation(lg[:, :, :, :], lg[:, :, :, :], ACT.Exp, scale=SCALE).then_inc(ex_ready, 1)
                for half in range(2):
                    act.wait_ge(misc_full[half], PUSES * NB + AUSES * g + 1)
                    if half == 1:
                        act.wait_ge(misc_full[0], PUSES * NB + AUSES * (g + 1))
                    act.activation(aoT[:, :], misc[half], ACT.Copy).then_inc(misc_free[half], 1)

            rounds(act, first, left, right, lambda: None)

        @block.tensor
        def _(pe):
            def mm(o, lhsT, rhs, start=True, stop=True):
                return nc.tensor.matmul(o, lhsT, rhs, start=start, stop=stop)

            def transposes(k, src):
                for t in range(NT):
                    last = nc.tensor.transpose(misc[k][:, t * P:(t + 1) * P], src(t), ident[:, :])
                last.then_inc(misc_full[k], 1)

            def prepare(b, i):
                if i == 0:
                    pe.wait_ge(xn_ready, b + 1)
                    ge(pe, misc_free[0], PUSES * b)
                    transposes(0, lambda t: xn[:, t, :])
                elif i == 1:
                    pe.wait_ge(xh_ready, b + 1)
                    ge(pe, misc_free[1], PUSES * b)
                    transposes(1, lambda t: xh[:, t, :])
                elif 2 <= i < 2 + NT:
                    t = i - 2
                    x = xnT[:, t * P:(t + 1) * P]
                    pe.wait_ge(misc_free[0], PUSES * b + 1 + t)
                    mm(misc[0][:, 0:3 * P], x, wqkv[:, :]).then_inc(misc_full[0], 1)
                    pe.wait_ge(misc_free[1], PUSES * b + 1 + t)
                    mm(misc[1][:, 0:SD], x, wside[:, :]).then_inc(misc_full[1], 1)

            def up(c, i):
                e = (i + NRT) % NE
                n = c * NE + i
                ge(pe, hid_ready, n - 1)
                if i == 0:
                    pe.wait_ge(misc_free[1], 1 + PUSES * c)
                for k in range(HID):
                    last = mm(a_bank[i % 2][:, k, :], w1[:, e * HID * P + k * P:e * HID * P + (k + 1) * P], tok(hT_all, c))
                last.then_inc(a_full, 1)

            def down(c, i):
                e = (i + NRT) % NE
                n = c * NE + i
                pe.wait_ge(hid_ready, n + 1)
                if i < NSH:
                    ge(pe, scaled_ready, NRT * (c - 1) + NRT - 1 + i)
                elif i < 2 * NSH:
                    pe.wait_ge(shared_added, NSH * c + i - NSH + 1)
                else:
                    pe.wait_ge(scaled_ready, NRT * c + i - 2 * NSH + 1)
                for t in range(NT):
                    for k in range(HID):
                        last = mm(w_bank[i % 2][:, t * P:(t + 1) * P], hid[:, i % 2, k, t * P:(t + 1) * P],
                                  w2[:, (e * HID + k) * P:(e * HID + k + 1) * P], start=(k == 0), stop=(k == HID - 1))
                last.then_inc(w_full, 1)

            pe.wait_ge(w_loaded, 16 * NW)
            pe.wait_ge(blk_ready, 2)
            blk = pe_blk[:, :, :].rearrange("p h n -> p (h n)")
            mm(misc[0][:, 0:ND], wqT[:, :], blk).then_inc(side_full, 1)
            mm(misc[1][:, 0:ND], bqw[:, :], blk).then_inc(side_full, 1)
            pe.wait_ge(side_ready, 2)

            def first():
                for i in range(8):
                    prepare(0, i)

            def left(c, b1, b2):
                up(c, 0)
                for i in range(NE):
                    if i < 8:
                        prepare(b1, i)
                    elif b2 is not None:
                        prepare(b2, i - 8)
                    if i + 1 < NE:
                        up(c, i + 1)
                    down(c, i)

            def right(c, g):
                up(c, 0)
                for i in range(NE):
                    if i + 1 < NE:
                        up(c, i + 1)
                    down(c, i)
                pe.wait_ge(sprod_free, POOL_MUL * 2 * (g + 1))
                pe.wait_ge(ao_ready, (NB - POOL_MUL) * (g + 1))
                for half in range(2):
                    pe.wait_ge(misc_free[half], PUSES * NB + AUSES * g)
                    transposes(half, lambda t: ao[:, half * NT + t, :])
                for half in range(2):
                    pe.wait_ge(misc_free[half], PUSES * NB + AUSES * g + 1)
                    for t in range(NT):
                        last = mm(misc[half][:, t * P:(t + 1) * P], aoT[:, t * P:(t + 1) * P], wo[:, :])
                    last.then_inc(misc_full[half], 1)

            rounds(pe, first, left, right, lambda: None)


def build(nc, m):
    with ExitStack() as ctx:
        sb = lambda n, s, d=F32: ctx.enter_context(nc.sbuf_tensor(n, s, d))
        m["ident"] = sb("ident", [P, P])
        m["rms"] = sb("rms", [P, E1])
        m["w1"] = sb("w1", [P, E1 * 2 * P])
        m["w2"] = sb("w2", [P, E1 * 2 * P])
        m["x_all"] = sb("x_all", [P, NTILE * P])
        with ExitStack() as first:
            sb1 = lambda n, s, d=F32: first.enter_context(nc.sbuf_tensor(n, s, d))
            m["v_all"] = sb1("v_all", [P, NTILE * P])
            m["yT_all"] = sb1("yT_all", [P, NTILE * P])
            m["qs"] = sb1("qs", [P, 2, H, NTOK], BF16)
            m["ks"] = sb1("ks", [P, 2, H, NTOK], BF16)
            m["zero"] = sb1("zero", [2, NTOK], BF16)
            m["one"] = sb1("one", [2, NTOK], BF16)
            m["vw"] = sb1("vw", [P, 2, NT, H, VW])
            m["qk_parts"] = nc.dram_tensor("qk_parts", [NB, 2, H, PARTS, HD, NTOK], BF16, kind="Internal").ap()
            with ExitStack() as c:
                prepare_and_mix(nc, c, m)
            with ExitStack() as c:
                attend(nc, c, m)
        with ExitStack() as c:
            second_layer(nc, c, m)


def _laid_out(a):
    import numpy as np

    tile = lambda v: np.ascontiguousarray(v)
    ups = np.concatenate([a["L1_ffn_w1"], a["L1_ffn_w1_s"]])
    downs = np.concatenate([a["L1_ffn_w2"], a["L1_ffn_w2_s"]])
    row = np.arange(P)[:, None]
    weight = np.arange(2 * L)[None, :]
    return {
        "x": tile(a["L0_attn_x"].reshape(NB, NT, P, P).transpose(0, 2, 1, 3)),
        "ident": np.eye(P, dtype=np.float32),
        "selcol": ((row % (2 * L) == weight) & (row < PARTS * 2 * L)).astype(np.float32),
        "blockm": (row // HD == np.arange(H)[None, :]).astype(np.float32),
        "wqkv0": tile(a["L0_attn_w_qkv"]),
        "PwT": tile(a["L0_ffn_P_w"].T),
        "UT": tile(np.concatenate([a["L0_ffn_U1"], a["L0_ffn_U2"], a["L0_ffn_U3"]]).T),
        "W1T": tile(a["L0_ffn_W1"].transpose(2, 0, 1)),
        "W2T": tile(a["L0_ffn_W2"].transpose(2, 0, 1)),
        "b2": tile(a["L0_ffn_b2"]),
        "wproj": tile(a["L0_attn_w_proj"]),
        "bproj": tile(a["L0_attn_b_proj"].reshape(P, 1)),
        "wqT": tile(a["L1_attn_Wq"].T),
        "bqc": tile(a["L1_attn_bq"].reshape(P, 1)),
        "pe_rows": tile(np.tile(a["L1_attn_pos_emb"][0, :, :NB + 1], (H, 1))),
        "wqkv1": tile(np.concatenate([a["L1_attn_Wq"], a["L1_attn_Wk"], a["L1_attn_Wv"]], axis=1)),
        "bqkv": tile(np.concatenate([a["L1_attn_bq"], a["L1_attn_bk"], a["L1_attn_bv"]]).reshape(1, 3 * P)),
        "wo": tile(a["L1_attn_Wo"]),
        "bo": tile(a["L1_attn_bo"].reshape(1, P)),
        "router": tile(a["L1_ffn_router_w"]),
        "rms": tile(np.concatenate([a["L1_ffn_rms_w"], a["L1_ffn_rms_w_s"]]).T),
        "w1": tile(ups.transpose(1, 0, 2).reshape(P, -1)),
        "w2": tile(downs.reshape(E1, 2, P, P).transpose(2, 0, 1, 3).reshape(P, -1)),
    }


def kernel(**inputs):
    import numpy as np
    import concourse.bacc as bacc
    from concourse.bass_utils import run_bass_kernel_spmd

    laid = _laid_out({k: np.asarray(v) for k, v in inputs.items()})
    nc = bacc.Bacc("TRN2", target_bir_lowering=False, num_devices=1)
    m = {}
    for name, a in laid.items():
        ap = nc.dram_tensor(f"in_{name}", a.shape, mybir.dt.from_np(a.dtype), kind="ExternalInput").ap()
        m["x" if name == "x" else name + "_d"] = ap
    m["out"] = nc.dram_tensor("out", [NB, P, NT, P], F32, kind="ExternalOutput").ap()
    build(nc, m)
    r = run_bass_kernel_spmd(nc, [{f"in_{k}": a for k, a in laid.items()}], core_ids=[0])
    return np.asarray(r.results[0]["out"]).transpose(0, 2, 1, 3).reshape(NB, NTOK, P)
```

```python
import concourse.bass as bass
from concourse import mybir
from contextlib import ExitStack

F32 = mybir.dt.float32
BF16 = mybir.dt.bfloat16
ALU = mybir.AluOpType
ACT = mybir.ActivationFunctionType
AX = mybir.AxisListType

P = 128
NB = 8
NTOK = 512
NT = NTOK // P
NTILE = NB * NT
H = 16
HD = P // H
L = 12
NR = 3
DA = 64
VW = 32
PARTS = 3
E1 = 16
LN_EPS = 1e-5
RMS_EPS = 1.1920929e-07
SCALE = float(HD) ** -0.5
LARGE = 3.0e38


def wait_apart(eng, sem, value, passed):
    eng.wait_ge(sem, value)
    eng.sem_inc(passed, 1)


class Chain:

    def __init__(self, eng, sem, per):
        self.eng, self.sem, self.per = eng, sem, per

    def round(self, b):
        self.base, self.k = b * self.per, 0

    def mark(self, ins):
        self.k += 1
        assert self.k <= self.per
        ins.then_inc(self.sem, 1)
        return self.base + self.k

    def wait(self, value):
        self.eng.wait_ge(self.sem, value)

    def link_apart(self, ins, passed):
        wait_apart(self.eng, self.sem, self.mark(ins), passed)

    def link(self, ins):
        self.wait(self.mark(ins))

    def end(self):
        assert self.k == self.per, (self.k, self.per)


def prepare_and_mix(nc, ctx, m):
    sb = lambda n, s, d=F32: ctx.enter_context(nc.sbuf_tensor(n, s, d))
    sem = lambda n: ctx.enter_context(nc.semaphore(n))
    x_all, v_all, yT_all, ident = m["x_all"], m["v_all"], m["yT_all"], m["ident"]
    RING = 4
    AHEAD = RING - 1
    qk_parts = m["qk_parts"]

    wqkv = sb("wqkv0", [P, 3 * P])
    PwT = sb("PwT", [P, DA])
    UT = sb("UT", [DA, NR * L])
    W1T = m["w2"][:, 0:L * P].rearrange("p (e d) -> p e d", e=L)
    W2T = m["w2"][:, L * P:2 * L * P].rearrange("p (e d) -> p e d", e=L)
    b2 = sb("b2", [L, P])
    selcol = sb("selcol", [P, 2 * L])
    sel = sb("sel", [P, 2 * L, P], BF16)
    identb = sb("identb", [P, P], BF16)

    stats = sb("stats", [P, NT, 6])
    mv = sb("mv", [P, NT, 2])
    ve = sb("ve", [P, NT])
    sd = sb("sd", [P, NT])
    r0 = sb("r0", [P, NT])
    nt_ = sb("nt_", [P, NT])
    rstd = sb("rstd", [P, NT])
    xn = sb("xn", [P, NT, P])
    xnT = sb("xnT", [P, 2, NTOK])
    split = sb("split", [P, 2, PARTS, NTOK], BF16)
    resid = sb("resid", [P, 2, NTOK])
    xa = sb("xa", [DA, NTOK])
    Z = sb("Z", [P, NT * NR, L])
    Zr = sb("Zr", [P, NT * NR, L])
    mx = sb("mx", [P, NT * NR, 8])
    Zd = sb("Zd", [P, NT * NR, L])
    Ex = sb("Ex", [P, NT * NR, L])
    Mk = sb("Mk", [P, NT * NR, L])
    Sm = sb("Sm", [P, NT * NR])
    C = sb("C", [P, NT * NR, L])
    Cs = sb("Cs", [P, NT, PARTS, 2, L], BF16)
    Cr = sb("Cr", [P, NT, 2, L])
    CsT = sb("CsT", [P, 2, NTOK], BF16)
    C3T = sb("C3T", [L, 2, NTOK])
    hT = m["w2"][:, 2 * L * P:2 * L * P + NTOK]
    xs_low = sb("xs", [P, RING - 1, NTOK])
    xs = [xs_low[:, k, :] for k in range(RING - 1)] + [m["w2"][:, 2 * L * P + NTOK:2 * L * P + 2 * NTOK]]

    banks = ctx.enter_context(nc.psum_tensor("banks0", [P, 8, NTOK], F32))
    prep_bank = [banks[:, 0, :], banks[:, 1, :]]
    bc_bank = [banks[:, 2 + i, :] for i in range(RING)]
    h_bank, y_bank = banks[:, 6, :], banks[:, 7, :]

    x_loaded, ident_loaded, w_loaded, passed = sem("x_loaded"), sem("ident_loaded"), sem("w_loaded"), sem("passed0")
    consts_ready, vw_clear, w1_loaded = sem("consts_ready"), sem("vw_clear"), sem("w1_loaded")
    stats_ready, sd_ready, xn_ready, dve_prep = sem("stats_ready"), sem("sd_ready"), sem("xn_ready"), sem("dve_prep")
    bank_full, bank_free = [sem("bank_full0"), sem("bank_full1")], [sem("bank_free0"), sem("bank_free1")]
    xnT_ready, high_ready, resid_ready, parts_ready, parts_stored = (sem("xnT_ready"), sem("high_ready"), sem("resid_ready"),
                                                      sem("parts_ready"), sem("parts_stored"))
    xa_ready, zd_ready, ex_ready, cs_ready, cT_ready = (sem("xa_ready"), sem("zd_ready"), sem("ex_ready"),
                                                        sem("cs_ready"), sem("cT_ready"))
    bc_ready, xs_ready, xs_used = sem("bc_ready"), sem("xs_ready"), sem("xs_used")
    gelu_done, y_done = sem("gelu_done"), sem("y_done")
    USES = 4
    NW = 7
    STORES = 16 * 2 * PARTS

    def tok(t, b, at=0, n=NTOK):
        return t[:, bass.ds(b * NTOK + at, n)]

    def rounds(eng, first, both):
        first()
        both(1, 1, 0, 0)
        with eng.Fori(1, NB // 2) as i:
            both(2 * i, 0, 2 * i - 1, 1)
            both(2 * i + 1, 1, 2 * i, 0)
        both(None, None, NB - 1, 1)

    with nc.Block() as block:
        @block.sync
        def _(sp):
            sp.dma_start(tok(x_all, 0).rearrange("p (t d) -> p t d", t=NT), m["x"][0]).then_inc(x_loaded, 16)
            sp.dma_start(ident[:, :], m["ident_d"]).then_inc(ident_loaded, 16)
            sp.dma_start(PwT[:, :], m["PwT_d"]).then_inc(w_loaded, 16)
            sp.dma_start(UT[:, :], m["UT_d"]).then_inc(w_loaded, 16)
            sp.dma_start(wqkv[:, :], m["wqkv0_d"]).then_inc(w_loaded, 16)
            sp.dma_start(selcol[:, :], m["selcol_d"]).then_inc(w_loaded, 16)
            sp.dma_start(W1T[:, :, :], m["W1T_d"]).then_inc(w_loaded, 16)
            sp.dma_start(W2T[:, :, :], m["W2T_d"]).then_inc(w_loaded, 16)
            sp.dma_start(b2[:, :], m["b2_d"]).then_inc(w_loaded, 16)
            sp.dma_start(m["rms"][:, :], m["rms_d"]).then_inc(w1_loaded, 16)
            sp.dma_start(m["w1"][:, :], m["w1_d"]).then_inc(w1_loaded, 16)
            with sp.Fori(1, NB) as b:
                sp.wait_ge(x_loaded, 16 * b)
                sp.dma_start(tok(x_all, b).rearrange("p (t d) -> p t d", t=NT),
                             m["x"][bass.ds(b, 1)].rearrange("a p t d -> p (a t) d")).then_inc(x_loaded, 16)
                for w in range(2):
                    sp.wait_ge(parts_ready, 2 * b - 1 + w)
                    for c in range(PARTS):
                        sp.dma_start(qk_parts[bass.ds(b - 1, 1), w, :, c].rearrange("a h d n -> (a h) d n"), split[:, w, c, :])\
                            .then_inc(parts_stored, 16)
            for w in range(2):
                sp.wait_ge(parts_ready, 2 * NB - 1 + w)
                for c in range(PARTS):
                    sp.dma_start(qk_parts[NB - 1, w, :, c], split[:, w, c, :]).then_inc(parts_stored, 16)
            sp.wait_ge(parts_stored, STORES * NB)

        @block.gpsimd
        def _(pool):
            pool.memset(CsT[:, :, :], 0.0).then_inc(consts_ready, 1)
            pool.memset(m["qs"][:, :, :, :].bitcast(F32), 0.0)
            pool.memset(m["ks"][:, :, :, :].bitcast(F32), 0.0)
            pool.memset(m["zero"][:, :], 0.0)
            pool.memset(m["one"][:, :], 1.0)
            pool.memset(m["vw"][:, :, :, :, :], 0.0).then_inc(vw_clear, 1)
            pool.wait_ge(vw_clear, 1)
            pool.memset(m["vw"][:, :, :, :, HD:HD + 1], 1.0)
            pool.wait_ge(w1_loaded, 32)
            for e in range(E1):
                w = m["w1"][:, e * 2 * P:(e + 1) * 2 * P]
                pool.tensor_scalar(w, w, m["rms"][:, e:e + 1], None, ALU.mult)

        @block.vector
        def _(v):
            own = Chain(v, dve_prep, 13 + 2 + 26 + 7)

            def moments(b):
                own.round(b)
                v.wait_ge(x_loaded, 16 * (b + 1))
                for t in range(NT):
                    done = own.mark(v.bn_stats(stats[:, t, :], tok(x_all, b, t * P, P)))
                wait_apart(v, dve_prep, done, passed)
                for t in range(NT):
                    done = own.mark(v.bn_aggr(mv[:, t, :], stats[:, t, :]))
                own.wait(done)
                v.tensor_scalar(ve[:, :], mv[:, :, 1], LN_EPS, None, ALU.add).then_inc(stats_ready, 1)

            def inverse_deviation(b):
                v.wait_ge(sd_ready, b + 1)
                own.link(v.reciprocal(r0[:, :], sd[:, :]))
                own.link(v.tensor_tensor(nt_[:, :], r0[:, :], r0[:, :], ALU.mult))
                own.link(v.tensor_tensor(nt_[:, :], nt_[:, :], ve[:, :], ALU.mult))
                own.link(v.tensor_scalar(nt_[:, :], nt_[:, :], -0.5, 1.5, ALU.mult, ALU.add))
                own.link(v.tensor_tensor(rstd[:, :], r0[:, :], nt_[:, :], ALU.mult))

            def norm(b):
                if not isinstance(b, int) or b > 0:
                    v.wait_ge(bank_full[0], USES * (b - 1) + 1)
                for t in range(NT):
                    ins = v.tensor_scalar(xn[:, t, :], tok(x_all, b, t * P, P), mv[:, t, 0:1], rstd[:, t:t + 1],
                                          ALU.subtract, ALU.mult)
                ins.then_inc(xn_ready, 1)

            def residual(b, w):
                v.wait_ge(high_ready, 2 * b + w + 1)
                v.tensor_tensor(resid[:, w, :], prep_bank[1 - w], split[:, w, 0, :], ALU.subtract).then_inc(bank_free[1 - w], 1)

            def low_parts(b, w):
                v.wait_ge(bank_free[1 - w], USES * b + (2 if w == 0 else 3))
                own.link(v.tensor_copy(split[:, w, 1, :], resid[:, w, :]))
                v.tensor_tensor(split[:, w, 2, :], resid[:, w, :], split[:, w, 1, :], ALU.subtract).then_inc(parts_ready, 1)

            def keep_scores(b):
                v.wait_ge(bank_full[0], USES * b + 2)
                v.tensor_copy(Z[:, :, :].rearrange("p a e -> p (a e)"), prep_bank[0][:, 0:NT * NR * L]).then_inc(bank_free[0], 1)
                wait_apart(v, bank_free[0], USES * b + 2, passed)
                for i in range(NT * NR):
                    done = own.mark(v.max(mx[:, i, :], Z[:, i, :]))
                own.wait(done)
                v.tensor_tensor(Zd[:, :, :], Z[:, :, :], mx[:, :, 0:1].broadcast_to([P, NT * NR, L]), ALU.subtract).then_inc(zd_ready, 1)

            def choose(b):
                own.link_apart(v.memset(mx[:, :, 3:8], LARGE), passed)
                for i in range(NT * NR):
                    done = own.mark(v.match_replace(Zr[:, i, :], mx[:, i, :], Z[:, i, :], -LARGE))
                own.wait(done)
                own.link(v.tensor_tensor(Mk[:, :, :], Zr[:, :, :], Z[:, :, :], ALU.not_equal))

            def weigh(b):
                v.wait_ge(ex_ready, b + 1)
                own.link(v.tensor_tensor(Mk[:, :, :], Mk[:, :, :], Ex[:, :, :], ALU.mult))
                own.link(v.tensor_reduce(Sm[:, :], Mk[:, :, :], AX.X, ALU.add))
                own.link(v.reciprocal(Sm[:, :], Sm[:, :]))
                own.link(v.tensor_tensor(C[:, :, :], Mk[:, :, :], Sm[:, :, None].broadcast_to([P, NT * NR, L]), ALU.mult))

            def split_weights(b):
                C12 = C[:, :, :].rearrange("p (t r) e -> p t r e", r=NR)[:, :, 0:2, :]
                own.link(v.tensor_copy(Cs[:, :, 0, :, :], C12))
                own.link(v.tensor_tensor(Cr[:, :, :, :], C12, Cs[:, :, 0, :, :], ALU.subtract))
                own.link(v.tensor_copy(Cs[:, :, 1, :, :], Cr[:, :, :, :]))
                v.tensor_tensor(Cs[:, :, 2, :, :], Cr[:, :, :, :], Cs[:, :, 1, :, :], ALU.subtract).then_inc(cs_ready, 1)

            def scale_inputs(b, par, e):
                n = 2 * L * b + e
                src = xnT[:, par, :] if e < L else hT[:, :]
                if e == L:
                    v.wait_ge(gelu_done, b + 1)
                v.wait_ge(bc_ready, n + 1)
                if not isinstance(b, int) or b > 0 or e >= RING:
                    v.wait_ge(xs_used, n - RING + 1)
                v.tensor_tensor(xs[e % RING], bc_bank[e % RING], src, ALU.mult).then_inc(xs_ready, 1)

            def first():
                moments(0)
                inverse_deviation(0)
                norm(0)
                v.wait_ge(ident_loaded, 16)
                v.tensor_copy(identb[:, :], ident[:, :]).then_inc(consts_ready, 1)
                v.wait_ge(w_loaded, 16 * NW)
                v.tensor_copy(sel[:, :, :], selcol[:, :, None].broadcast_to([P, 2 * L, P])).then_inc(consts_ready, 1)
                keep_scores(0)
                choose(0)
                weigh(0)
                split_weights(0)
                residual(0, 0)
                residual(0, 1)
                low_parts(0, 0)
                low_parts(0, 1)
                own.end()

            def both(b, par, a, apar):
                for e in range(2 * L):
                    if b is not None:
                        if e == 1:
                            moments(b)
                        if e == 5:
                            inverse_deviation(b)
                            norm(b)
                        if e == 11:
                            keep_scores(b)
                        if e == L:
                            choose(b)
                            weigh(b)
                            split_weights(b)
                        if e == L + 4:
                            residual(b, 0)
                        if e == L + 5:
                            residual(b, 1)
                        if e == L + 7:
                            low_parts(b, 0)
                        if e == L + 9:
                            low_parts(b, 1)
                            own.end()
                    scale_inputs(a, apar, e)

            rounds(v, first, both)

        @block.scalar
        def _(act):
            def deviation(b):
                act.wait_ge(stats_ready, b + 1)
                act.activation(sd[:, :], ve[:, :], ACT.Sqrt).then_inc(sd_ready, 1)

            def evacuate_norm(b, par):
                act.wait_ge(bank_full[0], USES * b + 1)
                if not isinstance(b, int) or b > 1:
                    act.wait_ge(xs_ready, 2 * L * (b - 1))
                act.activation(xnT[:, par, :], prep_bank[0], ACT.Copy).then_inc(bank_free[0], 1)

            def high_parts(b):
                for w in range(2):
                    act.wait_ge(bank_full[1 - w], USES * b + (2 if w == 0 else 3))
                    if not isinstance(b, int) or b > 0:
                        act.wait_ge(parts_stored, STORES * b)
                    act.activation(split[:, w, 0, :], prep_bank[1 - w], ACT.Copy).then_inc(high_ready, 1)

            def address(b):
                act.wait_ge(bank_full[1], USES * b + 1)
                act.activation(xa[:, :], prep_bank[1][0:DA, :], ACT.Copy).then_inc(bank_free[1], 1)

            def values(b):
                act.wait_ge(bank_full[1], USES * b + 4)
                act.activation(tok(v_all, b), prep_bank[1], ACT.Copy).then_inc(bank_free[1], 1)

            def exponentials(b):
                act.wait_ge(zd_ready, b + 1)
                act.activation(Ex[:, :, :], Zd[:, :, :], ACT.Exp).then_inc(ex_ready, 1)

            def weights_transposed(b, par):
                act.wait_ge(bank_full[1], USES * b + 3)
                act.activation(C3T[:, par, :], prep_bank[1][0:L, :], ACT.Copy).then_inc(bank_free[1], 1)
                act.wait_ge(bank_full[0], USES * b + 4)
                act.activation(CsT[0:PARTS * 2 * L, par, :], prep_bank[0].bitcast(BF16)[0:PARTS * 2 * L, 0:NTOK], ACT.Copy)\
                    .then_inc(bank_free[0], 1)

            def gelu(b):
                act.wait_ge(xs_used, 2 * L * b + L)
                act.activation(hT[:, :], h_bank, ACT.Gelu).then_inc(gelu_done, 1)

            def keep_mixture(b):
                act.wait_ge(xs_used, 2 * L * (b + 1))
                act.activation(tok(yT_all, b), y_bank, ACT.Copy).then_inc(y_done, 1)

            def first():
                deviation(0)
                evacuate_norm(0, 0)
                address(0)
                exponentials(0)
                high_parts(0)
                act.wait_ge(consts_ready, 3)
                weights_transposed(0, 0)
                values(0)

            def both(b, par, a, apar):
                if b is not None:
                    deviation(b)
                    evacuate_norm(b, par)
                    address(b)
                    exponentials(b)
                gelu(a)
                if b is not None:
                    high_parts(b)
                    weights_transposed(b, par)
                    values(b)
                keep_mixture(a)

            rounds(act, first, both)

        @block.tensor
        def _(pe):
            def claim(b, k):
                if not isinstance(b, int) or b > 0 or k >= 2:
                    pe.wait_ge(bank_free[k % 2], USES * b + k // 2)
                return prep_bank[k % 2]

            def mm(out, lhsT, rhs, start=True, stop=True):
                return nc.tensor.matmul(out, lhsT, rhs, start=start, stop=stop)

            def transpose_norm(b):
                pe.wait_ge(xn_ready, b + 1)
                o = claim(b, 0)
                for t in range(NT):
                    last = nc.tensor.transpose(o[:, t * P:(t + 1) * P], xn[:, t, :], ident[:, :])
                last.then_inc(bank_full[0], 1)

            def address(b, par):
                pe.wait_ge(bank_free[0], USES * b + 1)
                mm(claim(b, 1)[0:DA, :], PwT[:, :], xnT[:, par, :]).then_inc(bank_full[1], 1)

            def scores(b):
                pe.wait_ge(bank_free[1], USES * b + 1)
                o = claim(b, 2)
                for t in range(NT):
                    last = mm(o[:, t * NR * L:(t + 1) * NR * L], xa[:, t * P:(t + 1) * P], UT[:, :])
                last.then_inc(bank_full[0], 1)

            def queries_keys(b, par):
                mm(claim(b, 3), wqkv[:, 0:P], xnT[:, par, :]).then_inc(bank_full[1], 1)
                mm(claim(b, 4), wqkv[:, P:2 * P], xnT[:, par, :]).then_inc(bank_full[0], 1)

            def transpose_weights(b):
                pe.wait_ge(cs_ready, b + 1)
                o = claim(b, 5)
                for t in range(NT):
                    last = nc.tensor.transpose(o[0:L, t * P:(t + 1) * P], C[:, t * NR + 2, :], ident[:, :])
                last.then_inc(bank_full[1], 1)
                o = claim(b, 6).bitcast(BF16)
                for t in range(NT):
                    last = nc.tensor.transpose(o[0:PARTS * 2 * L, t * P:(t + 1) * P], Cs[:, t, :, :, :].rearrange("p c r e -> p (c r e)"), identb[:, :])
                last.then_inc(bank_full[0], 1)

            def values(b, par):
                o = claim(b, 7)
                for t in range(NT):
                    last = mm(o[:, t * P:(t + 1) * P], xnT[:, par, t * P:(t + 1) * P], wqkv[:, 2 * P:3 * P])
                last.then_inc(bank_full[1], 1)

            def broadcast_weight(b, par, e):
                n = 2 * L * b + e
                if not isinstance(b, int) or b > 0 or e >= RING:
                    pe.wait_ge(xs_ready, n - RING + 1)
                if e == 0:
                    pe.wait_ge(bank_free[0], USES * (b + 1))
                mm(bc_bank[e % RING], sel[:, e, :], CsT[:, par, :]).then_inc(bc_ready, 1)

            def accumulate(b, par, e):
                n = 2 * L * b + e
                if e == 0 and (not isinstance(b, int) or b > 0):
                    pe.wait_ge(gelu_done, b)
                if e == L:
                    if not isinstance(b, int) or b > 0:
                        pe.wait_ge(y_done, b)
                    pe.wait_ge(bank_free[1], USES * b + 3)
                    mm(y_bank, b2[:, :], C3T[:, par, :], stop=False)
                pe.wait_ge(xs_ready, n + 1)
                w = (W1T if e < L else W2T)[:, e % L, :]
                mm(h_bank if e < L else y_bank, w, xs[e % RING], start=(e == 0), stop=(e % L == L - 1))\
                    .then_inc(xs_used, 1)

            def first():
                pe.wait_ge(ident_loaded, 16)
                transpose_norm(0)
                pe.wait_ge(w_loaded, 16 * NW)
                address(0, 0)
                scores(0)
                queries_keys(0, 0)
                pe.wait_ge(consts_ready, 3)
                transpose_weights(0)
                values(0, 0)
                for e in range(AHEAD):
                    broadcast_weight(0, 0, e)

            def both(b, par, a, apar):
                for e in range(2 * L):
                    if e + AHEAD < 2 * L:
                        broadcast_weight(a, apar, e + AHEAD)
                    elif b is not None:
                        broadcast_weight(b, par, e + AHEAD - 2 * L)
                    accumulate(a, apar, e)
                    if b is not None:
                        if e == 3:
                            transpose_norm(b)
                        if e == 5:
                            address(b, par)
                        if e == 7:
                            scores(b)
                        if e == L - 1:
                            queries_keys(b, par)
                        if e == L + 4:
                            transpose_weights(b)
                        if e == L + 6:
                            values(b, par)

            rounds(pe, first, both)


def attend(nc, ctx, m):
    sb = lambda n, s, d=F32: ctx.enter_context(nc.sbuf_tensor(n, s, d))
    sem = lambda n: ctx.enter_context(nc.semaphore(n))
    x_all, v_all, yT_all, ident = m["x_all"], m["v_all"], m["yT_all"], m["ident"]
    qk_parts = m["qk_parts"]
    NPROD = PARTS * PARTS
    ROWS = NPROD * HD
    OCT, QUAD = 8, 4
    UNITS = OCT * NT
    STEPS = UNITS // QUAD
    LEAD = 3

    qs, ks, vw, zero, one = m["qs"], m["ks"], m["vw"], m["zero"], m["one"]
    wproj = sb("wproj", [P, P])
    bproj = sb("bproj", [P, 1])
    identb = sb("identb1", [P, P], BF16)
    probs = sb("probs", [P, 2, QUAD, NTOK])
    mx = sb("mx1", [P, 2, OCT * NT])
    mhl = sb("mhl", [P, 2, 4, OCT * NT], BF16)
    mT = sb("mT", [2 * OCT * NT, 2, P], BF16)
    oT = sb("oT", [P, 2, NTOK])
    rden = sb("rden", [P, NT, QUAD])
    att = sb("att", [P, NT, P])
    attT = sb("attT", [P, NTOK])
    x1T = sb("x1T", [P, NTOK])

    banks = ctx.enter_context(nc.psum_tensor("banks1", [P, 8, NTOK], F32))
    RING = 3
    e_bank = [banks[:, i, :] for i in range(RING)]
    s_bank = [banks[:, RING + i, :] for i in range(RING)]
    o_bank, misc = banks[:, 6, :], banks[:, 7, :]

    w_loaded, w2_loaded, filled = sem("w_loaded1"), sem("w2_loaded"), sem("filled1")
    stack_loaded = [[sem(f"stack_loaded{p}{o}") for o in range(2)] for p in range(2)]
    m_loaded = [sem("m_loaded0"), sem("m_loaded1")]
    v_ready = sem("v_ready")
    s_full, s_free, e_full, exp_done, av_done = sem("s_full"), sem("s_free"), sem("e_full"), sem("exp_done"), sem("av_done")
    m_hi, m_split, mt_full, mt_free = sem("m_hi"), sem("m_split"), sem("mt_full"), sem("mt_free")
    o_kept, ot_full, rden_ready, ot_free = sem("o_kept"), sem("ot_full"), sem("rden_ready"), sem("ot_free")
    at_full, at_free, pj_full, pj_free, xt_full, xt_free = (sem("at_full"), sem("at_free"), sem("pj_full"),
                                                            sem("pj_free"), sem("xt_full"), sem("xt_free"))
    LOADS = PARTS * PARTS + PARTS + 1

    def tok(t, b, at=0, n=NTOK):
        return t[:, bass.ds(b * NTOK + at, n)]

    def ge(eng, s, value):
        if not isinstance(value, int) or value > 0:
            eng.wait_ge(s, value)

    def slot(par, o, u):
        return ((2 * par + o) * UNITS + u) % RING

    def readers(par, o, b, u):
        at = (2 * par + o) * UNITS + u
        back = RING if at >= RING else at + 4 * UNITS - max(i for i in range(4 * UNITS) if i % RING == at % RING)
        return (2 * b + o) * UNITS + (u - back + 1)

    def rounds(eng, first, octet, last):
        first()
        def pair(b, end):
            for r in range(4):
                octet(b + r // 2, r // 2, r % 2, not end or r < 3, not end or r < 2)
        pair(0, False)
        with eng.Fori(1, NB // 2 - 1) as i:
            pair(2 * i, False)
        pair(NB - 2, True)
        last()

    with nc.Block() as block:
        @block.sync
        def _(sp):
            def gather(b, par, o):
                s = stack_loaded[par][o]
                heads = slice(o * OCT, (o + 1) * OCT)
                for a in range(PARTS):
                    lo = a * PARTS * HD
                    sp.dma_start(ks[lo:lo + PARTS * HD, par, heads, :],
                                 qk_parts[b, 1, heads].rearrange("h c d n -> (c d) h n") if isinstance(b, int) else
                                 qk_parts[bass.ds(b, 1), 1, heads].rearrange("a h c d n -> (a c d) h n")).then_inc(s, 16)
                    for c in range(PARTS):
                        at = lo + c * HD
                        sp.dma_start(qs[at:at + HD, par, heads, :],
                                     qk_parts[b, 0, heads, a].rearrange("h d n -> d h n") if isinstance(b, int) else
                                     qk_parts[bass.ds(b, 1), 0, heads, a].rearrange("a h d n -> (a d) h n")).then_inc(s, 16)
                sp.dma_start(qs[ROWS:ROWS + 2, par, heads, :], zero[:, None, :].broadcast_to([2, OCT, NTOK])).then_inc(s, 16)

            def put_maxima(b, par, o):
                n = 2 * b + o
                sp.wait_ge(mt_free, n + 1)
                sp.dma_start(qs[ROWS:ROWS + 2, par, o * OCT:(o + 1) * OCT, :], mT[:, o, :]).then_inc(m_loaded[o], 16)

            sp.dma_start(wproj[:, :], m["wproj_d"]).then_inc(w_loaded, 16)
            sp.dma_start(bproj[:, :], m["bproj_d"]).then_inc(w_loaded, 16)
            for par in range(2):
                sp.dma_start(ks[ROWS:ROWS + 2, par, :, :], one[:, None, :].broadcast_to([2, H, NTOK])).then_inc(filled, 16)

            def first():
                gather(0, 0, 0)
                gather(0, 0, 1)
                put_maxima(0, 0, 0)

            def octet(b, pb, o, more1, more2):
                if more2:
                    ge(sp, e_full, 2 * UNITS * b)
                    gather(b + 1, 1 - pb, o)
                if more1:
                    put_maxima(b + o, (pb + o) % 2, 1 - o)

            sp.dma_start(m["w2"][:, :], m["w2_d"]).then_inc(w2_loaded, 16)
            rounds(sp, first, octet, lambda: None)
            sp.wait_ge(w2_loaded, 16)
            for o in range(2):
                sp.wait_ge(m_loaded[o], 16 * NB)

        @block.gpsimd
        def _(pool):
            def spread(b, par):
                pool.tensor_copy(vw[:, par, :, :, 0:HD], tok(v_all, b).rearrange("p (t h d) -> p t h d", t=NT, h=H))\
                    .then_inc(v_ready, 1)

            def octet(b, pb, o, more1, more2):
                if o == 0 and more2:
                    ge(pool, av_done, 2 * STEPS * b)
                    spread(b + 1, 1 - pb)

            rounds(pool, lambda: spread(0, 0), octet, lambda: None)

        @block.vector
        def _(v):
            v.memset(mhl[:, :, 2:4, :], 0.0)
            v.tensor_copy(identb[:, :], ident[:, :]).then_inc(filled, 1)

            def maxima(b, par, o, s, js=range(QUAD)):
                for j in js:
                    u = s * QUAD + j
                    n = (2 * b + o) * UNITS + u
                    v.wait_ge(s_full, n + 1)
                    if u == 0:
                        ge(v, m_split, 2 * b + o - 1)
                    v.tensor_reduce(mx[:, o, u:u + 1], s_bank[slot(par, o, u)], AX.X, ALU.max).then_inc(s_free, 1)

            def split_maxima(b, o):
                n = 2 * b + o
                v.wait_ge(s_free, UNITS * (n + 1))
                ge(v, mt_full, n - 1)
                v.tensor_scalar(mhl[:, o, 0, :], mx[:, o, :], -1.0, None, ALU.mult).then_inc(m_hi, 1)
                v.wait_ge(m_hi, n + 1)
                v.scalar_tensor_tensor(mhl[:, o, 1, :], mx[:, o, :], -1.0, mhl[:, o, 0, :], ALU.mult, ALU.subtract)\
                    .then_inc(m_split, 1)

            def normalize(b, quad):
                g = QUAD * b + quad
                v.wait_ge(ot_full, g + 1)
                o = misc.rearrange("p (t j c) -> p t j c", t=NT, j=QUAD)
                v.reciprocal(rden[:, :, :], o[:, :, :, HD]).then_inc(rden_ready, 1)
                v.wait_ge(rden_ready, g + 1)
                if quad == 0:
                    ge(v, at_full, b)
                v.tensor_tensor(att[:, :, quad * QUAD * HD:(quad + 1) * QUAD * HD].rearrange("p t (j d) -> p t j d", d=HD),
                                o[:, :, :, 0:HD], rden[:, :, :, None].broadcast_to([P, NT, QUAD, HD]), ALU.mult)\
                    .then_inc(ot_free, 1)

            def add_mixture(b):
                v.wait_ge(pj_full, b + 1)
                ge(v, xt_full, b)
                v.scalar_tensor_tensor(x1T[:, :], misc, bproj[:, 0:1], tok(yT_all, b), ALU.add, ALU.add).then_inc(pj_free, 1)

            def add_input(b):
                v.wait_ge(xt_full, b + 1)
                v.tensor_tensor(tok(x_all, b), misc, tok(x_all, b), ALU.add).then_inc(xt_free, 1)

            def first():
                v.wait_ge(w_loaded, 32)
                for s in range(STEPS):
                    maxima(0, 0, 0, s)
                split_maxima(0, 0)
                for s in range(LEAD):
                    maxima(0, 0, 1, s)

            def octet(b, pb, o, more1, more2):
                begin = isinstance(b, int) and b == 0 and o == 0
                for s in range(STEPS):
                    for js in ((0, 1), (2, 3)):
                        if s < STEPS - LEAD:
                            if more1:
                                maxima(b + o, (pb + o) % 2, 1 - o, s + LEAD, js)
                        elif more2:
                            maxima(b + 1, 1 - pb, o, s + LEAD - STEPS, js)
                        if js[0] == 0:
                            if s == 2 and not begin:
                                normalize(b - 1 + o, 3 if o == 0 else 1)
                            if o == 0 and not begin:
                                if s == 4:
                                    add_mixture(b - 1)
                                if s == 5:
                                    add_input(b - 1)
                            if s == 7:
                                normalize(b, 2 * o)
                    if s == STEPS - LEAD - 1 and more1:
                        split_maxima(b + o, 1 - o)

            def last():
                normalize(NB - 1, 3)
                add_mixture(NB - 1)
                add_input(NB - 1)

            rounds(v, first, octet, last)

        @block.scalar
        def _(act):
            def exponentiate(b, par, o, s, js):
                g = (2 * b + o) * STEPS + s
                for j in js:
                    act.wait_ge(e_full, g * QUAD + j + 1)
                    if j == 0:
                        ge(act, av_done, g - 1)
                    act.activation(probs[:, s % 2, j, :], e_bank[slot(par, o, s * QUAD + j)], ACT.Exp, scale=SCALE).then_inc(exp_done, 1)

            def keep_products(b, quad):
                g = QUAD * b + quad
                act.wait_ge(av_done, NT * (g + 1))
                ge(act, ot_full, g - 1)
                act.activation(oT[:, quad % 2, :], o_bank, ACT.Copy).then_inc(o_kept, 1)

            def keep_maxima(b, o):
                n = 2 * b + o
                act.wait_ge(mt_full, n + 1)
                ge(act, m_loaded[o], 16 * b)
                act.activation(mT[:, o, :], misc.bitcast(BF16)[0:2 * OCT * NT, 0:P], ACT.Copy).then_inc(mt_free, 1)

            def keep_attention(b):
                act.wait_ge(at_full, b + 1)
                act.activation(attT[:, :], misc, ACT.Copy).then_inc(at_free, 1)

            def octet(b, pb, o, more1, more2):
                begin = isinstance(b, int) and b == 0 and o == 0
                for s in range(STEPS):
                    exponentiate(b, pb, o, s, (0, 1))
                    if s == 3 and o == 0 and not begin:
                        keep_attention(b - 1)
                    if s == 6 and more1:
                        keep_maxima(b + o, 1 - o)
                    exponentiate(b, pb, o, s, (2, 3))
                    if s == 0 and not begin:
                        keep_products(b - 1 + o, 3 if o == 0 else 1)
                    if s == 4:
                        keep_products(b, 2 * o)

            def last():
                keep_products(NB - 1, 3)
                keep_attention(NB - 1)

            rounds(act, lambda: keep_maxima(0, 0), octet, last)

        @block.tensor
        def _(pe):
            def mm(out, lhsT, rhs, start=True, stop=True):
                return nc.tensor.matmul(out, lhsT, rhs, start=start, stop=stop)

            def score(b, par, o, s, js=range(QUAD)):
                if s == 0 and js[0] == 0:
                    pe.wait_ge(stack_loaded[par][o], 16 * LOADS * (b // 2 + 1) if isinstance(b, int) else 8 * LOADS * (b - par + 2))
                for j in js:
                    u = s * QUAD + j
                    h, t = o * OCT + u // NT, u % NT
                    ge(pe, s_free, readers(par, o, b, u))
                    mm(s_bank[slot(par, o, u)], qs[:, par, h, t * P:(t + 1) * P], ks[:, par, h, :]).then_inc(s_full, 1)

            def shifted(b, par, o, s, js):
                if s == 0 and js[0] == 0:
                    pe.wait_ge(m_loaded[o], 16 * (b + 1))
                t = s % NT
                for j in js:
                    h = o * OCT + s // NT * QUAD + j
                    if j != 2:
                        ge(pe, exp_done, readers(par, o, b, s * QUAD + j))
                    mm(e_bank[slot(par, o, s * QUAD + j)], ks[:, par, h, t * P:(t + 1) * P], qs[:, par, h, :]).then_inc(e_full, 1)

            def values(b, par, o, s):
                g = (2 * b + o) * STEPS + s
                t = s % NT
                if o == 0 and s == 0:
                    pe.wait_ge(v_ready, b + 1)
                if t == 0:
                    ge(pe, o_kept, (2 * b + o) * 2 + s // NT)
                pe.wait_ge(exp_done, (g + 1) * QUAD)
                for j in range(QUAD):
                    h = o * OCT + s // NT * QUAD + j
                    last = mm(o_bank[j * VW:(j + 1) * VW, :], vw[:, par, t, h, :], probs[:, s % 2, j, :],
                              start=(t == 0), stop=(t == NT - 1))
                last.then_inc(av_done, 1)

            def transposes(src, full):
                for t in range(NT):
                    last = nc.tensor.transpose(misc[:, t * P:(t + 1) * P], src(t), ident[:, :])
                last.then_inc(full, 1)

            def transpose_maxima(b, o, before, count):
                n = 2 * b + o
                ge(pe, before, count)
                pe.wait_ge(m_split, n + 1)
                nc.tensor.transpose(misc.bitcast(BF16)[:, 0:P], mhl[:, o, :, :].rearrange("p c u -> p (c u)"),
                                    identb[:, :]).then_inc(mt_full, 1)

            def transpose_products(b, quad, before, count):
                ge(pe, before, count)
                pe.wait_ge(o_kept, QUAD * b + quad + 1)
                transposes(lambda t: oT[:, quad % 2, t * P:(t + 1) * P], ot_full)

            def transpose_attention(b):
                pe.wait_ge(ot_free, QUAD * (b + 1))
                transposes(lambda t: att[:, t, :], at_full)

            def project(b):
                pe.wait_ge(at_free, b + 1)
                mm(misc, wproj[:, :], attT[:, :]).then_inc(pj_full, 1)

            def transpose_sum(b):
                pe.wait_ge(pj_free, b + 1)
                transposes(lambda t: x1T[:, t * P:(t + 1) * P], xt_full)

            pe.wait_ge(filled, 33)
            pe.wait_ge(w_loaded, 32)

            def first():
                for s in range(STEPS):
                    score(0, 0, 0, s)
                transpose_maxima(0, 0, mt_free, 0)
                for s in range(LEAD):
                    score(0, 0, 1, s)

            def octet(b, pb, o, more1, more2):
                begin = isinstance(b, int) and b == 0 and o == 0
                n = 2 * b + o
                for s in range(STEPS):
                    for j in range(QUAD):
                        if s < STEPS - LEAD:
                            if more1:
                                score(b + o, (pb + o) % 2, 1 - o, s + LEAD, [j])
                        elif more2:
                            score(b + 1, 1 - pb, o, s + LEAD - STEPS, [j])
                        shifted(b, pb, o, s, [j])
                        if j == 1:
                            if s > 0:
                                values(b, pb, o, s - 1)
                            elif not begin:
                                values(b - 1 + o, (pb + 1 + o) % 2, 1 - o, STEPS - 1)
                    if s == 1 and not begin:
                        transpose_products(b - 1 + o, 3 if o == 0 else 1, ot_free, 2 * n - 1)
                    if o == 0 and not begin:
                        if s == 2:
                            transpose_attention(b - 1)
                        if s == 3:
                            project(b - 1)
                        if s == 4:
                            transpose_sum(b - 1)
                    if s == 5 and more1:
                        if o == 1:
                            transpose_maxima(b + o, 1 - o, ot_free, 2 * n)
                        elif begin:
                            transpose_maxima(b, 1, mt_free, 1)
                        else:
                            transpose_maxima(b, 1, xt_free, b)
                    if s == 6:
                        if more1:
                            transpose_products(b, 2 * o, mt_free, n + 2)
                        else:
                            transpose_products(b, 2 * o, ot_free, 2 * n)

            def last():
                values(NB - 1, 1, 1, STEPS - 1)
                transpose_products(NB - 1, 3, ot_free, QUAD * NB - 1)
                transpose_attention(NB - 1)
                project(NB - 1)
                transpose_sum(NB - 1)

            rounds(pe, first, octet, last)


def second_layer(nc, ctx, m):
    sb = lambda n, s, d=F32: ctx.enter_context(nc.sbuf_tensor(n, s, d))
    sem = lambda n: ctx.enter_context(nc.semaphore(n))
    x_all, ident, w1, w2, rms = m["x_all"], m["ident"], m["w1"], m["w2"], m["rms"]
    out = m["out"]
    NE, NSH = 16, 2
    NRT = NE - NSH
    HID = 2
    NKNOT = NB + 1
    ND = H * NKNOT
    SD = ND + NRT
    HT = H * NB

    hT_all = sb("hT_all", [P, NTILE * P])
    qkv = sb("qkv_all", [P, NTILE, 3 * P])
    dl = sb("dl_all", [P, NTILE, SD])
    gate = sb("gate_all", [P, NTILE, NRT])
    wqkv = sb("wqkv1", [P, 3 * P])
    wside = sb("wside", [P, SD])
    bqkv = sb("bqkv", [P, 3 * P])
    bside = sb("bside", [P, SD])
    wqT = sb("wqT", [P, P])
    bqc = sb("bqc", [P, 1])
    bqw = sb("bqw", [P, P])
    pe_rows = sb("pe_rows", [P, NKNOT])
    knots = sb("knots", [P, NKNOT])
    blockm = sb("blockm", [P, H])
    pe_blk = sb("pe_blk", [P, H, NKNOT])
    wo = sb("wo", [P, P])
    bo = sb("bo", [P, P])
    stats, mv = sb("stats2", [P, NT, 6]), sb("mv2", [P, NT, 2])
    ve, sd, r0, nt_, rstd = (sb(n, [P, NT]) for n in ("ve2", "sd2", "r02", "nt2", "rstd2"))
    norms, xnT, sq = sb("norms", [P, 2 * NT, P]), sb("xnT2", [P, NTOK]), sb("sq", [P, P])
    xn, xh = norms[:, 0:NT, :], norms[:, NT:2 * NT, :]
    ms = sb("ms", [P, NT])
    lmax, ld, lex, lsum = sb("lmax", [P, NT]), sb("ld", [P, NT, NRT]), sb("lex", [P, NT, NRT]), sb("lsum", [P, NT])
    top, rest = sb("top", [P, NT, 8]), sb("rest", [P, NT, NRT])
    hid = sb("hid", [P, 2, HID, NTOK])
    scaled = sb("scaled", [P, 2, NTOK])
    prod = sb("prod", [P, 3, HT * HD])
    prodv = norms[:, :, :].rearrange("p t d -> p (t d)")
    sc, pos, lg = (sb(n, [P, NB, H, NB]) for n in ("sc", "pos", "lg"))
    minus = sb("minus", [P, NB])
    ramps = sb("ramps", [P, H * NB * NB * (NB - 1) // 2])
    smx = sb("smx", [P, NB, H])
    ao = sb("ao", [P, NB, P])
    aoT = xnT

    banks = ctx.enter_context(nc.psum_tensor("banks2", [P, 8, NTOK], F32))
    a_bank = [banks[:, 0:2, :], banks[:, 2:4, :]]
    w_bank = [banks[:, 4, :], banks[:, 5, :]]
    misc = [banks[:, 6, :], banks[:, 7, :]]

    w_loaded, knots_done, blk_ready = sem("w_loaded2"), sem("knots_done"), sem("blk_ready")
    passed, pool_passed = sem("passed2"), sem("pool_passed")
    side_full, side_ready = sem("side_full"), sem("side_ready")
    stats_ready, sd_ready, xn_ready, ms_ready, ve2_ready, sd2_ready, xh_ready, dve_prep, dve_routing = (
        sem(n) for n in ("stats_ready2", "sd_ready2", "xn_ready2", "ms_ready", "msv_ready", "sdr_ready", "xh_ready", "dve_prep2",
                         "dve_routing2"))
    misc_full, misc_free = [sem("misc_full0"), sem("misc_full1")], [sem("misc_free0"), sem("misc_free1")]
    ld_ready, lex_ready, gate_ready = sem("ld_ready"), sem("lex_ready"), sem("gate_ready")
    a_full, hid_ready, w_full, added = sem("a_full"), sem("hid_ready"), sem("w_full"), sem("added")
    scaled_left, scaled_right, shared_added = sem("scaled_left"), sem("scaled_right"), sem("shared_added")
    ramp_ready, mul_done, lg_done = sem("ramp_ready"), [sem("mulq_done"), sem("mulv_done")], sem("lg_done")
    prod_ready, prod_free = [sem("qprod_ready"), sem("vprod_ready")], [sem("qprod_free"), sem("vprod_free")]
    sc_ready, pos_ready, lgm_ready, ex_ready, pr_ready, ao_ready, dve_att = (
        sem(n) for n in ("sc_ready", "sig_ready", "lgm_ready", "ex_ready2", "pr_ready", "ao_ready", "dve_att"))
    att_done, sum_ready, out_done = sem("att_done"), sem("sum_ready"), sem("out_done")
    NW = 9
    PUSES = 1 + NT
    AUSES = 2
    POOL_MUL = 6

    def tok(t, b, at=0, n=NTOK):
        return t[:, bass.ds(b * NTOK + at, n)]

    def ge(eng, s, value):
        if not isinstance(value, int) or value > 0:
            eng.wait_ge(s, value)

    def rounds(eng, first, left, right, last):
        first()
        left(0, 1, 2)
        with eng.Fori(1, NB // 2 - 1) as c:
            left(c, 2 * c + 1, 2 * c + 2)
        left(NB // 2 - 1, NB - 1, None)
        right(NB // 2, 0)
        with eng.Fori(1, NT - 1) as g:
            right(g + NB // 2, g)
        right(NB - 1, NT - 1)
        last()

    def ramp(n):
        w = NB - n
        at = HT * sum(NB - k for k in range(1, n))
        return ramps[:, at:at + HT * w].rearrange("p (s h t) -> p s h t", s=NB, h=H)

    def group(t, g, lo, hi):
        v = t[:, :, :].rearrange("p (s g) c -> p g s c", g=NT)
        return v[:, bass.ds(g, 1), :, lo:hi].rearrange("p a s c -> p (a s) c")

    def factors(g, s, kind):
        if kind == 0:
            q = group(qkv, g, 0, P)[:, s, :].rearrange("p (h d) -> p h d", h=H)[:, :, None, :].broadcast_to([P, H, NB, HD])
            k = group(qkv, g, P, 2 * P).rearrange("p t (h d) -> p h t d", h=H)
            return q, k
        w = lg[:, s, :, None, :].broadcast_to([P, H, HD, NB])
        v = group(qkv, g, 2 * P, 3 * P).rearrange("p t (h d) -> p h d t", h=H)
        return w, v

    with nc.Block() as block:
        @block.sync
        def _(sp):
            for dst, name in ((wqT, "wqT"), (bqc, "bqc"), (pe_rows, "pe_rows"), (blockm, "blockm"), (wqkv, "wqkv1"), (wo, "wo")):
                sp.dma_start(dst[:, :], m[name + "_d"]).then_inc(w_loaded, 16)
            sp.dma_start(wside[:, ND:SD], m["router_d"]).then_inc(w_loaded, 16)
            sp.dma_start(bqkv[:, :], m["bqkv_d"].broadcast_to([P, 3 * P])).then_inc(w_loaded, 16)
            sp.dma_start(bo[:, :], m["bo_d"].broadcast_to([P, P])).then_inc(w_loaded, 16)
            for s in range(NB):
                sp.wait_ge(sum_ready, s + 1)
                sp.dma_start(out[s], x_all[:, s * NTOK:(s + 1) * NTOK].rearrange("p (g d) -> p g d", g=NT)).then_inc(out_done, 16)
            sp.wait_ge(out_done, 16 * NB)

        @block.gpsimd
        def _(pool):
            def add(c, i, ready, base):
                n = c * NRT + i - NSH
                wait_apart(pool, ready, n + 1 - base, pool_passed)
                pool.tensor_tensor(tok(x_all, c), tok(x_all, c), scaled[:, i % 2, :], ALU.add).then_inc(added, 1)
                wait_apart(pool, added, n + 1, pool_passed)

            def multiply(g, s, kind, before=None):
                if s >= 3:
                    before = prod_free[kind], POOL_MUL * g + s - 2
                if before is not None:
                    wait_apart(pool, *before, pool_passed)
                o = prod[:, s % 3, :].rearrange("p (h a b) -> p h a b", h=H, a=NB)
                pool.tensor_tensor(o, *factors(g, s, kind), ALU.mult).then_inc(prod_ready[kind], 1)

            def left(c, b1, b2):
                for i in range(NE):
                    if i >= NSH:
                        add(c, i, scaled_left, 0)
                    if b2 is None and 8 <= i < 8 + POOL_MUL:
                        if i == 8:
                            pool.wait_ge(misc_free[0], PUSES * NB)
                        multiply(0, i - 8, 0)

            def right(c, g):
                first, final = isinstance(g, int) and g == 0, isinstance(g, int) and g == NT - 1
                for i in range(NE):
                    if 1 <= i < 1 + POOL_MUL and not final:
                        multiply(g + 1, i - 1, 0, None if first else (prod_free[1], POOL_MUL * g + i - 3))
                    if 9 <= i < 9 + POOL_MUL:
                        if i == 9:
                            wait_apart(pool, pr_ready, g + 1, pool_passed)
                        multiply(g, i - 9, 1, (prod_free[1], POOL_MUL * g + i - 11) if final else
                                 (prod_free[0], POOL_MUL * (g + 1) + i - 5))
                    if i >= NSH:
                        add(c, i, scaled_right, NRT * NB // 2)

            rounds(pool, lambda: None, left, right, lambda: None)

        @block.vector
        def _(v):
            own = Chain(v, dve_prep, 13 + 5 + 1)
            routing = Chain(v, dve_routing, 17)
            att = Chain(v, dve_att, (NB - 1) + 2 * (NB - 1) + 3 + 1 + 2)

            def inverse_root(src, done):
                v.wait_ge(*done)
                own.link(v.reciprocal(r0[:, :], sd[:, :]))
                own.link(v.tensor_tensor(nt_[:, :], r0[:, :], r0[:, :], ALU.mult))
                own.link(v.tensor_tensor(nt_[:, :], nt_[:, :], src[:, :], ALU.mult))
                own.link(v.tensor_scalar(nt_[:, :], nt_[:, :], -0.5, 1.5, ALU.mult, ALU.add))
                own.link(v.tensor_tensor(rstd[:, :], r0[:, :], nt_[:, :], ALU.mult))

            def norm(b):
                own.round(b)
                for t in range(NT):
                    done = own.mark(v.bn_stats(stats[:, t, :], tok(x_all, b, t * P, P)))
                wait_apart(v, dve_prep, done, passed)
                for t in range(NT):
                    done = own.mark(v.bn_aggr(mv[:, t, :], stats[:, t, :]))
                own.wait(done)
                v.tensor_scalar(ve[:, :], mv[:, :, 1], LN_EPS, None, ALU.add).then_inc(stats_ready, 1)

            def make_norm(b):
                inverse_root(ve, (sd_ready, b + 1))
                ge(v, misc_full[0], PUSES * (b - 1) + 1)
                for t in range(NT):
                    ins = v.tensor_scalar(xn[:, t, :], tok(x_all, b, t * P, P), mv[:, t, 0:1], rstd[:, t:t + 1],
                                          ALU.subtract, ALU.mult)
                ins.then_inc(xn_ready, 1)

            def mean_squares(b):
                v.wait_ge(ms_ready, NT * (b + 1))
                v.tensor_scalar(ve[:, :], ms[:, :], 1.0 / P, RMS_EPS, ALU.mult, ALU.add).then_inc(ve2_ready, 1)

            def root_mean_square(b):
                inverse_root(ve, (sd2_ready, b + 1))
                ge(v, misc_full[1], PUSES * (b - 1) + 1)
                for t in range(NT):
                    ins = v.tensor_scalar(xh[:, t, :], xn[:, t, :], rstd[:, t:t + 1], None, ALU.mult)
                ins.then_inc(xh_ready, 1)

            def keep_projections(b, t):
                v.wait_ge(misc_full[0], PUSES * b + 2 + t)
                v.tensor_tensor(qkv[:, bass.ds(b * NT + t, 1), :].rearrange("p a c -> p (a c)"), misc[0][:, 0:3 * P], bqkv[:, :], ALU.add)\
                    .then_inc(misc_free[0], 1)
                v.wait_ge(misc_full[1], PUSES * b + 2 + t)
                v.tensor_tensor(dl[:, bass.ds(b * NT + t, 1), :].rearrange("p a c -> p (a c)"), misc[1][:, 0:SD], bside[:, :], ALU.add)\
                    .then_inc(misc_free[1], 1)

            def logits(b):
                v.wait_ge(misc_free[1], PUSES * (b + 1))
                l = dl[:, bass.ds(b * NT, NT), ND:SD]
                own.link(v.tensor_reduce(lmax[:, :], l, AX.X, ALU.max))
                v.tensor_tensor(ld[:, :, :], l, lmax[:, :, None].broadcast_to([P, NT, NRT]), ALU.subtract).then_inc(ld_ready, 1)
                own.end()

            def choose(b):
                routing.round(b)
                v.wait_ge(lex_ready, b + 1)
                wide = lambda t: t[:, :, None].broadcast_to([P, NT, NRT])
                routing.link(v.tensor_reduce(lsum[:, :], lex[:, :, :], AX.X, ALU.add))
                routing.link(v.reciprocal(lsum[:, :], lsum[:, :]))
                routing.link_apart(v.tensor_tensor(lex[:, :, :], lex[:, :, :], wide(lsum), ALU.mult), passed)
                for t in range(NT):
                    done = routing.mark(v.max(top[:, t, :], lex[:, t, :]))
                routing.wait(done)
                routing.link_apart(v.memset(top[:, :, 2:8], LARGE), passed)
                for t in range(NT):
                    done = routing.mark(v.match_replace(rest[:, t, :], top[:, t, :], lex[:, t, :], -LARGE))
                routing.wait(done)
                routing.link(v.tensor_tensor(rest[:, :, :], rest[:, :, :], lex[:, :, :], ALU.not_equal))
                routing.link(v.tensor_tensor(lex[:, :, :], lex[:, :, :], rest[:, :, :], ALU.mult))
                routing.link(v.tensor_reduce(lsum[:, :], lex[:, :, :], AX.X, ALU.add))
                routing.link(v.tensor_scalar(lsum[:, :], lsum[:, :], 1e-9, None, ALU.add))
                routing.link(v.reciprocal(lsum[:, :], lsum[:, :]))
                v.tensor_tensor(gate[:, bass.ds(b * NT, NT), :], lex[:, :, :], wide(lsum), ALU.mult).then_inc(gate_ready, 1)
                routing.end()

            def add_shared(c, i):
                v.wait_ge(w_full, c * NE + i + 1)
                if i == 1:
                    v.wait_ge(shared_added, NSH * c + 1)
                v.tensor_tensor(tok(x_all, c), w_bank[i % 2], tok(x_all, c), ALU.add).then_inc(shared_added, 1)

            def scale_routed(c, i):
                e = i - NSH
                v.wait_ge(w_full, c * NE + i + 1)
                if i == NSH:
                    v.wait_ge(gate_ready, c + 1)
                ge(v, added, c * NRT + e - 1)
                g = gate[:, bass.ds(c * NT, NT), e:e + 1].broadcast_to([P, NT, P])
                v.tensor_tensor(scaled[:, i % 2, :].rearrange("p (t d) -> p t d", t=NT),
                                w_bank[i % 2].rearrange("p (t d) -> p t d", t=NT), g, ALU.mult).then_inc(scaled_left, 1)

            v.wait_ge(w_loaded, 16 * NW)
            def setup(k, ins):
                ins.then_inc(knots_done, 1)
                v.wait_ge(knots_done, k)
            setup(1, v.tensor_copy(knots[:, 0:1], pe_rows[:, 0:1]))
            setup(2, v.tensor_tensor(knots[:, 1:], pe_rows[:, 1:], pe_rows[:, 0:NKNOT - 1], ALU.subtract))
            setup(3, v.tensor_copy(pe_rows[:, 1:], knots[:, 1:]))
            setup(4, v.tensor_tensor(knots[:, 2:], pe_rows[:, 2:], pe_rows[:, 1:NKNOT - 1], ALU.subtract))
            setup(5, v.tensor_scalar(knots[:, :], knots[:, :], 1.0 / SCALE, None, ALU.mult))
            v.tensor_tensor(pe_blk[:, :, :], knots[:, None, :].broadcast_to([P, H, NKNOT]), blockm[:, :, None].broadcast_to([P, H, NKNOT]),
                            ALU.mult).then_inc(blk_ready, 1)
            v.memset(bside[:, ND:SD], 0.0)
            for n in range(NB):
                v.memset(minus[:, n:n + 1], -float(n))
            v.tensor_copy(bqw[:, :], bqc[:, 0:1].broadcast_to([P, P])).then_inc(blk_ready, 1)
            v.wait_ge(side_full, 2)
            v.tensor_copy(wside[:, 0:ND], misc[0][:, 0:ND]).then_inc(side_ready, 1)
            v.tensor_copy(bside[:, 0:ND], misc[1][:, 0:ND]).then_inc(side_ready, 1)

            def reduce_products(g, s, kind):
                o = sc[:, s, :, :] if kind == 0 else ao[:, s, :].rearrange("p (h d) -> p h d", h=H)
                if s < POOL_MUL:
                    v.wait_ge(prod_ready[kind], POOL_MUL * g + s + 1)
                    v.tensor_reduce(o, prod[:, s % 3, :].rearrange("p (h a b) -> p h a b", h=H, a=NB), AX.X, ALU.add)\
                        .then_inc(prod_free[kind], 1)
                else:
                    own_count, n = NB - POOL_MUL, s - POOL_MUL
                    if kind == 0:
                        ge(v, sc_ready, own_count * g + n)
                        if n == 0:
                            ge(v, ao_ready, own_count * (g - 1))
                    elif n == 0:
                        final = isinstance(g, int) and g == NT - 1
                        v.wait_ge(sc_ready, own_count * (NT if final else g + 2))
                    else:
                        v.wait_ge(ao_ready, own_count * g + n)
                    p = prodv.rearrange("p (h a b) -> p h a b", h=H, a=NB)
                    v.tensor_tensor(p, *factors(g, s, kind), ALU.mult).then_inc(mul_done[kind], 1)
                    v.wait_ge(mul_done[kind], (NB - POOL_MUL) * g + s - POOL_MUL + 1)
                    v.tensor_reduce(o, p, AX.X, ALU.add).then_inc(sc_ready if kind == 0 else ao_ready, 1)

            def positions(g):
                v.wait_ge(pos_ready, g + 1)
                for t in range(NB - 2, -1, -1):
                    done = att.mark(v.tensor_tensor(pos[:, :, :, t], pos[:, :, :, t], pos[:, :, :, t + 1], ALU.add))
                    att.wait(done)
                v.sem_inc(lg_done, 1)
                att.link(v.tensor_tensor(lg[:, :, :, :], sc[:, :, :, :], group_knots(g, 0)[:, :, :, None].broadcast_to([P, NB, H, NB]),
                                         ALU.add))

            def first_slope(g):
                D0 = group_knots(g, 1)
                v.wait_ge(ramp_ready, (NB - 1) * (g + 1))
                att.link(v.tensor_tensor(pos[:, :, :, :], pos[:, :, :, :], D0[:, :, :, None].broadcast_to([P, NB, H, NB]), ALU.mult))
                att.link(v.tensor_tensor(lg[:, :, :, :], lg[:, :, :, :], pos[:, :, :, :], ALU.add))

            def group_knots(g, n):
                return group(dl, g, 0, ND).rearrange("p s (h n) -> p s h n", n=NKNOT)[:, :, :, n]

            def knot(g, n):
                w = NB - n
                r = ramp(n)
                D = group_knots(g, n + 1)[:, :, :, None].broadcast_to([P, NB, H, w])
                v.wait_ge(ramp_ready, (NB - 1) * g + n)
                att.link(v.tensor_tensor(r, r, D, ALU.mult))
                att.link(v.tensor_tensor(lg[:, :, :, 0:w], lg[:, :, :, 0:w], r, ALU.add))

            def subtract_maximum(g):
                att.link(v.tensor_reduce(smx[:, :, :], lg[:, :, :, :], AX.X, ALU.max))
                v.tensor_tensor(lg[:, :, :, :], lg[:, :, :, :], smx[:, :, :, None].broadcast_to([P, NB, H, NB]), ALU.subtract)\
                    .then_inc(lgm_ready, 1)

            def normalize(g):
                v.wait_ge(ex_ready, g + 1)
                att.link(v.tensor_reduce(smx[:, :, :], lg[:, :, :, :], AX.X, ALU.add))
                att.link(v.reciprocal(smx[:, :, :], smx[:, :, :]))
                v.tensor_tensor(lg[:, :, :, :], lg[:, :, :, :], smx[:, :, :, None].broadcast_to([P, NB, H, NB]), ALU.mult)\
                    .then_inc(pr_ready, 1)
                v.wait_ge(pr_ready, g + 1)

            def keep_attention(g, half):
                v.wait_ge(misc_full[half], PUSES * NB + AUSES * (g + 1))
                o = group(qkv, g, 0, P)[:, half * NT:(half + 1) * NT, :]
                v.tensor_tensor(o, misc[half].rearrange("p (s d) -> p s d", s=NT), bo[:, None, :].broadcast_to([P, NT, P]), ALU.add)\
                    .then_inc(misc_free[half], 1)

            def prepare(b, i):
                if i == 0:
                    norm(b)
                elif i == 1:
                    make_norm(b)
                elif i == 2:
                    mean_squares(b)
                elif i == 3:
                    root_mean_square(b)
                elif i == 4:
                    keep_projections(b, 0)
                elif i == 5:
                    keep_projections(b, 1)
                    keep_projections(b, 2)
                elif i == 6:
                    keep_projections(b, 3)
                    logits(b)

            def first():
                for i in range(8):
                    prepare(0, i)

            def left(c, b1, b2):
                for i in range(NE):
                    if i < 8:
                        if i == 0:
                            choose(2 * c)
                        prepare(b1, i)
                    else:
                        if i == 8:
                            choose(b1)
                        if b2 is not None:
                            prepare(b2, i - 8)
                        else:
                            reduce_products(0, {8: 6, 15: 7}.get(i, i - 9), 0)
                    if i < NSH:
                        add_shared(c, i)
                    else:
                        scale_routed(c, i)

            def right(c, g):
                first, final = isinstance(g, int) and g == 0, isinstance(g, int) and g == NT - 1
                att.round(g)
                for i in range(NE):
                    if i < NSH:
                        add_shared(c, i)
                    if i == 1:
                        positions(g)
                    if i == 2 and not first:
                        keep_attention(g - 1, 0)
                        keep_attention(g - 1, 1)
                    if 2 <= i < 2 + POOL_MUL and not final:
                        reduce_products(g + 1, i - 2, 0)
                    for n in {3: (1,), 4: (2,), 5: (3, 4), 6: (5, 6, 7)}.get(i, ()):
                        knot(g, n)
                    if i == 7:
                        first_slope(g)
                    if i == 8:
                        subtract_maximum(g)
                    if i == 9:
                        normalize(g)
                    if 8 <= i < 10 and not final:
                        reduce_products(g + 1, i - 2, 0)
                    if 10 <= i:
                        reduce_products(g, i - 10, 1)
                    if i in (11, 12):
                        reduce_products(g, i - 5, 1)
                att.end()

            def last():
                keep_attention(NT - 1, 0)
                keep_attention(NT - 1, 1)
                v.wait_ge(added, NRT * NB)
                v.wait_ge(misc_free[0], PUSES * NB + AUSES * NT)
                v.wait_ge(misc_free[1], PUSES * NB + AUSES * NT)
                for s in range(NB):
                    x = x_all[:, s * NTOK:(s + 1) * NTOK].rearrange("p (g d) -> p g d", g=NT)
                    v.tensor_tensor(x, x, qkv[:, s * NT:(s + 1) * NT, 0:P], ALU.add).then_inc(sum_ready, 1)

            rounds(v, first, left, right, last)

        @block.scalar
        def _(act):
            def deviation(b):
                act.wait_ge(stats_ready, b + 1)
                act.activation(sd[:, :], ve[:, :], ACT.Sqrt).then_inc(sd_ready, 1)

            def squares(b):
                act.wait_ge(xn_ready, b + 1)
                for t in range(NT):
                    ge(act, ms_ready, NT * b + t)
                    act.activation(sq[:, :], xn[:, t, :], ACT.Square, accum_out=ms[:, t:t + 1]).then_inc(ms_ready, 1)

            def root_mean_square(b):
                act.wait_ge(ve2_ready, b + 1)
                act.activation(sd[:, :], ve[:, :], ACT.Sqrt).then_inc(sd2_ready, 1)

            def keep_norm(b):
                act.wait_ge(misc_full[0], PUSES * b + 1)
                act.activation(xnT[:, :], misc[0], ACT.Copy).then_inc(misc_free[0], 1)

            def keep_hidden_input(b):
                act.wait_ge(misc_full[1], PUSES * b + 1)
                act.activation(tok(hT_all, b), misc[1], ACT.Copy).then_inc(misc_free[1], 1)

            def exponentials(b):
                act.wait_ge(ld_ready, b + 1)
                act.activation(lex[:, :, :], ld[:, :, :], ACT.Exp).then_inc(lex_ready, 1)

            def silu(c, i):
                n = c * NE + i
                act.wait_ge(a_full, n + 1)
                ge(act, w_full, n - 1)
                act.activation(hid[:, i % 2, :, :], a_bank[i % 2], ACT.Silu).then_inc(hid_ready, 1)

            def prepare(b, i):
                if i == 0:
                    deviation(b)
                elif i == 1:
                    squares(b)
                elif i == 2:
                    root_mean_square(b)
                    keep_norm(b)
                elif i == 4:
                    keep_hidden_input(b)
                elif i == 7:
                    exponentials(b)

            def scale_routed(c, i):
                e = i - NSH
                act.wait_ge(w_full, c * NE + i + 1)
                if i == NSH:
                    act.wait_ge(gate_ready, NB)
                act.wait_ge(added, c * NRT + e - 1)
                for t in range(NT):
                    last = act.activation(scaled[:, i % 2, t * P:(t + 1) * P], w_bank[i % 2][:, t * P:(t + 1) * P], ACT.Copy,
                                          scale=gate[:, bass.ds(c * NT + t, 1), e:e + 1].rearrange("p a b -> p (a b)"))
                last.then_inc(scaled_right, 1)

            def first():
                for i in range(8):
                    prepare(0, i)

            def left(c, b1, b2):
                for i in range(NE):
                    silu(c, i)
                    if i < 8:
                        prepare(b1, i)
                    elif b2 is not None:
                        prepare(b2, i - 8)

            def right(c, g):
                first = isinstance(g, int) and g == 0
                for i in range(NE):
                    silu(c, i)
                    if i == 0:
                        act.wait_ge(sc_ready, (NB - POOL_MUL) * (g + 1))
                        act.wait_ge(prod_free[0], POOL_MUL * (g + 1))
                        act.activation(pos[:, :, :, :], sc[:, :, :, :], ACT.Sigmoid, scale=SCALE).then_inc(pos_ready, 1)
                    if i == 1 and not first:
                        keep_transposed(g - 1, 0)
                    if i == 2 and not first:
                        keep_transposed(g - 1, 1)
                    for n in {2: (1, 2), 3: (3, 4), 4: (5, 6, 7)}.get(i, ()):
                        if n == 1:
                            act.wait_ge(lg_done, g + 1)
                        act.activation(ramp(n), pos[:, :, :, 0:NB - n], ACT.Relu, bias=minus[:, n:n + 1]).then_inc(ramp_ready, 1)
                    if i == 9:
                        act.wait_ge(lgm_ready, g + 1)
                        act.activation(lg[:, :, :, :], lg[:, :, :, :], ACT.Exp, scale=SCALE).then_inc(ex_ready, 1)
                    if i > NSH:
                        scale_routed(c, i - 1)
                scale_routed(c, NE - 1)

            def keep_transposed(g, half):
                act.wait_ge(misc_full[half], PUSES * NB + AUSES * g + 1)
                if half == 1:
                    act.wait_ge(misc_full[0], PUSES * NB + AUSES * (g + 1))
                act.activation(aoT[:, :], misc[half], ACT.Copy).then_inc(misc_free[half], 1)

            def last():
                keep_transposed(NT - 1, 0)
                keep_transposed(NT - 1, 1)

            rounds(act, first, left, right, last)

        @block.tensor
        def _(pe):
            def mm(o, lhsT, rhs, start=True, stop=True):
                return nc.tensor.matmul(o, lhsT, rhs, start=start, stop=stop)

            def transposes(k, src):
                for t in range(NT):
                    last = nc.tensor.transpose(misc[k][:, t * P:(t + 1) * P], src(t), ident[:, :])
                last.then_inc(misc_full[k], 1)

            def project(b, t):
                x = xnT[:, t * P:(t + 1) * P]
                pe.wait_ge(misc_free[0], PUSES * b + 1 + t)
                mm(misc[0][:, 0:3 * P], x, wqkv[:, :]).then_inc(misc_full[0], 1)
                pe.wait_ge(misc_free[1], PUSES * b + 1 + t)
                mm(misc[1][:, 0:SD], x, wside[:, :]).then_inc(misc_full[1], 1)

            def prepare(b, i, late):
                if i == 2 and not late:
                    pe.wait_ge(xn_ready, b + 1)
                    ge(pe, misc_free[0], PUSES * b)
                    transposes(0, lambda t: xn[:, t, :])
                elif i == 4 and not late:
                    pe.wait_ge(xh_ready, b + 1)
                    ge(pe, misc_free[1], PUSES * b)
                    transposes(1, lambda t: xh[:, t, :])
                elif i == 4 and late:
                    project(b, 0)
                elif i == 5:
                    project(b, 2 if late else 1)
                elif i == 6 and not late:
                    project(b, 3)

            def up(c, i):
                e = (i + NRT) % NE
                n = c * NE + i
                ge(pe, hid_ready, n - 1)
                if i == 0:
                    pe.wait_ge(misc_free[1], 1 + PUSES * c)
                for k in range(HID):
                    last = mm(a_bank[i % 2][:, k, :], w1[:, e * HID * P + k * P:e * HID * P + (k + 1) * P], tok(hT_all, c))
                last.then_inc(a_full, 1)

            def down(c, i, right_half):
                e = (i + NRT) % NE
                n = c * NE + i
                pe.wait_ge(hid_ready, n + 1)
                half = NB // 2
                if i < NSH:
                    if isinstance(c, int) and c == half:
                        pe.wait_ge(scaled_left, NRT * (c - 1) + NRT - 1 + i)
                    elif right_half:
                        pe.wait_ge(scaled_right, NRT * (c - half - 1) + NRT - 1 + i)
                    else:
                        ge(pe, scaled_left, NRT * (c - 1) + NRT - 1 + i)
                elif i < 2 * NSH:
                    pe.wait_ge(shared_added, NSH * c + i - NSH + 1)
                elif right_half:
                    pe.wait_ge(scaled_right, NRT * (c - half) + i - 2 * NSH + 1)
                else:
                    pe.wait_ge(scaled_left, NRT * c + i - 2 * NSH + 1)
                for t in range(NT):
                    for k in range(HID):
                        last = mm(w_bank[i % 2][:, t * P:(t + 1) * P], hid[:, i % 2, k, t * P:(t + 1) * P],
                                  w2[:, (e * HID + k) * P:(e * HID + k + 1) * P], start=(k == 0), stop=(k == HID - 1))
                last.then_inc(w_full, 1)

            pe.wait_ge(w_loaded, 16 * NW)
            pe.wait_ge(blk_ready, 2)
            blk = pe_blk[:, :, :].rearrange("p h n -> p (h n)")
            mm(misc[0][:, 0:ND], wqT[:, :], blk).then_inc(side_full, 1)
            mm(misc[1][:, 0:ND], bqw[:, :], blk).then_inc(side_full, 1)
            pe.wait_ge(side_ready, 2)

            def first():
                for i in range(8):
                    prepare(0, i, False)
                    prepare(0, i, True)

            def left(c, b1, b2):
                up(c, 0)
                for i in range(NE):
                    b = b1 if i < 8 else b2
                    if b is not None:
                        prepare(b, i % 8, False)
                    if i + 1 < NE:
                        up(c, i + 1)
                    down(c, i, False)
                    if b is not None:
                        prepare(b, i % 8, True)

            def transpose_attention(g):
                pe.wait_ge(prod_free[1], POOL_MUL * (g + 1))
                pe.wait_ge(ao_ready, (NB - POOL_MUL) * (g + 1))
                for half in range(2):
                    pe.wait_ge(misc_free[half], PUSES * NB + AUSES * g)
                    transposes(half, lambda t: ao[:, half * NT + t, :])

            def project_attention(g, half):
                pe.wait_ge(misc_free[half], PUSES * NB + AUSES * g + 1)
                for t in range(NT):
                    last = mm(misc[half][:, t * P:(t + 1) * P], aoT[:, t * P:(t + 1) * P], wo[:, :])
                last.then_inc(misc_full[half], 1)

            def right(c, g):
                first = isinstance(g, int) and g == 0
                up(c, 0)
                for i in range(NE):
                    if i + 1 < NE:
                        up(c, i + 1)
                    if not first:
                        if i == 0:
                            transpose_attention(g - 1)
                        if i == 1:
                            project_attention(g - 1, 0)
                        if i == 2:
                            project_attention(g - 1, 1)
                    down(c, i, True)

            def last():
                transpose_attention(NT - 1)
                project_attention(NT - 1, 0)
                project_attention(NT - 1, 1)

            rounds(pe, first, left, right, last)


def build(nc, m):
    with ExitStack() as ctx:
        sb = lambda n, s, d=F32: ctx.enter_context(nc.sbuf_tensor(n, s, d))
        m["ident"] = sb("ident", [P, P])
        m["rms"] = sb("rms", [P, E1])
        m["w1"] = sb("w1", [P, E1 * 2 * P])
        m["w2"] = sb("w2", [P, E1 * 2 * P])
        m["x_all"] = sb("x_all", [P, NTILE * P])
        with ExitStack() as first:
            sb1 = lambda n, s, d=F32: first.enter_context(nc.sbuf_tensor(n, s, d))
            m["v_all"] = sb1("v_all", [P, NTILE * P])
            m["yT_all"] = sb1("yT_all", [P, NTILE * P])
            m["qs"] = sb1("qs", [P, 2, H, NTOK], BF16)
            m["ks"] = sb1("ks", [P, 2, H, NTOK], BF16)
            m["zero"] = sb1("zero", [2, NTOK], BF16)
            m["one"] = sb1("one", [2, NTOK], BF16)
            m["vw"] = sb1("vw", [P, 2, NT, H, VW])
            m["qk_parts"] = nc.dram_tensor("qk_parts", [NB, 2, H, PARTS, HD, NTOK], BF16, kind="Internal").ap()
            with ExitStack() as c:
                prepare_and_mix(nc, c, m)
            with ExitStack() as c:
                attend(nc, c, m)
        with ExitStack() as c:
            second_layer(nc, c, m)


def _laid_out(a):
    import numpy as np

    tile = lambda v: np.ascontiguousarray(v)
    ups = np.concatenate([a["L1_ffn_w1"], a["L1_ffn_w1_s"]])
    downs = np.concatenate([a["L1_ffn_w2"], a["L1_ffn_w2_s"]])
    row = np.arange(P)[:, None]
    weight = np.arange(2 * L)[None, :]
    return {
        "x": tile(a["L0_attn_x"].reshape(NB, NT, P, P).transpose(0, 2, 1, 3)),
        "ident": np.eye(P, dtype=np.float32),
        "selcol": ((row % (2 * L) == weight) & (row < PARTS * 2 * L)).astype(np.float32),
        "blockm": (row // HD == np.arange(H)[None, :]).astype(np.float32),
        "wqkv0": tile(a["L0_attn_w_qkv"]),
        "PwT": tile(a["L0_ffn_P_w"].T),
        "UT": tile(np.concatenate([a["L0_ffn_U1"], a["L0_ffn_U2"], a["L0_ffn_U3"]]).T),
        "W1T": tile(a["L0_ffn_W1"].transpose(2, 0, 1)),
        "W2T": tile(a["L0_ffn_W2"].transpose(2, 0, 1)),
        "b2": tile(a["L0_ffn_b2"]),
        "wproj": tile(a["L0_attn_w_proj"]),
        "bproj": tile(a["L0_attn_b_proj"].reshape(P, 1)),
        "wqT": tile(a["L1_attn_Wq"].T),
        "bqc": tile(a["L1_attn_bq"].reshape(P, 1)),
        "pe_rows": tile(np.tile(a["L1_attn_pos_emb"][0, :, :NB + 1], (H, 1))),
        "wqkv1": tile(np.concatenate([a["L1_attn_Wq"], a["L1_attn_Wk"], a["L1_attn_Wv"]], axis=1)),
        "bqkv": tile(np.concatenate([a["L1_attn_bq"], a["L1_attn_bk"], a["L1_attn_bv"]]).reshape(1, 3 * P)),
        "wo": tile(a["L1_attn_Wo"]),
        "bo": tile(a["L1_attn_bo"].reshape(1, P)),
        "router": tile(a["L1_ffn_router_w"]),
        "rms": tile(np.concatenate([a["L1_ffn_rms_w"], a["L1_ffn_rms_w_s"]]).T),
        "w1": tile(ups.transpose(1, 0, 2).reshape(P, -1)),
        "w2": tile(downs.reshape(E1, 2, P, P).transpose(2, 0, 1, 3).reshape(P, -1)),
    }


def kernel(**inputs):
    import numpy as np
    import concourse.bacc as bacc
    from concourse.bass_utils import run_bass_kernel_spmd

    laid = _laid_out({k: np.asarray(v) for k, v in inputs.items()})
    nc = bacc.Bacc("TRN2", target_bir_lowering=False, num_devices=1)
    m = {}
    for name, a in laid.items():
        ap = nc.dram_tensor(f"in_{name}", a.shape, mybir.dt.from_np(a.dtype), kind="ExternalInput").ap()
        m["x" if name == "x" else name + "_d"] = ap
    m["out"] = nc.dram_tensor("out", [NB, P, NT, P], F32, kind="ExternalOutput").ap()
    build(nc, m)
    r = run_bass_kernel_spmd(nc, [{f"in_{k}": a for k, a in laid.items()}], core_ids=[0])
    return np.asarray(r.results[0]["out"]).transpose(0, 2, 1, 3).reshape(NB, NTOK, P)
```

```python
import concourse.bass as bass
from concourse import mybir
from contextlib import ExitStack

F32 = mybir.dt.float32
F32R = mybir.dt.float32r
BF16 = mybir.dt.bfloat16
ALU = mybir.AluOpType
ACT = mybir.ActivationFunctionType
AX = mybir.AxisListType

P = 128
NB = 8
NTOK = 512
NT = NTOK // P
NTILE = NB * NT
H = 16
HD = P // H
L = 12
NR = 3
DA = 64
VW = 32
PARTS = 3
E1 = 16
LN_EPS = 1e-5
RMS_EPS = 1.1920929e-07
SCALE = float(HD) ** -0.5
LARGE = 3.0e38


def wait_apart(eng, sem, value, passed):
    eng.wait_ge(sem, value)
    eng.sem_inc(passed, 1)


OCT = 8
LOADS = PARTS * PARTS + PARTS + 1
EARLY = 20
ROWS = PARTS * PARTS * HD


class Chain:

    def __init__(self, eng, sem, per):
        self.eng, self.sem, self.per = eng, sem, per

    def round(self, b):
        self.base, self.k = b * self.per, 0

    def mark(self, ins):
        self.k += 1
        assert self.k <= self.per
        ins.then_inc(self.sem, 1)
        return self.base + self.k

    def wait(self, value):
        self.eng.wait_ge(self.sem, value)

    def link_apart(self, ins, passed):
        wait_apart(self.eng, self.sem, self.mark(ins), passed)

    def link(self, ins):
        self.wait(self.mark(ins))

    def end(self):
        assert self.k == self.per, (self.k, self.per)


def gather_stacks(sp, m, b, par, o):
    qs, ks, qk_parts, s = m["qs"], m["ks"], m["qk_parts"], m["stack_loaded"][par][o]
    heads = slice(o * OCT, (o + 1) * OCT)
    for a in range(PARTS):
        lo = a * PARTS * HD
        sp.dma_start(ks[lo:lo + PARTS * HD, par, heads, :],
                     qk_parts[b, 1, heads].rearrange("h c d n -> (c d) h n") if isinstance(b, int) else
                     qk_parts[bass.ds(b, 1), 1, heads].rearrange("a h c d n -> (a c d) h n")).then_inc(s, 16)
        for c in range(PARTS):
            at = lo + c * HD
            sp.dma_start(qs[at:at + HD, par, heads, :],
                         qk_parts[b, 0, heads, a].rearrange("h d n -> d h n") if isinstance(b, int) else
                         qk_parts[bass.ds(b, 1), 0, heads, a].rearrange("a h d n -> (a d) h n")).then_inc(s, 16)
    sp.dma_start(qs[ROWS:ROWS + 2, par, heads, :], m["zero"][:, None, :].broadcast_to([2, OCT, NTOK])).then_inc(s, 16)


def prepare_and_mix(nc, ctx, m):
    sb = lambda n, s, d=F32: ctx.enter_context(nc.sbuf_tensor(n, s, d))
    sem = lambda n: ctx.enter_context(nc.semaphore(n))
    x_all, v_all, yT_all, ident = m["x_all"], m["v_all"], m["yT_all"], m["ident"]
    RING = 4
    AHEAD = RING - 1
    qk_parts = m["qk_parts"]

    wqkv = sb("wqkv0", [P, 3 * P])
    PwT = sb("PwT", [P, DA])
    UT = sb("UT", [DA, NR * L])
    W1T = m["w2"][:, 0:L * P].rearrange("p (e d) -> p e d", e=L)
    W2T = m["w2"][:, L * P:2 * L * P].rearrange("p (e d) -> p e d", e=L)
    b2 = sb("b2", [L, P])
    selcol = sb("selcol", [P, 2 * L])
    sel = sb("sel", [P, 2 * L, P], BF16)
    identb = sb("identb", [P, P], BF16)

    stats = sb("stats", [P, NT, 6])
    mv = sb("mv", [P, NT, 2])
    ve = sb("ve", [P, NT])
    sd = sb("sd", [P, NT])
    r0 = sb("r0", [P, NT])
    nt_ = sb("nt_", [P, NT])
    rstd = sb("rstd", [P, NT])
    xn = sb("xn", [P, NT, P])
    xnT = sb("xnT", [P, 2, NTOK])
    split = sb("split", [P, 2, PARTS, NTOK], BF16)
    resid = sb("resid", [P, 2, NTOK])
    xa = sb("xa", [DA, NTOK])
    Z = sb("Z", [P, NT * NR, L])
    Zr = sb("Zr", [P, NT * NR, L])
    mx = sb("mx", [P, NT * NR, 8])
    Zd = sb("Zd", [P, NT * NR, L])
    Ex = sb("Ex", [P, NT * NR, L])
    Mk = sb("Mk", [P, NT * NR, L])
    Sm = sb("Sm", [P, NT * NR])
    C = sb("C", [P, NT * NR, L])
    Cs = sb("Cs", [P, NT, PARTS, 2, L], BF16)
    Cr = sb("Cr", [P, NT, 2, L])
    CsT = sb("CsT", [P, 2, NTOK], BF16)
    C3T = sb("C3T", [L, 2, NTOK])
    hT = m["w2"][:, 2 * L * P:2 * L * P + NTOK]
    xs_low = sb("xs", [P, RING - 1, NTOK])
    xs = [xs_low[:, k, :] for k in range(RING - 1)] + [m["w2"][:, 2 * L * P + NTOK:2 * L * P + 2 * NTOK]]

    banks = ctx.enter_context(nc.psum_tensor("banks0", [P, 8, NTOK], F32))
    prep_bank = [banks[:, 0, :], banks[:, 1, :]]
    bc_bank = [banks[:, 2 + i, :] for i in range(RING)]
    h_bank, y_bank = banks[:, 6, :], banks[:, 7, :]

    x_loaded, ident_loaded, passed = sem("x_loaded"), sem("ident_loaded"), sem("passed0")
    proj_loaded, w_loaded = sem("proj_loaded"), sem("w_loaded")
    consts_ready, vw_clear, w1_loaded = sem("consts_ready"), sem("vw_clear"), sem("w1_loaded")
    stacks_clear, ones_put = sem("stacks_clear"), sem("ones_put")
    stats_ready, sd_ready, xn_ready, dve_prep = sem("stats_ready"), sem("sd_ready"), sem("xn_ready"), sem("dve_prep")
    bank_full, bank_free = [sem("bank_full0"), sem("bank_full1")], [sem("bank_free0"), sem("bank_free1")]
    xnT_ready, high_ready, resid_ready, parts_ready, parts_stored = (sem("xnT_ready"), sem("high_ready"), sem("resid_ready"),
                                                      sem("parts_ready"), sem("parts_stored"))
    xa_ready, zd_ready, ex_ready, cs_ready, cT_ready = (sem("xa_ready"), sem("zd_ready"), sem("ex_ready"),
                                                        sem("cs_ready"), sem("cT_ready"))
    bc_ready, xs_ready, xs_used = sem("bc_ready"), sem("xs_ready"), sem("xs_used")
    gelu_done, y_done = sem("gelu_done"), sem("y_done")
    USES = 4
    NPROJ, NEXP = 4, 3
    STORES = 16 * 2 * PARTS

    def tok(t, b, at=0, n=NTOK):
        return t[:, bass.ds(b * NTOK + at, n)]

    def rounds(eng, first, both):
        first()
        both(1, 1, 0, 0)
        with eng.Fori(1, NB // 2) as i:
            both(2 * i, 0, 2 * i - 1, 1)
            both(2 * i + 1, 1, 2 * i, 0)
        both(None, None, NB - 1, 1)

    with nc.Block() as block:
        @block.sync
        def _(sp):
            sp.dma_start(tok(x_all, 0).rearrange("p (t d) -> p t d", t=NT), m["x"][0]).then_inc(x_loaded, 16)
            sp.dma_start(ident[:, :], m["ident_d"]).then_inc(ident_loaded, 16)
            sp.dma_start(PwT[:, :], m["PwT_d"]).then_inc(proj_loaded, 16)
            sp.dma_start(UT[:, :], m["UT_d"]).then_inc(proj_loaded, 16)
            sp.dma_start(wqkv[:, :], m["wqkv0_d"]).then_inc(proj_loaded, 16)
            sp.dma_start(selcol[:, :], m["selcol_d"]).then_inc(proj_loaded, 16)
            sp.dma_start(W1T[:, :, :], m["W1T_d"]).then_inc(w_loaded, 16)
            sp.dma_start(W2T[:, :, :], m["W2T_d"]).then_inc(w_loaded, 16)
            sp.dma_start(b2[:, :], m["b2_d"]).then_inc(w_loaded, 16)
            sp.dma_start(m["rms"][:, :], m["rms_d"]).then_inc(w1_loaded, 16)
            sp.dma_start(m["w1"][:, :], m["w1_d"]).then_inc(w1_loaded, 16)
            with sp.Fori(1, NB) as b:
                sp.wait_ge(x_loaded, 16 * b)
                sp.dma_start(tok(x_all, b).rearrange("p (t d) -> p t d", t=NT),
                             m["x"][bass.ds(b, 1)].rearrange("a p t d -> p (a t) d")).then_inc(x_loaded, 16)
                for w in range(2):
                    sp.wait_ge(parts_ready, 2 * b - 1 + w)
                    for c in range(PARTS):
                        sp.dma_start(qk_parts[bass.ds(b - 1, 1), w, :, c].rearrange("a h d n -> (a h) d n"), split[:, w, c, :])\
                            .then_inc(parts_stored, 16)
            sp.wait_ge(stacks_clear, 1)
            for par in range(2):
                sp.dma_start(m["ks"][ROWS:ROWS + 2, par, :, :], m["one"][:, None, :].broadcast_to([2, H, NTOK])).then_inc(ones_put, 16)
            sp.wait_ge(parts_stored, STORES)
            for o in range(2):
                gather_stacks(sp, m, 0, 0, o)
            for w in range(2):
                sp.wait_ge(parts_ready, 2 * NB - 1 + w)
                for c in range(PARTS):
                    sp.dma_start(qk_parts[NB - 1, w, :, c], split[:, w, c, :]).then_inc(parts_stored, 16)
            sp.wait_ge(parts_stored, STORES * NB)
            sp.wait_ge(ones_put, 32)

        @block.gpsimd
        def _(pool):
            pool.memset(CsT[:, :, :], 0.0).then_inc(consts_ready, 1)
            pool.memset(m["qs"][:, :, :, :].bitcast(F32), 0.0)
            pool.memset(m["ks"][:, :, :, :].bitcast(F32), 0.0)
            pool.memset(m["zero"][:, :], 0.0)
            pool.memset(m["one"][:, :], 1.0).then_inc(stacks_clear, 1)
            pool.memset(m["vw"][:, :, :, :, :], 0.0).then_inc(vw_clear, 1)
            pool.wait_ge(vw_clear, 1)
            pool.memset(m["vw"][:, :, :, :, HD:HD + 1], 1.0)
            pool.wait_ge(w1_loaded, 32)
            for e in range(E1):
                w = m["w1"][:, e * 2 * P:(e + 1) * 2 * P]
                pool.tensor_scalar(w, w, m["rms"][:, e:e + 1], None, ALU.mult)

        @block.vector
        def _(v):
            own = Chain(v, dve_prep, 13 + 2 + 26 + 7)

            def moments(b):
                own.round(b)
                v.wait_ge(x_loaded, 16 * (b + 1))
                for t in range(NT):
                    done = own.mark(v.bn_stats(stats[:, t, :], tok(x_all, b, t * P, P)))
                wait_apart(v, dve_prep, done, passed)
                for t in range(NT):
                    done = own.mark(v.bn_aggr(mv[:, t, :], stats[:, t, :]))
                own.wait(done)
                v.tensor_scalar(ve[:, :], mv[:, :, 1], LN_EPS, None, ALU.add).then_inc(stats_ready, 1)

            def inverse_deviation(b):
                v.wait_ge(sd_ready, b + 1)
                own.link(v.reciprocal(r0[:, :], sd[:, :]))
                own.link(v.tensor_tensor(nt_[:, :], r0[:, :], r0[:, :], ALU.mult))
                own.link(v.tensor_tensor(nt_[:, :], nt_[:, :], ve[:, :], ALU.mult))
                own.link(v.tensor_scalar(nt_[:, :], nt_[:, :], -0.5, 1.5, ALU.mult, ALU.add))
                own.link(v.tensor_tensor(rstd[:, :], r0[:, :], nt_[:, :], ALU.mult))

            def norm(b):
                if not isinstance(b, int) or b > 0:
                    v.wait_ge(bank_full[0], USES * (b - 1) + 1)
                for t in range(NT):
                    ins = v.tensor_scalar(xn[:, t, :], tok(x_all, b, t * P, P), mv[:, t, 0:1], rstd[:, t:t + 1],
                                          ALU.subtract, ALU.mult)
                ins.then_inc(xn_ready, 1)

            def residual(b, w):
                v.wait_ge(high_ready, 2 * b + w + 1)
                v.tensor_tensor(resid[:, w, :], prep_bank[1 - w], split[:, w, 0, :], ALU.subtract).then_inc(bank_free[1 - w], 1)

            def low_parts(b, w):
                v.wait_ge(bank_free[1 - w], USES * b + (2 if w == 0 else 3))
                own.link(v.tensor_copy(split[:, w, 1, :], resid[:, w, :]))
                v.tensor_tensor(split[:, w, 2, :], resid[:, w, :], split[:, w, 1, :], ALU.subtract).then_inc(parts_ready, 1)

            def keep_scores(b):
                v.wait_ge(bank_full[0], USES * b + 2)
                v.tensor_copy(Z[:, :, :].rearrange("p a e -> p (a e)"), prep_bank[0][:, 0:NT * NR * L]).then_inc(bank_free[0], 1)
                wait_apart(v, bank_free[0], USES * b + 2, passed)
                for i in range(NT * NR):
                    done = own.mark(v.max(mx[:, i, :], Z[:, i, :]))
                own.wait(done)
                v.tensor_tensor(Zd[:, :, :], Z[:, :, :], mx[:, :, 0:1].broadcast_to([P, NT * NR, L]), ALU.subtract).then_inc(zd_ready, 1)

            def choose(b):
                own.link_apart(v.memset(mx[:, :, 3:8], LARGE), passed)
                for i in range(NT * NR):
                    done = own.mark(v.match_replace(Zr[:, i, :], mx[:, i, :], Z[:, i, :], -LARGE))
                own.wait(done)
                own.link(v.tensor_tensor(Mk[:, :, :], Zr[:, :, :], Z[:, :, :], ALU.not_equal))

            def weigh(b):
                v.wait_ge(ex_ready, b + 1)
                own.link(v.tensor_tensor(Mk[:, :, :], Mk[:, :, :], Ex[:, :, :], ALU.mult))
                own.link(v.tensor_reduce(Sm[:, :], Mk[:, :, :], AX.X, ALU.add))
                own.link(v.reciprocal(Sm[:, :], Sm[:, :]))
                own.link(v.tensor_tensor(C[:, :, :], Mk[:, :, :], Sm[:, :, None].broadcast_to([P, NT * NR, L]), ALU.mult))

            def split_weights(b):
                C12 = C[:, :, :].rearrange("p (t r) e -> p t r e", r=NR)[:, :, 0:2, :]
                own.link(v.tensor_copy(Cs[:, :, 0, :, :], C12))
                own.link(v.tensor_tensor(Cr[:, :, :, :], C12, Cs[:, :, 0, :, :], ALU.subtract))
                own.link(v.tensor_copy(Cs[:, :, 1, :, :], Cr[:, :, :, :]))
                v.tensor_tensor(Cs[:, :, 2, :, :], Cr[:, :, :, :], Cs[:, :, 1, :, :], ALU.subtract).then_inc(cs_ready, 1)

            def scale_inputs(b, par, e):
                n = 2 * L * b + e
                src = xnT[:, par, :] if e < L else hT[:, :]
                if e == L:
                    v.wait_ge(gelu_done, b + 1)
                v.wait_ge(bc_ready, n + 1)
                if not isinstance(b, int) or b > 0 or e >= RING:
                    v.wait_ge(xs_used, n - RING + 1)
                v.tensor_tensor(xs[e % RING], bc_bank[e % RING], src, ALU.mult).then_inc(xs_ready, 1)

            def first():
                moments(0)
                inverse_deviation(0)
                norm(0)
                v.wait_ge(ident_loaded, 16)
                v.tensor_copy(identb[:, :], ident[:, :]).then_inc(consts_ready, 1)
                v.wait_ge(proj_loaded, 16 * NPROJ)
                v.tensor_copy(sel[:, :, :], selcol[:, :, None].broadcast_to([P, 2 * L, P])).then_inc(consts_ready, 1)
                keep_scores(0)
                choose(0)
                weigh(0)
                split_weights(0)
                residual(0, 0)
                residual(0, 1)
                low_parts(0, 0)
                low_parts(0, 1)
                own.end()

            def both(b, par, a, apar):
                for e in range(2 * L):
                    if b is not None:
                        if e == 1:
                            moments(b)
                        if e == 5:
                            inverse_deviation(b)
                            norm(b)
                        if e == 11:
                            keep_scores(b)
                        if e == L:
                            choose(b)
                            weigh(b)
                            split_weights(b)
                        if e == L + 4:
                            residual(b, 0)
                        if e == L + 5:
                            residual(b, 1)
                        if e == L + 7:
                            low_parts(b, 0)
                        if e == L + 9:
                            low_parts(b, 1)
                            own.end()
                    if b is None and RING <= e < RING + EARLY:
                        first_maximum(e - RING)
                    scale_inputs(a, apar, e)

            def first_maximum(u):
                v.wait_ge(m["s_full"], u + 1)
                v.tensor_reduce(m["mx"][:, 0, u:u + 1], prep_bank[u % 2], AX.X, ALU.max).then_inc(m["s_free"], 1)

            rounds(v, first, both)

        @block.scalar
        def _(act):
            def deviation(b):
                act.wait_ge(stats_ready, b + 1)
                act.activation(sd[:, :], ve[:, :], ACT.Sqrt).then_inc(sd_ready, 1)

            def evacuate_norm(b, par):
                act.wait_ge(bank_full[0], USES * b + 1)
                if not isinstance(b, int) or b > 1:
                    act.wait_ge(xs_ready, 2 * L * (b - 1))
                act.activation(xnT[:, par, :], prep_bank[0], ACT.Copy).then_inc(bank_free[0], 1)

            def high_parts(b):
                for w in range(2):
                    act.wait_ge(bank_full[1 - w], USES * b + (2 if w == 0 else 3))
                    if not isinstance(b, int) or b > 0:
                        act.wait_ge(parts_stored, STORES * b)
                    act.activation(split[:, w, 0, :], prep_bank[1 - w], ACT.Copy).then_inc(high_ready, 1)

            def address(b):
                act.wait_ge(bank_full[1], USES * b + 1)
                act.activation(xa[:, :], prep_bank[1][0:DA, :], ACT.Copy).then_inc(bank_free[1], 1)

            def values(b):
                act.wait_ge(bank_full[1], USES * b + 4)
                act.activation(tok(v_all, b), prep_bank[1], ACT.Copy).then_inc(bank_free[1], 1)

            def exponentials(b):
                act.wait_ge(zd_ready, b + 1)
                act.activation(Ex[:, :, :], Zd[:, :, :], ACT.Exp).then_inc(ex_ready, 1)

            def weights_transposed(b, par):
                act.wait_ge(bank_full[1], USES * b + 3)
                act.activation(C3T[:, par, :], prep_bank[1][0:L, :], ACT.Copy).then_inc(bank_free[1], 1)
                act.wait_ge(bank_full[0], USES * b + 4)
                act.activation(CsT[0:PARTS * 2 * L, par, :], prep_bank[0].bitcast(BF16)[0:PARTS * 2 * L, 0:NTOK], ACT.Copy)\
                    .then_inc(bank_free[0], 1)

            def gelu(b):
                act.wait_ge(xs_used, 2 * L * b + L)
                act.activation(hT[:, :], h_bank, ACT.Gelu).then_inc(gelu_done, 1)

            def keep_mixture(b):
                act.wait_ge(xs_used, 2 * L * (b + 1))
                act.activation(tok(yT_all, b), y_bank, ACT.Copy).then_inc(y_done, 1)

            def first():
                deviation(0)
                evacuate_norm(0, 0)
                address(0)
                exponentials(0)
                high_parts(0)
                act.wait_ge(consts_ready, 3)
                weights_transposed(0, 0)
                values(0)

            def both(b, par, a, apar):
                if b is not None:
                    deviation(b)
                    evacuate_norm(b, par)
                    address(b)
                    exponentials(b)
                gelu(a)
                if b is not None:
                    high_parts(b)
                    weights_transposed(b, par)
                    values(b)
                keep_mixture(a)

            rounds(act, first, both)

        @block.tensor
        def _(pe):
            def claim(b, k):
                if not isinstance(b, int) or b > 0 or k >= 2:
                    pe.wait_ge(bank_free[k % 2], USES * b + k // 2)
                return prep_bank[k % 2]

            def mm(out, lhsT, rhs, start=True, stop=True):
                return nc.tensor.matmul(out, lhsT, rhs, start=start, stop=stop)

            def transpose_norm(b):
                pe.wait_ge(xn_ready, b + 1)
                o = claim(b, 0)
                for t in range(NT):
                    last = nc.tensor.transpose(o[:, t * P:(t + 1) * P], xn[:, t, :], ident[:, :])
                last.then_inc(bank_full[0], 1)

            def address(b, par):
                pe.wait_ge(bank_free[0], USES * b + 1)
                mm(claim(b, 1)[0:DA, :], PwT[:, :], xnT[:, par, :]).then_inc(bank_full[1], 1)

            def scores(b):
                pe.wait_ge(bank_free[1], USES * b + 1)
                o = claim(b, 2)
                for t in range(NT):
                    last = mm(o[:, t * NR * L:(t + 1) * NR * L], xa[:, t * P:(t + 1) * P], UT[:, :])
                last.then_inc(bank_full[0], 1)

            def queries_keys(b, par):
                mm(claim(b, 3), wqkv[:, 0:P], xnT[:, par, :]).then_inc(bank_full[1], 1)
                mm(claim(b, 4), wqkv[:, P:2 * P], xnT[:, par, :]).then_inc(bank_full[0], 1)

            def transpose_weights(b):
                pe.wait_ge(cs_ready, b + 1)
                o = claim(b, 5)
                for t in range(NT):
                    last = nc.tensor.transpose(o[0:L, t * P:(t + 1) * P], C[:, t * NR + 2, :], ident[:, :])
                last.then_inc(bank_full[1], 1)
                o = claim(b, 6).bitcast(BF16)
                for t in range(NT):
                    last = nc.tensor.transpose(o[0:PARTS * 2 * L, t * P:(t + 1) * P], Cs[:, t, :, :, :].rearrange("p c r e -> p (c r e)"), identb[:, :])
                last.then_inc(bank_full[0], 1)

            def values(b, par):
                o = claim(b, 7)
                for t in range(NT):
                    last = mm(o[:, t * P:(t + 1) * P], xnT[:, par, t * P:(t + 1) * P], wqkv[:, 2 * P:3 * P])
                last.then_inc(bank_full[1], 1)

            def broadcast_weight(b, par, e):
                n = 2 * L * b + e
                if not isinstance(b, int) or b > 0 or e >= RING:
                    pe.wait_ge(xs_ready, n - RING + 1)
                if e == 0:
                    pe.wait_ge(bank_free[0], USES * (b + 1))
                mm(bc_bank[e % RING], sel[:, e, :], CsT[:, par, :]).then_inc(bc_ready, 1)

            def accumulate(b, par, e):
                n = 2 * L * b + e
                if e == 0 and (not isinstance(b, int) or b > 0):
                    pe.wait_ge(gelu_done, b)
                if e == L:
                    if not isinstance(b, int) or b > 0:
                        pe.wait_ge(y_done, b)
                    pe.wait_ge(bank_free[1], USES * b + 3)
                    mm(y_bank, b2[:, :], C3T[:, par, :], stop=False)
                pe.wait_ge(xs_ready, n + 1)
                w = (W1T if e < L else W2T)[:, e % L, :]
                mm(h_bank if e < L else y_bank, w, xs[e % RING], start=(e == 0), stop=(e % L == L - 1))\
                    .then_inc(xs_used, 1)

            def first():
                pe.wait_ge(ident_loaded, 16)
                transpose_norm(0)
                pe.wait_ge(proj_loaded, 16 * NPROJ)
                address(0, 0)
                scores(0)
                queries_keys(0, 0)
                pe.wait_ge(consts_ready, 3)
                transpose_weights(0)
                values(0, 0)
                for e in range(AHEAD):
                    broadcast_weight(0, 0, e)
                pe.wait_ge(w_loaded, 16 * NEXP)

            def both(b, par, a, apar):
                for e in range(2 * L):
                    if e + AHEAD < 2 * L:
                        broadcast_weight(a, apar, e + AHEAD)
                    elif b is not None:
                        broadcast_weight(b, par, e + AHEAD - 2 * L)
                    accumulate(a, apar, e)
                    if b is None and e < EARLY:
                        first_scores(e)
                    if b is not None:
                        if e == 3:
                            transpose_norm(b)
                        if e == 5:
                            address(b, par)
                        if e == 7:
                            scores(b)
                        if e == L - 1:
                            queries_keys(b, par)
                        if e == L + 4:
                            transpose_weights(b)
                        if e == L + 6:
                            values(b, par)

            def first_scores(u):
                if u == 0:
                    pe.wait_ge(m["stack_loaded"][0][0], 16 * LOADS)
                    pe.wait_ge(ones_put, 32)
                if u < 2:
                    pe.wait_ge(bank_free[u], USES * NB)
                else:
                    pe.wait_ge(m["s_free"], u - 1)
                h, t = u // NT, u % NT
                mm(prep_bank[u % 2], m["qs"][:, 0, h, t * P:(t + 1) * P], m["ks"][:, 0, h, :]).then_inc(m["s_full"], 1)

            rounds(pe, first, both)


def attend(nc, ctx, m):
    sb = lambda n, s, d=F32: ctx.enter_context(nc.sbuf_tensor(n, s, d))
    sem = lambda n: ctx.enter_context(nc.semaphore(n))
    x_all, v_all, yT_all, ident = m["x_all"], m["v_all"], m["yT_all"], m["ident"]
    qk_parts = m["qk_parts"]
    QUAD = 4
    UNITS = OCT * NT
    STEPS = UNITS // QUAD
    LEAD = 3

    qs, ks, vw, zero, one = m["qs"], m["ks"], m["vw"], m["zero"], m["one"]
    wproj = sb("wproj", [P, P])
    bproj = sb("bproj", [P, 1])
    identb = sb("identb1", [P, P], BF16)
    probs = sb("probs", [P, 2, QUAD, NTOK])
    mx = m["mx"]
    mhl = sb("mhl", [P, 2, 4, OCT * NT], BF16)
    mT = sb("mT", [2 * OCT * NT, 2, P], BF16)
    oT = sb("oT", [P, 2, NTOK])
    rden = sb("rden", [P, NT, QUAD])
    att = sb("att", [P, NT, P])
    attT = sb("attT", [P, NTOK])
    x1T = sb("x1T", [P, NTOK])

    banks = ctx.enter_context(nc.psum_tensor("banks1", [P, 8, NTOK], F32))
    RING = 3
    e_bank = [banks[:, i, :] for i in range(RING)]
    s_bank = [banks[:, RING + i, :] for i in range(RING)]
    o_bank, misc = banks[:, 6, :], banks[:, 7, :]

    w_loaded, w2_loaded, filled = sem("w_loaded1"), sem("w2_loaded"), sem("filled1")
    stack_loaded = m["stack_loaded"]
    m_loaded = [sem("m_loaded0"), sem("m_loaded1")]
    v_ready = sem("v_ready")
    s_full, s_free = m["s_full"], m["s_free"]
    e_full, exp_done, av_done = sem("e_full"), sem("exp_done"), sem("av_done")
    m_hi, m_split, mt_full, mt_free = sem("m_hi"), sem("m_split"), sem("mt_full"), sem("mt_free")
    o_kept, ot_full, rden_ready, ot_free = sem("o_kept"), sem("ot_full"), sem("rden_ready"), sem("ot_free")
    at_full, at_free, pj_full, pj_free, xt_full, xt_free = (sem("at_full"), sem("at_free"), sem("pj_full"),
                                                            sem("pj_free"), sem("xt_full"), sem("xt_free"))

    def tok(t, b, at=0, n=NTOK):
        return t[:, bass.ds(b * NTOK + at, n)]

    def ge(eng, s, value):
        if not isinstance(value, int) or value > 0:
            eng.wait_ge(s, value)

    def slot(par, o, u):
        return ((2 * par + o) * UNITS + u) % RING

    def readers(par, o, b, u):
        at = (2 * par + o) * UNITS + u
        back = RING if at >= RING else at + 4 * UNITS - max(i for i in range(4 * UNITS) if i % RING == at % RING)
        return (2 * b + o) * UNITS + (u - back + 1)

    def rounds(eng, first, octet, last):
        first()
        def pair(b, end):
            for r in range(4):
                octet(b + r // 2, r // 2, r % 2, not end or r < 3, not end or r < 2)
        pair(0, False)
        with eng.Fori(1, NB // 2 - 1) as i:
            pair(2 * i, False)
        pair(NB - 2, True)
        last()

    with nc.Block() as block:
        @block.sync
        def _(sp):
            def put_maxima(b, par, o):
                n = 2 * b + o
                sp.wait_ge(mt_free, n + 1)
                sp.dma_start(qs[ROWS:ROWS + 2, par, o * OCT:(o + 1) * OCT, :], mT[:, o, :]).then_inc(m_loaded[o], 16)

            sp.dma_start(wproj[:, :], m["wproj_d"]).then_inc(w_loaded, 16)
            sp.dma_start(bproj[:, :], m["bproj_d"]).then_inc(w_loaded, 16)

            def first():
                sp.dma_start(m["w2"][:, :], m["w2_d"]).then_inc(w2_loaded, 16)
                put_maxima(0, 0, 0)

            def octet(b, pb, o, more1, more2):
                if more2:
                    ge(sp, e_full, 2 * UNITS * b)
                    gather_stacks(sp, m, b + 1, 1 - pb, o)
                if more1:
                    put_maxima(b + o, (pb + o) % 2, 1 - o)

            rounds(sp, first, octet, lambda: None)
            sp.wait_ge(w2_loaded, 16)
            for o in range(2):
                sp.wait_ge(m_loaded[o], 16 * NB)

        @block.gpsimd
        def _(pool):
            def spread(b, par):
                pool.tensor_copy(vw[:, par, :, :, 0:HD], tok(v_all, b).rearrange("p (t h d) -> p t h d", t=NT, h=H))\
                    .then_inc(v_ready, 1)

            def octet(b, pb, o, more1, more2):
                if o == 0 and more2:
                    ge(pool, av_done, 2 * STEPS * b)
                    spread(b + 1, 1 - pb)

            rounds(pool, lambda: spread(0, 0), octet, lambda: None)

        @block.vector
        def _(v):
            v.memset(mhl[:, :, 2:4, :], 0.0)
            v.tensor_copy(identb[:, :], ident[:, :]).then_inc(filled, 1)

            def maxima(b, par, o, s, js=range(QUAD)):
                for j in js:
                    u = s * QUAD + j
                    n = (2 * b + o) * UNITS + u
                    v.wait_ge(s_full, n + 1)
                    if u == 0:
                        ge(v, m_split, 2 * b + o - 1)
                    v.tensor_reduce(mx[:, o, u:u + 1], s_bank[slot(par, o, u)], AX.X, ALU.max).then_inc(s_free, 1)

            def split_maxima(b, o):
                n = 2 * b + o
                v.wait_ge(s_free, UNITS * (n + 1))
                ge(v, mt_full, n - 1)
                v.tensor_scalar(mhl[:, o, 0, :], mx[:, o, :], -1.0, None, ALU.mult).then_inc(m_hi, 1)
                v.wait_ge(m_hi, n + 1)
                v.scalar_tensor_tensor(mhl[:, o, 1, :], mx[:, o, :], -1.0, mhl[:, o, 0, :], ALU.mult, ALU.subtract)\
                    .then_inc(m_split, 1)

            def normalize(b, quad):
                g = QUAD * b + quad
                v.wait_ge(ot_full, g + 1)
                o = misc.rearrange("p (t j c) -> p t j c", t=NT, j=QUAD)
                v.reciprocal(rden[:, :, :], o[:, :, :, HD]).then_inc(rden_ready, 1)
                v.wait_ge(rden_ready, g + 1)
                if quad == 0:
                    ge(v, at_full, b)
                v.tensor_tensor(att[:, :, quad * QUAD * HD:(quad + 1) * QUAD * HD].rearrange("p t (j d) -> p t j d", d=HD),
                                o[:, :, :, 0:HD], rden[:, :, :, None].broadcast_to([P, NT, QUAD, HD]), ALU.mult)\
                    .then_inc(ot_free, 1)

            def add_mixture(b):
                v.wait_ge(w_loaded, 32)
                v.wait_ge(pj_full, b + 1)
                ge(v, xt_full, b)
                v.scalar_tensor_tensor(x1T[:, :], misc, bproj[:, 0:1], tok(yT_all, b), ALU.add, ALU.add).then_inc(pj_free, 1)

            def add_input(b):
                v.wait_ge(xt_full, b + 1)
                v.tensor_tensor(tok(x_all, b), misc, tok(x_all, b), ALU.add).then_inc(xt_free, 1)

            def first():
                for s in range(EARLY // QUAD, STEPS):
                    maxima(0, 0, 0, s)
                split_maxima(0, 0)
                for s in range(LEAD):
                    maxima(0, 0, 1, s)

            def octet(b, pb, o, more1, more2):
                begin = isinstance(b, int) and b == 0 and o == 0
                for s in range(STEPS):
                    for js in ((0, 1), (2, 3)):
                        if s < STEPS - LEAD:
                            if more1:
                                maxima(b + o, (pb + o) % 2, 1 - o, s + LEAD, js)
                        elif more2:
                            maxima(b + 1, 1 - pb, o, s + LEAD - STEPS, js)
                        if js[0] == 0:
                            if s == 2 and not begin:
                                normalize(b - 1 + o, 3 if o == 0 else 1)
                            if o == 0 and not begin:
                                if s == 4:
                                    add_mixture(b - 1)
                                if s == 5:
                                    add_input(b - 1)
                            if s == 7:
                                normalize(b, 2 * o)
                    if s == STEPS - LEAD - 1 and more1:
                        split_maxima(b + o, 1 - o)

            def last():
                normalize(NB - 1, 3)
                add_mixture(NB - 1)
                add_input(NB - 1)

            rounds(v, first, octet, last)

        @block.scalar
        def _(act):
            def exponentiate(b, par, o, s, js):
                g = (2 * b + o) * STEPS + s
                for j in js:
                    act.wait_ge(e_full, g * QUAD + j + 1)
                    if j == 0:
                        ge(act, av_done, g - 1)
                    act.activation(probs[:, s % 2, j, :], e_bank[slot(par, o, s * QUAD + j)], ACT.Exp, scale=SCALE).then_inc(exp_done, 1)

            def keep_products(b, quad):
                g = QUAD * b + quad
                act.wait_ge(av_done, NT * (g + 1))
                ge(act, ot_full, g - 1)
                act.activation(oT[:, quad % 2, :], o_bank, ACT.Copy).then_inc(o_kept, 1)

            def keep_maxima(b, o):
                n = 2 * b + o
                act.wait_ge(mt_full, n + 1)
                ge(act, m_loaded[o], 16 * b)
                act.activation(mT[:, o, :], misc.bitcast(BF16)[0:2 * OCT * NT, 0:P], ACT.Copy).then_inc(mt_free, 1)

            def keep_attention(b):
                act.wait_ge(at_full, b + 1)
                act.activation(attT[:, :], misc, ACT.Copy).then_inc(at_free, 1)

            def octet(b, pb, o, more1, more2):
                begin = isinstance(b, int) and b == 0 and o == 0
                for s in range(STEPS):
                    exponentiate(b, pb, o, s, (0, 1))
                    if s == 3 and o == 0 and not begin:
                        keep_attention(b - 1)
                    if s == 6 and more1:
                        keep_maxima(b + o, 1 - o)
                    exponentiate(b, pb, o, s, (2, 3))
                    if s == 0 and not begin:
                        keep_products(b - 1 + o, 3 if o == 0 else 1)
                    if s == 4:
                        keep_products(b, 2 * o)

            def last():
                keep_products(NB - 1, 3)
                keep_attention(NB - 1)

            rounds(act, lambda: keep_maxima(0, 0), octet, last)

        @block.tensor
        def _(pe):
            def mm(out, lhsT, rhs, start=True, stop=True):
                return nc.tensor.matmul(out, lhsT, rhs, start=start, stop=stop)

            def score(b, par, o, s, js=range(QUAD)):
                if s == 0 and js[0] == 0:
                    pe.wait_ge(stack_loaded[par][o], 16 * LOADS * (b // 2 + 1) if isinstance(b, int) else 8 * LOADS * (b - par + 2))
                for j in js:
                    u = s * QUAD + j
                    h, t = o * OCT + u // NT, u % NT
                    ge(pe, s_free, readers(par, o, b, u))
                    mm(s_bank[slot(par, o, u)], qs[:, par, h, t * P:(t + 1) * P], ks[:, par, h, :]).then_inc(s_full, 1)

            def shifted(b, par, o, s, js):
                if s == 0 and js[0] == 0:
                    pe.wait_ge(m_loaded[o], 16 * (b + 1))
                t = s % NT
                for j in js:
                    h = o * OCT + s // NT * QUAD + j
                    if j != 2:
                        ge(pe, exp_done, readers(par, o, b, s * QUAD + j))
                    mm(e_bank[slot(par, o, s * QUAD + j)], ks[:, par, h, t * P:(t + 1) * P], qs[:, par, h, :]).then_inc(e_full, 1)

            def values(b, par, o, s):
                g = (2 * b + o) * STEPS + s
                t = s % NT
                if o == 0 and s == 0:
                    pe.wait_ge(v_ready, b + 1)
                if t == 0:
                    ge(pe, o_kept, (2 * b + o) * 2 + s // NT)
                pe.wait_ge(exp_done, (g + 1) * QUAD)
                for j in range(QUAD):
                    h = o * OCT + s // NT * QUAD + j
                    last = mm(o_bank[j * VW:(j + 1) * VW, :], vw[:, par, t, h, :], probs[:, s % 2, j, :],
                              start=(t == 0), stop=(t == NT - 1))
                last.then_inc(av_done, 1)

            def transposes(src, full):
                for t in range(NT):
                    last = nc.tensor.transpose(misc[:, t * P:(t + 1) * P], src(t), ident[:, :])
                last.then_inc(full, 1)

            def transpose_maxima(b, o, before, count):
                n = 2 * b + o
                ge(pe, before, count)
                pe.wait_ge(m_split, n + 1)
                nc.tensor.transpose(misc.bitcast(BF16)[:, 0:P], mhl[:, o, :, :].rearrange("p c u -> p (c u)"),
                                    identb[:, :]).then_inc(mt_full, 1)

            def transpose_products(b, quad, before, count):
                ge(pe, before, count)
                pe.wait_ge(o_kept, QUAD * b + quad + 1)
                transposes(lambda t: oT[:, quad % 2, t * P:(t + 1) * P], ot_full)

            def transpose_attention(b):
                pe.wait_ge(ot_free, QUAD * (b + 1))
                transposes(lambda t: att[:, t, :], at_full)

            def project(b):
                pe.wait_ge(w_loaded, 32)
                pe.wait_ge(at_free, b + 1)
                mm(misc, wproj[:, :], attT[:, :]).then_inc(pj_full, 1)

            def transpose_sum(b):
                pe.wait_ge(pj_free, b + 1)
                transposes(lambda t: x1T[:, t * P:(t + 1) * P], xt_full)

            pe.wait_ge(filled, 1)

            def first():
                for s in range(EARLY // QUAD, STEPS):
                    score(0, 0, 0, s)
                transpose_maxima(0, 0, mt_free, 0)
                for s in range(LEAD):
                    score(0, 0, 1, s)

            def octet(b, pb, o, more1, more2):
                begin = isinstance(b, int) and b == 0 and o == 0
                n = 2 * b + o
                for s in range(STEPS):
                    for j in range(QUAD):
                        if s < STEPS - LEAD:
                            if more1:
                                score(b + o, (pb + o) % 2, 1 - o, s + LEAD, [j])
                        elif more2:
                            score(b + 1, 1 - pb, o, s + LEAD - STEPS, [j])
                        shifted(b, pb, o, s, [j])
                        if j == 1:
                            if s > 0:
                                values(b, pb, o, s - 1)
                            elif not begin:
                                values(b - 1 + o, (pb + 1 + o) % 2, 1 - o, STEPS - 1)
                    if s == 1 and not begin:
                        transpose_products(b - 1 + o, 3 if o == 0 else 1, ot_free, 2 * n - 1)
                    if o == 0 and not begin:
                        if s == 2:
                            transpose_attention(b - 1)
                        if s == 3:
                            project(b - 1)
                        if s == 4:
                            transpose_sum(b - 1)
                    if s == 5 and more1:
                        if o == 1:
                            transpose_maxima(b + o, 1 - o, ot_free, 2 * n)
                        elif begin:
                            transpose_maxima(b, 1, mt_free, 1)
                        else:
                            transpose_maxima(b, 1, xt_free, b)
                    if s == 6:
                        if more1:
                            transpose_products(b, 2 * o, mt_free, n + 2)
                        else:
                            transpose_products(b, 2 * o, ot_free, 2 * n)

            def last():
                values(NB - 1, 1, 1, STEPS - 1)
                transpose_products(NB - 1, 3, ot_free, QUAD * NB - 1)
                transpose_attention(NB - 1)
                project(NB - 1)
                transpose_sum(NB - 1)

            rounds(pe, first, octet, last)


def second_layer(nc, ctx, m):
    sb = lambda n, s, d=F32: ctx.enter_context(nc.sbuf_tensor(n, s, d))
    sem = lambda n: ctx.enter_context(nc.semaphore(n))
    x_all, ident, w1, w2, rms = m["x_all"], m["ident"], m["w1"], m["w2"], m["rms"]
    out = m["out"]
    NE, NSH = 16, 2
    NRT = NE - NSH
    HID = 2
    NKNOT = NB + 1
    ND = H * NKNOT
    SD = ND + NRT
    HT = H * NB

    hT_all = sb("hT_all", [P, NTILE * P])
    hT_high, hT_low = sb("hT_high", [P, NTOK], F32R), sb("hT_low", [P, NTOK], F32R)
    w1_high, w1_low = sb("w1_high", [P, NE * HID * P], F32R), sb("w1_low", [P, NE * HID * P], F32R)
    qkv = sb("qkv_all", [P, NTILE, 3 * P])
    dl = sb("dl_all", [P, NTILE, SD])
    gate = sb("gate_all", [P, NTILE, NRT])
    wqkv = sb("wqkv1", [P, 3 * P])
    wside = sb("wside", [P, SD])
    bqkv = sb("bqkv", [P, 3 * P])
    bside = sb("bside", [P, SD])
    bqc = sb("bqc", [P, 1])
    pe_rows = sb("pe_rows", [P, NKNOT])
    knots = sb("knots", [P, NKNOT])
    blockm = sb("blockm", [P, H])
    wo = sb("wo", [P, P])
    bo = sb("bo", [P, P])
    stats, mv = sb("stats2", [P, NT, 6]), sb("mv2", [P, NT, 2])
    ve, sd, r0, nt_, rstd = (sb(n, [P, NT]) for n in ("ve2", "sd2", "r02", "nt2", "rstd2"))
    norms, xnT, sq = sb("norms", [P, 2 * NT, P]), sb("xnT2", [P, NTOK]), sb("sq", [P, P])
    xn, xh = norms[:, 0:NT, :], norms[:, NT:2 * NT, :]
    ms = sb("ms", [P, NT])
    lmax, ld, lex, lsum = sb("lmax", [P, NT]), sb("ld", [P, NT, NRT]), sb("lex", [P, NT, NRT]), sb("lsum", [P, NT])
    top, rest = sb("top", [P, NT, 8]), sb("rest", [P, NT, NRT])
    hid = sb("hid", [P, 2, HID, NTOK])
    scaled = sb("scaled", [P, 2, NTOK])
    prodv = norms[:, :, :].rearrange("p t d -> p (t d)")
    at = HT * HD
    prod = [w1[:, k * at:(k + 1) * at] for k in range(3)]
    pos, sc, lg = (t.rearrange("p (s h t) -> p s h t", s=NB, h=H) for t in (w1[:, 3 * at:4 * at], hT_all[:, 0:at], hT_all[:, at:2 * at]))
    minus = sb("minus", [P, NB])
    smx = sb("smx", [P, NB, H])
    lgf = lg[:, :, :, :].rearrange("p s h t -> p (s h t)")
    wqT, bqw = lgf[:, 0:P], lgf[:, P:2 * P]
    pe_blk = lgf[:, 2 * P:2 * P + ND].rearrange("p (h n) -> p h n", h=H)
    ramps = sb("ramps", [P, HT * (NB - 3 + NB - 4) + HT * (NB - 2)])
    ao = ramps[:, 0:NB * P].rearrange("p (s d) -> p s d", s=NB)
    aoT = xnT

    banks = ctx.enter_context(nc.psum_tensor("banks2", [P, 8, NTOK], F32))
    a_bank = [banks[:, 0:2, :], banks[:, 2:4, :]]
    w_bank = [banks[:, 4, :], banks[:, 5, :]]
    misc = [banks[:, 6, :], banks[:, 7, :]]

    w_loaded, knots_done, blk_ready = sem("w_loaded2"), sem("knots_done"), sem("blk_ready")
    passed, pool_passed = sem("passed2"), sem("pool_passed")
    side_full, side_ready = sem("side_full"), sem("side_ready")
    stats_ready, sd_ready, xn_ready, ms_ready, ve2_ready, sd2_ready, xh_ready, dve_prep, dve_routing = (
        sem(n) for n in ("stats_ready2", "sd_ready2", "xn_ready2", "ms_ready", "msv_ready", "sdr_ready", "xh_ready", "dve_prep2",
                         "dve_routing2"))
    misc_full, misc_free = [sem("misc_full0"), sem("misc_full1")], [sem("misc_free0"), sem("misc_free1")]
    ld_ready, lex_ready, gate_ready = sem("ld_ready"), sem("lex_ready"), sem("gate_ready")
    a_full, hid_ready, w_full, added = sem("a_full"), sem("hid_ready"), sem("w_full"), sem("added")
    scaled_left, scaled_right, shared_added = sem("scaled_left"), sem("scaled_right"), sem("shared_added")
    ramp_ready, own_made, own_summed, lg_done = sem("ramp_ready"), sem("own_made"), sem("own_summed"), sem("lg_done")
    knot_done, in_high, in_split, weight_high, weight_split = (sem("knot_done"), sem("in_high"), sem("in_split"),
                                                               sem("weight_high"), sem("weight_split"))
    prod_ready, prod_free = [sem("qprod_ready"), sem("vprod_ready")], [sem("qprod_free"), sem("vprod_free")]
    pos_ready, lgm_ready, ex_ready, pr_ready, dve_att = (
        sem(n) for n in ("sig_ready", "lgm_ready", "ex_ready2", "pr_ready", "dve_att"))
    sum_ready, out_done = sem("sum_ready"), sem("out_done")
    NW = 9
    PUSES = 1 + NT
    AUSES = 2
    POOL_MUL = 5
    OWN = NB - POOL_MUL
    OWN_ORDER = [(0, 5), (1, 5), (0, 6), (1, 6), (1, 7), (0, 7)]
    PRODS = 3
    last_in = lambda k: max(s for s in range(POOL_MUL) if s % PRODS == k) + 1
    SCORES_MUL, SCORES_SUM = {1: 0, 2: 1, 4: 2, 5: 3, 7: 4}, {2: (5,), 3: (0,), 4: (1,), 6: (2,), 7: (3,), 9: (4,), 11: (6,), 14: (7,)}
    FIRST_SUM = {8: (5,), 9: (6,), 10: (0,), 11: (1,), 12: (2,), 13: (3,), 14: (4,), 15: (7,)}
    VALUES_MUL, VALUES_SUM = {9: 0, 10: 1, 11: 2, 12: 3, 14: 4}, {10: (5,), 12: (0, 6), 13: (1, 7), 14: (2,), 15: (3, 4)}
    KNOTS, RAMPS = {3: (1,), 4: (2,), 5: (3, 4), 6: (5, 6, 7)}, {2: (1, 2), 4: (3, 4), 5: (5, 6, 7)}
    SOONER = 2
    LAST_KNOTS, LAST_RAMPS = {2: (1,), 3: (2,), 4: (3, 4), 5: (5, 6, 7)}, {2: (1, 2), 3: (3, 4), 4: (5, 6, 7)}

    def own_before(g, kind, s):
        if isinstance(g, int) and (g == NT - 1 if kind else g == 0):
            return 2 * OWN * g + (OWN if kind else 0) + s - POOL_MUL
        return 2 * OWN * g + (OWN if kind else -OWN) + OWN_ORDER.index((kind, s))

    def tok(t, b, at=0, n=NTOK):
        return t[:, bass.ds(b * NTOK + at, n)]

    def ge(eng, s, value):
        if not isinstance(value, int) or value > 0:
            eng.wait_ge(s, value)

    def rounds(eng, first, left, right, last):
        first()
        left(0, 1, 2)
        with eng.Fori(1, NB // 2 - 1) as c:
            left(c, 2 * c + 1, 2 * c + 2)
        left(NB // 2 - 1, NB - 1, None)
        right(NB // 2, 0)
        with eng.Fori(1, NT - 1) as g:
            right(g + NB // 2, g)
        right(NB - 1, NT - 1)
        last()

    def up_weights(w, i):
        e = (i + NRT) % NE
        return w[:, e * HID * P:(e + 1) * HID * P]

    def ramp(n):
        w = NB - n
        second = HT * (NB - 3 + NB - 4)
        at = {1: 0, 3: 0, 4: HT * (NB - 3), 2: second, 5: second, 6: second + HT * (NB - 5), 7: second + HT * (NB - 5 + NB - 6)}[n]
        return ramps[:, at:at + HT * w].rearrange("p (s h t) -> p s h t", s=NB, h=H)

    def group(t, g, lo, hi):
        v = t[:, :, :].rearrange("p (s g) c -> p g s c", g=NT)
        return v[:, bass.ds(g, 1), :, lo:hi].rearrange("p a s c -> p (a s) c")

    def factors(g, s, kind):
        if kind == 0:
            q = group(qkv, g, 0, P)[:, s, :].rearrange("p (h d) -> p h d", h=H)[:, :, None, :].broadcast_to([P, H, NB, HD])
            k = group(qkv, g, P, 2 * P).rearrange("p t (h d) -> p h t d", h=H)
            return q, k
        w = lg[:, s, :, None, :].broadcast_to([P, H, HD, NB])
        v = group(qkv, g, 2 * P, 3 * P).rearrange("p t (h d) -> p h d t", h=H)
        return w, v

    with nc.Block() as block:
        @block.sync
        def _(sp):
            for dst, name in ((wqT, "wqT"), (bqc, "bqc"), (pe_rows, "pe_rows"), (blockm, "blockm"), (wqkv, "wqkv1"), (wo, "wo")):
                sp.dma_start(dst[:, :], m[name + "_d"]).then_inc(w_loaded, 16)
            sp.dma_start(wside[:, ND:SD], m["router_d"]).then_inc(w_loaded, 16)
            sp.dma_start(bqkv[:, :], m["bqkv_d"].broadcast_to([P, 3 * P])).then_inc(w_loaded, 16)
            sp.dma_start(bo[:, :], m["bo_d"].broadcast_to([P, P])).then_inc(w_loaded, 16)
            x = x_all[:, :].rearrange("p (s g d) -> p s g d", s=NB, g=NT)

            def store(n, s, count, g0, g1):
                sp.wait_ge(sum_ready, n)
                for k in range(s, s + count):
                    sp.dma_start(out[k, :, g0:g1, :], x[:, k, g0:g1, :]).then_inc(out_done, 16)

            for s in range(NB - 1):
                store(s + 1, s, 1, 0, NT - 1)
            store(NB, 0, NB // 2, NT - 1, NT)
            store(NB + 1, NB - 1, 1, 0, NT - 1)
            store(NB + 2, NB // 2, NB // 2, NT - 1, NT)
            sp.wait_ge(out_done, 16 * 2 * NB)

        @block.gpsimd
        def _(pool):
            def add(c, i, ready, base):
                n = c * NRT + i - NSH
                wait_apart(pool, ready, n + 1 - base, pool_passed)
                pool.tensor_tensor(tok(x_all, c), tok(x_all, c), scaled[:, i % 2, :], ALU.add).then_inc(added, 1)
                wait_apart(pool, added, n + 1, pool_passed)

            def multiply(g, s, kind):
                at = last_in(s % PRODS)
                first, final = isinstance(g, int) and g == 0, isinstance(g, int) and g == NT - 1
                if s >= PRODS:
                    wait_apart(pool, prod_free[kind], POOL_MUL * g + s - PRODS + 1, pool_passed)
                elif kind == 1:
                    wait_apart(pool, prod_free[1 if final else 0], POOL_MUL * (g - 1 if final else g + 1) + at, pool_passed)
                elif isinstance(g, int) and g == 1:
                    wait_apart(pool, prod_free[0], at, pool_passed)
                elif not first:
                    wait_apart(pool, prod_free[1], POOL_MUL * (g - 2) + at, pool_passed)
                o = prod[s % PRODS].rearrange("p (h a b) -> p h a b", h=H, a=NB)
                pool.tensor_tensor(o, *factors(g, s, kind), ALU.mult).then_inc(prod_ready[kind], 1)

            def left(c, b1, b2):
                for i in range(NE):
                    if i >= NSH:
                        add(c, i, scaled_left, 0)
                    if b2 is None and 8 <= i < 8 + POOL_MUL:
                        if i == 8:
                            pool.wait_ge(misc_free[0], PUSES * NB)
                        multiply(0, i - 8, 0)

            def right(c, g):
                final = isinstance(g, int) and g == NT - 1
                for i in range(NE):
                    if i in SCORES_MUL and not final:
                        multiply(g + 1, SCORES_MUL[i], 0)
                    v = i + SOONER if final else i
                    if v in VALUES_MUL:
                        if VALUES_MUL[v] == 0:
                            wait_apart(pool, pr_ready, g + 1, pool_passed)
                        multiply(g, VALUES_MUL[v], 1)
                    if i >= NSH:
                        add(c, i, scaled_right, NRT * NB // 2)

            rounds(pool, lambda: None, left, right, lambda: None)

        @block.vector
        def _(v):
            own = Chain(v, dve_prep, 13 + 5 + 1)
            routing = Chain(v, dve_routing, 17)
            att = Chain(v, dve_att, (NB - 1) + 2 * (NB - 1) + 3 + 1 + 2)

            def inverse_root(src, done):
                v.wait_ge(*done)
                own.link(v.reciprocal(r0[:, :], sd[:, :]))
                own.link(v.tensor_tensor(nt_[:, :], r0[:, :], r0[:, :], ALU.mult))
                own.link(v.tensor_tensor(nt_[:, :], nt_[:, :], src[:, :], ALU.mult))
                own.link(v.tensor_scalar(nt_[:, :], nt_[:, :], -0.5, 1.5, ALU.mult, ALU.add))
                own.link(v.tensor_tensor(rstd[:, :], r0[:, :], nt_[:, :], ALU.mult))

            def norm(b):
                own.round(b)
                for t in range(NT):
                    done = own.mark(v.bn_stats(stats[:, t, :], tok(x_all, b, t * P, P)))
                wait_apart(v, dve_prep, done, passed)
                for t in range(NT):
                    done = own.mark(v.bn_aggr(mv[:, t, :], stats[:, t, :]))
                own.wait(done)
                v.tensor_scalar(ve[:, :], mv[:, :, 1], LN_EPS, None, ALU.add).then_inc(stats_ready, 1)

            def make_norm(b):
                inverse_root(ve, (sd_ready, b + 1))
                ge(v, misc_full[0], PUSES * (b - 1) + 1)
                for t in range(NT):
                    ins = v.tensor_scalar(xn[:, t, :], tok(x_all, b, t * P, P), mv[:, t, 0:1], rstd[:, t:t + 1],
                                          ALU.subtract, ALU.mult)
                ins.then_inc(xn_ready, 1)

            def mean_squares(b):
                v.wait_ge(ms_ready, NT * (b + 1))
                v.tensor_scalar(ve[:, :], ms[:, :], 1.0 / P, RMS_EPS, ALU.mult, ALU.add).then_inc(ve2_ready, 1)

            def root_mean_square(b):
                inverse_root(ve, (sd2_ready, b + 1))
                ge(v, misc_full[1], PUSES * (b - 1) + 1)
                for t in range(NT):
                    ins = v.tensor_scalar(xh[:, t, :], xn[:, t, :], rstd[:, t:t + 1], None, ALU.mult)
                ins.then_inc(xh_ready, 1)

            def keep_projections(b, t):
                v.wait_ge(misc_full[0], PUSES * b + 2 + t)
                v.tensor_tensor(qkv[:, bass.ds(b * NT + t, 1), :].rearrange("p a c -> p (a c)"), misc[0][:, 0:3 * P], bqkv[:, :], ALU.add)\
                    .then_inc(misc_free[0], 1)
                v.wait_ge(misc_full[1], PUSES * b + 2 + t)
                v.tensor_tensor(dl[:, bass.ds(b * NT + t, 1), :].rearrange("p a c -> p (a c)"), misc[1][:, 0:SD], bside[:, :], ALU.add)\
                    .then_inc(misc_free[1], 1)

            def logits(b):
                v.wait_ge(misc_free[1], PUSES * (b + 1))
                l = dl[:, bass.ds(b * NT, NT), ND:SD]
                own.link(v.tensor_reduce(lmax[:, :], l, AX.X, ALU.max))
                v.tensor_tensor(ld[:, :, :], l, lmax[:, :, None].broadcast_to([P, NT, NRT]), ALU.subtract).then_inc(ld_ready, 1)
                own.end()

            wide = lambda t: t[:, :, None].broadcast_to([P, NT, NRT])

            def choose(b):
                routing.round(b)
                v.wait_ge(lex_ready, b + 1)
                routing.link(v.tensor_reduce(lsum[:, :], lex[:, :, :], AX.X, ALU.add))
                routing.link(v.reciprocal(lsum[:, :], lsum[:, :]))
                routing.link_apart(v.tensor_tensor(lex[:, :, :], lex[:, :, :], wide(lsum), ALU.mult), passed)
                for t in range(NT):
                    done = routing.mark(v.max(top[:, t, :], lex[:, t, :]))
                routing.wait(done)

            def weigh(b):
                routing.link_apart(v.memset(top[:, :, 2:8], LARGE), passed)
                for t in range(NT):
                    done = routing.mark(v.match_replace(rest[:, t, :], top[:, t, :], lex[:, t, :], -LARGE))
                routing.wait(done)
                routing.link(v.tensor_tensor(rest[:, :, :], rest[:, :, :], lex[:, :, :], ALU.not_equal))
                routing.link(v.tensor_tensor(lex[:, :, :], lex[:, :, :], rest[:, :, :], ALU.mult))
                routing.link(v.tensor_reduce(lsum[:, :], lex[:, :, :], AX.X, ALU.add))
                routing.link(v.tensor_scalar(lsum[:, :], lsum[:, :], 1e-9, None, ALU.add))
                routing.link(v.reciprocal(lsum[:, :], lsum[:, :]))
                v.tensor_tensor(gate[:, bass.ds(b * NT, NT), :], lex[:, :, :], wide(lsum), ALU.mult).then_inc(gate_ready, 1)
                routing.end()

            def add_shared(c, i):
                v.wait_ge(w_full, c * NE + i + 1)
                if i == 1:
                    v.wait_ge(shared_added, NSH * c + 1)
                v.tensor_tensor(tok(x_all, c), w_bank[i % 2], tok(x_all, c), ALU.add).then_inc(shared_added, 1)

            def split_input(c):
                v.wait_ge(in_high, c + 1)
                if not isinstance(c, int) or c > 0:
                    v.wait_ge(a_full, NE * c)
                v.tensor_tensor(hT_low[:, :], tok(hT_all, c), hT_high[:, :].bitcast(F32), ALU.subtract).then_inc(in_split, 1)

            def split_weights(i):
                v.wait_ge(weight_high, i + 1)
                v.tensor_tensor(up_weights(w1_low, i), up_weights(w1, i), up_weights(w1_high, i).bitcast(F32), ALU.subtract)\
                    .then_inc(weight_split, 1)

            def scale_routed(c, i):
                e = i - NSH
                v.wait_ge(w_full, c * NE + i + 1)
                if i == NSH:
                    v.wait_ge(gate_ready, c + 1)
                ge(v, added, c * NRT + e - 1)
                g = gate[:, bass.ds(c * NT, NT), e:e + 1].broadcast_to([P, NT, P])
                v.tensor_tensor(scaled[:, i % 2, :].rearrange("p (t d) -> p t d", t=NT),
                                w_bank[i % 2].rearrange("p (t d) -> p t d", t=NT), g, ALU.mult).then_inc(scaled_left, 1)

            def reduce_products(g, s, kind):
                o = sc[:, s, :, :] if kind == 0 else ao[:, s, :].rearrange("p (h d) -> p h d", h=H)
                if s < POOL_MUL:
                    v.wait_ge(prod_ready[kind], POOL_MUL * g + s + 1)
                    v.tensor_reduce(o, prod[s % PRODS].rearrange("p (h a b) -> p h a b", h=H, a=NB), AX.X, ALU.add)\
                        .then_inc(prod_free[kind], 1)
                else:
                    n = own_before(g, kind, s)
                    ge(v, own_summed, n)
                    p = prodv.rearrange("p (h a b) -> p h a b", h=H, a=NB)
                    v.tensor_tensor(p, *factors(g, s, kind), ALU.mult).then_inc(own_made, 1)
                    v.wait_ge(own_made, n + 1)
                    v.tensor_reduce(o, p, AX.X, ALU.add).then_inc(own_summed, 1)

            def positions(g):
                v.wait_ge(pos_ready, g + 1)
                for t in range(NB - 2, -1, -1):
                    done = att.mark(v.tensor_tensor(pos[:, :, :, t], pos[:, :, :, t], pos[:, :, :, t + 1], ALU.add))
                    att.wait(done)
                v.sem_inc(lg_done, 1)
                att.link(v.tensor_tensor(lg[:, :, :, :], sc[:, :, :, :], group_knots(g, 0)[:, :, :, None].broadcast_to([P, NB, H, NB]),
                                         ALU.add))

            def first_slope(g):
                D0 = group_knots(g, 1)
                v.wait_ge(ramp_ready, (NB - 1) * (g + 1))
                att.link(v.tensor_tensor(pos[:, :, :, :], pos[:, :, :, :], D0[:, :, :, None].broadcast_to([P, NB, H, NB]), ALU.mult))
                att.link(v.tensor_tensor(lg[:, :, :, :], lg[:, :, :, :], pos[:, :, :, :], ALU.add))

            def group_knots(g, n):
                return group(dl, g, 0, ND).rearrange("p s (h n) -> p s h n", n=NKNOT)[:, :, :, n]

            def knot(g, n):
                w = NB - n
                r = ramp(n)
                D = group_knots(g, n + 1)[:, :, :, None].broadcast_to([P, NB, H, w])
                v.wait_ge(ramp_ready, (NB - 1) * g + n)
                att.link(v.tensor_tensor(r, r, D, ALU.mult))
                att.link(v.tensor_tensor(lg[:, :, :, 0:w], lg[:, :, :, 0:w], r, ALU.add))
                v.sem_inc(knot_done, 1)

            def subtract_maximum(g):
                att.link(v.tensor_reduce(smx[:, :, :], lg[:, :, :, :], AX.X, ALU.max))
                v.tensor_tensor(lg[:, :, :, :], lg[:, :, :, :], smx[:, :, :, None].broadcast_to([P, NB, H, NB]), ALU.subtract)\
                    .then_inc(lgm_ready, 1)

            def normalize(g):
                v.wait_ge(ex_ready, g + 1)
                att.link(v.tensor_reduce(smx[:, :, :], lg[:, :, :, :], AX.X, ALU.add))
                att.link(v.reciprocal(smx[:, :, :], smx[:, :, :]))
                v.tensor_tensor(lg[:, :, :, :], lg[:, :, :, :], smx[:, :, :, None].broadcast_to([P, NB, H, NB]), ALU.mult)\
                    .then_inc(pr_ready, 1)
                v.wait_ge(pr_ready, g + 1)

            def keep_attention(g, half):
                v.wait_ge(misc_full[half], PUSES * NB + AUSES * (g + 1))
                o = group(qkv, g, 0, P)[:, half * NT:(half + 1) * NT, :]
                v.tensor_tensor(o, misc[half].rearrange("p (s d) -> p s d", s=NT), bo[:, None, :].broadcast_to([P, NT, P]), ALU.add)\
                    .then_inc(misc_free[half], 1)

            def prepare(b, i):
                if i == 0:
                    norm(b)
                elif i == 1:
                    make_norm(b)
                elif i == 2:
                    mean_squares(b)
                elif i == 3:
                    root_mean_square(b)
                elif i == 4:
                    keep_projections(b, 0)
                elif i == 5:
                    keep_projections(b, 1)
                elif i == 6:
                    keep_projections(b, 2)
                elif i == 7:
                    keep_projections(b, 3)
                    logits(b)

            def side_weights():
                v.wait_ge(w_loaded, 16 * NW)
                def setup(k, ins):
                    ins.then_inc(knots_done, 1)
                    v.wait_ge(knots_done, k)
                setup(1, v.tensor_copy(knots[:, 0:1], pe_rows[:, 0:1]))
                setup(2, v.tensor_tensor(knots[:, 1:], pe_rows[:, 1:], pe_rows[:, 0:NKNOT - 1], ALU.subtract))
                setup(3, v.tensor_copy(pe_rows[:, 1:], knots[:, 1:]))
                setup(4, v.tensor_tensor(knots[:, 2:], pe_rows[:, 2:], pe_rows[:, 1:NKNOT - 1], ALU.subtract))
                setup(5, v.tensor_scalar(knots[:, :], knots[:, :], 1.0 / SCALE, None, ALU.mult))
                v.tensor_tensor(pe_blk[:, :, :], knots[:, None, :].broadcast_to([P, H, NKNOT]), blockm[:, :, None].broadcast_to([P, H, NKNOT]),
                                ALU.mult).then_inc(blk_ready, 1)
                v.memset(bside[:, ND:SD], 0.0)
                for n in range(NB):
                    v.memset(minus[:, n:n + 1], -float(n))
                v.tensor_copy(bqw[:, :], bqc[:, 0:1].broadcast_to([P, P])).then_inc(blk_ready, 1)

            def keep_side_weights():
                v.wait_ge(side_full, 2)
                v.tensor_copy(wside[:, 0:ND], misc[0][:, 0:ND]).then_inc(side_ready, 1)
                v.tensor_copy(bside[:, 0:ND], misc[1][:, 0:ND]).then_inc(side_ready, 1)

            def first():
                for i in range(8):
                    prepare(0, i)
                    if i == 1:
                        side_weights()
                    if i == 3:
                        keep_side_weights()
                    if i == 4:
                        split_input(0)
                        for j in range(NSH):
                            split_weights(j)

            def left(c, b1, b2):
                begin = isinstance(c, int) and c == 0
                for i in range(NE):
                    if begin and i + NSH < NE:
                        split_weights(i + NSH)
                    if i == NE - 1:
                        split_input(c + 1)
                    if i < 8:
                        if i == (0 if begin else 5):
                            choose(2 * c)
                        if i == (1 if begin else 6):
                            weigh(2 * c)
                        prepare(b1, i)
                    else:
                        if i == 13:
                            choose(b1)
                        if i == 14:
                            weigh(b1)
                        if b2 is not None:
                            prepare(b2, i - 8)
                        else:
                            for s in FIRST_SUM[i]:
                                reduce_products(0, s, 0)
                    if i < NSH:
                        add_shared(c, i)
                    else:
                        scale_routed(c, i)

            def right(c, g):
                first, final = isinstance(g, int) and g == 0, isinstance(g, int) and g == NT - 1
                att.round(g)
                for i in range(NE):
                    if i < NSH:
                        add_shared(c, i)
                    if i == 1:
                        positions(g)
                    if i == 3 and not first:
                        keep_attention(g - 1, 0)
                        keep_attention(g - 1, 1)
                    for n in (LAST_KNOTS if final else KNOTS).get(i, ()):
                        knot(g, n)
                    if not final and i < 9:
                        for s in SCORES_SUM.get(i, ()):
                            reduce_products(g + 1, s, 0)
                    late = i + SOONER if final else i
                    if late == 7:
                        first_slope(g)
                    if late == 8:
                        subtract_maximum(g)
                    if late == 9:
                        normalize(g)
                    if i == NE - 1 and not final:
                        split_input(c + 1)
                    for s in VALUES_SUM.get(late, ()):
                        reduce_products(g, s, 1)
                    if not final and i >= 9:
                        for s in SCORES_SUM.get(i, ()):
                            reduce_products(g + 1, s, 0)
                att.end()
                if final:
                    v.wait_ge(added, NRT * (NB - 1))
                    for g in range(NT - 1):
                        v.wait_ge(misc_free[1], PUSES * NB + AUSES * (g + 1))
                    for s in range(NB - 1):
                        add_attention(s, 1, 0, NT - 1)

            def add_attention(s, n, g0, g1):
                x = x_all[:, :].rearrange("p (s g d) -> p s g d", s=NB, g=NT)[:, s:s + n, g0:g1, :]
                a = qkv[:, :, 0:P].rearrange("p (s g) d -> p s g d", g=NT)[:, s:s + n, g0:g1, :]
                v.tensor_tensor(x, x, a, ALU.add).then_inc(sum_ready, 1)

            def last():
                keep_attention(NT - 1, 0)
                v.wait_ge(misc_free[0], PUSES * NB + AUSES * NT)
                add_attention(0, NB // 2, NT - 1, NT)
                keep_attention(NT - 1, 1)
                v.wait_ge(added, NRT * NB)
                add_attention(NB - 1, 1, 0, NT - 1)
                v.wait_ge(misc_free[1], PUSES * NB + AUSES * NT)
                add_attention(NB // 2, NB // 2, NT - 1, NT)

            rounds(v, first, left, right, last)

        @block.scalar
        def _(act):
            def deviation(b):
                act.wait_ge(stats_ready, b + 1)
                act.activation(sd[:, :], ve[:, :], ACT.Sqrt).then_inc(sd_ready, 1)

            def squares(b):
                act.wait_ge(xn_ready, b + 1)
                for t in range(NT):
                    ge(act, ms_ready, NT * b + t)
                    act.activation(sq[:, :], xn[:, t, :], ACT.Square, accum_out=ms[:, t:t + 1]).then_inc(ms_ready, 1)

            def root_mean_square(b):
                act.wait_ge(ve2_ready, b + 1)
                act.activation(sd[:, :], ve[:, :], ACT.Sqrt).then_inc(sd2_ready, 1)

            def keep_norm(b):
                act.wait_ge(misc_full[0], PUSES * b + 1)
                act.activation(xnT[:, :], misc[0], ACT.Copy).then_inc(misc_free[0], 1)

            def keep_hidden_input(b):
                act.wait_ge(misc_full[1], PUSES * b + 1)
                act.activation(tok(hT_all, b), misc[1], ACT.Copy).then_inc(misc_free[1], 1)

            def high_input(c):
                act.wait_ge(misc_free[1], PUSES * c + 1)
                act.activation(hT_high[:, :], tok(hT_all, c), ACT.Copy).then_inc(in_high, 1)

            def high_weights(i):
                act.activation(up_weights(w1_high, i), up_weights(w1, i), ACT.Copy).then_inc(weight_high, 1)

            def exponentials(b):
                act.wait_ge(ld_ready, b + 1)
                act.activation(lex[:, :, :], ld[:, :, :], ACT.Exp).then_inc(lex_ready, 1)

            def silu(c, i):
                n = c * NE + i
                act.wait_ge(a_full, n + 1)
                ge(act, w_full, n - 1)
                act.activation(hid[:, i % 2, :, :], a_bank[i % 2], ACT.Silu).then_inc(hid_ready, 1)

            def prepare(b, i):
                if i == 0:
                    deviation(b)
                elif i == 1:
                    squares(b)
                elif i == 2:
                    root_mean_square(b)
                    keep_norm(b)
                elif i == 4:
                    keep_hidden_input(b)

            def scale_routed(c, i):
                e = i - NSH
                act.wait_ge(w_full, c * NE + i + 1)
                if i == NSH:
                    act.wait_ge(gate_ready, NB)
                act.wait_ge(added, c * NRT + e - 1)
                for t in range(NT):
                    last = act.activation(scaled[:, i % 2, t * P:(t + 1) * P], w_bank[i % 2][:, t * P:(t + 1) * P], ACT.Copy,
                                          scale=gate[:, bass.ds(c * NT + t, 1), e:e + 1].rearrange("p a b -> p (a b)"))
                last.then_inc(scaled_right, 1)

            def first():
                for i in range(8):
                    if i == 1:
                        for j in range(NSH):
                            high_weights(j)
                    prepare(0, i)
                    if i == 4:
                        high_input(0)
                exponentials(0)

            def left(c, b1, b2):
                begin = isinstance(c, int) and c == 0
                for i in range(NE):
                    silu(c, i)
                    if begin and i + NSH < NE:
                        high_weights(i + NSH)
                    if i == NE - 1:
                        high_input(c + 1)
                    if i == 4 and not begin:
                        exponentials(2 * c)
                    if i == 12:
                        exponentials(b1)
                    if i < 8:
                        prepare(b1, i)
                    elif b2 is not None:
                        prepare(b2, i - 8)

            def right(c, g):
                first, final = isinstance(g, int) and g == 0, isinstance(g, int) and g == NT - 1
                for i in range(NE):
                    silu(c, i)
                    if i == NE - 1 and not final:
                        high_input(c + 1)
                    if i == 0:
                        act.wait_ge(own_summed, 2 * OWN * g + OWN)
                        act.wait_ge(prod_free[0], POOL_MUL * (g + 1))
                        act.activation(pos[:, :, :, :], sc[:, :, :, :], ACT.Sigmoid, scale=SCALE).then_inc(pos_ready, 1)
                    if i == 2 and not first:
                        keep_transposed(g - 1, 0)
                        act.wait_ge(misc_full[1], PUSES * NB + AUSES * (g - 1) + 1)
                    if i == 3 and not first:
                        keep_transposed(g - 1, 1)
                    for n in (LAST_RAMPS if final else RAMPS).get(i, ()):
                        if n == 1:
                            act.wait_ge(lg_done, g + 1)
                        if n in (3, 5):
                            act.wait_ge(knot_done, (NB - 1) * g + n // 2)
                        act.activation(ramp(n), pos[:, :, :, 0:NB - n], ACT.Relu, bias=minus[:, n:n + 1]).then_inc(ramp_ready, 1)
                    if i == (9 - SOONER if final else 9):
                        act.wait_ge(lgm_ready, g + 1)
                        act.activation(lg[:, :, :, :], lg[:, :, :, :], ACT.Exp, scale=SCALE).then_inc(ex_ready, 1)
                    if i > NSH:
                        scale_routed(c, i - 1)
                if final:
                    keep_transposed(g, 0)
                scale_routed(c, NE - 1)

            def keep_transposed(g, half):
                act.wait_ge(misc_full[half], PUSES * NB + AUSES * g + 1)
                if half == 1:
                    act.wait_ge(misc_full[0], PUSES * NB + AUSES * (g + 1))
                act.activation(aoT[:, :], misc[half], ACT.Copy).then_inc(misc_free[half], 1)

            def last():
                keep_transposed(NT - 1, 1)

            rounds(act, first, left, right, last)

        @block.tensor
        def _(pe):
            def mm(o, lhsT, rhs, start=True, stop=True):
                return nc.tensor.matmul(o, lhsT, rhs, start=start, stop=stop)

            def transposes(k, src):
                for t in range(NT):
                    last = nc.tensor.transpose(misc[k][:, t * P:(t + 1) * P], src(t), ident[:, :])
                last.then_inc(misc_full[k], 1)

            def project(b, t):
                x = xnT[:, t * P:(t + 1) * P]
                pe.wait_ge(misc_free[0], PUSES * b + 1 + t)
                mm(misc[0][:, 0:3 * P], x, wqkv[:, :]).then_inc(misc_full[0], 1)
                pe.wait_ge(misc_free[1], PUSES * b + 1 + t)
                mm(misc[1][:, 0:SD], x, wside[:, :]).then_inc(misc_full[1], 1)

            def prepare(b, i, behind):
                if i == 2 and behind:
                    pe.wait_ge(xn_ready, b + 1)
                    ge(pe, misc_free[0], PUSES * b)
                    transposes(0, lambda t: xn[:, t, :])
                elif i == 4 and not behind:
                    pe.wait_ge(xh_ready, b + 1)
                    ge(pe, misc_free[1], PUSES * b)
                    transposes(1, lambda t: xh[:, t, :])
                elif i >= 4 and behind:
                    project(b, i - 4)

            def up(c, i):
                n = c * NE + i
                ge(pe, hid_ready, n - 1)
                if i == 0:
                    pe.wait_ge(in_split, c + 1)
                if isinstance(c, int) and c == 0:
                    pe.wait_ge(weight_split, i + 1)
                x_high, x_low = hT_high[:, :], hT_low[:, :]
                for k in range(HID):
                    o = a_bank[i % 2][:, k, :]
                    high, low = (up_weights(w, i)[:, k * P:(k + 1) * P] for w in (w1_high, w1_low))
                    mm(o, high, x_high, stop=False)
                    mm(o, high, x_low, start=False, stop=False)
                    last = mm(o, low, x_high, start=False)
                last.then_inc(a_full, 1)

            def down(c, i, right_half):
                e = (i + NRT) % NE
                n = c * NE + i
                pe.wait_ge(hid_ready, n + 1)
                half = NB // 2
                if i < NSH:
                    if isinstance(c, int) and c == half:
                        pe.wait_ge(scaled_left, NRT * (c - 1) + NRT - 1 + i)
                    elif right_half:
                        pe.wait_ge(scaled_right, NRT * (c - half - 1) + NRT - 1 + i)
                    else:
                        ge(pe, scaled_left, NRT * (c - 1) + NRT - 1 + i)
                elif i < 2 * NSH:
                    pe.wait_ge(shared_added, NSH * c + i - NSH + 1)
                elif right_half:
                    pe.wait_ge(scaled_right, NRT * (c - half) + i - 2 * NSH + 1)
                else:
                    pe.wait_ge(scaled_left, NRT * c + i - 2 * NSH + 1)
                for t in range(NT):
                    for k in range(HID):
                        last = mm(w_bank[i % 2][:, t * P:(t + 1) * P], hid[:, i % 2, k, t * P:(t + 1) * P],
                                  w2[:, (e * HID + k) * P:(e * HID + k + 1) * P], start=(k == 0), stop=(k == HID - 1))
                last.then_inc(w_full, 1)

            def side_weights():
                pe.wait_ge(w_loaded, 16 * NW)
                pe.wait_ge(blk_ready, 2)
                pe.wait_ge(misc_free[0], 1)
                blk = pe_blk[:, :, :].rearrange("p h n -> p (h n)")
                mm(misc[0][:, 0:ND], wqT[:, :], blk).then_inc(side_full, 1)
                mm(misc[1][:, 0:ND], bqw[:, :], blk).then_inc(side_full, 1)
                pe.wait_ge(side_ready, 2)

            def first():
                prepare(0, 2, True)
                side_weights()
                prepare(0, 4, False)
                project(0, 0)
                up(0, 0)
                project(0, 1)
                up(0, 1)
                project(0, 2)
                project(0, 3)

            def left(c, b1, b2):
                begin = isinstance(c, int) and c == 0
                if not begin:
                    up(c, 0)
                for i in range(NE):
                    b = b1 if i < 8 else b2
                    if b is not None:
                        prepare(b, i % 8, False)
                    if i + 1 < NE and not (begin and i == 0):
                        up(c, i + 1)
                    if b is not None:
                        prepare(b, i % 8, True)
                    down(c, i, False)

            def transpose_attention(g):
                pe.wait_ge(prod_free[1], POOL_MUL * (g + 1))
                final = isinstance(g, int) and g == NT - 1
                pe.wait_ge(own_summed, 2 * OWN * (g + 1) if final else 2 * OWN * g + OWN + OWN_ORDER.index((1, NB - 1)) + 1)
                for half in range(2):
                    pe.wait_ge(misc_free[half], PUSES * NB + AUSES * g)
                    transposes(half, lambda t: ao[:, half * NT + t, :])

            def project_attention(g, half):
                pe.wait_ge(misc_free[half], PUSES * NB + AUSES * g + 1)
                for t in range(NT):
                    last = mm(misc[half][:, t * P:(t + 1) * P], aoT[:, t * P:(t + 1) * P], wo[:, :])
                last.then_inc(misc_full[half], 1)

            def right(c, g):
                first, final = isinstance(g, int) and g == 0, isinstance(g, int) and g == NT - 1
                up(c, 0)
                for i in range(NE):
                    if i + 1 < NE:
                        up(c, i + 1)
                    if not first:
                        if i == 1:
                            transpose_attention(g - 1)
                        if i == 2:
                            project_attention(g - 1, 0)
                        if i == 3:
                            project_attention(g - 1, 1)
                    if final and i == NE - 1:
                        transpose_attention(g)
                    down(c, i, True)

            def last():
                project_attention(NT - 1, 0)
                project_attention(NT - 1, 1)

            rounds(pe, first, left, right, last)


def build(nc, m):
    with ExitStack() as ctx:
        sb = lambda n, s, d=F32: ctx.enter_context(nc.sbuf_tensor(n, s, d))
        m["ident"] = sb("ident", [P, P])
        m["rms"] = sb("rms", [P, E1])
        m["w1"] = sb("w1", [P, E1 * 2 * P])
        m["w2"] = sb("w2", [P, E1 * 2 * P])
        m["x_all"] = sb("x_all", [P, NTILE * P])
        with ExitStack() as first:
            sb1 = lambda n, s, d=F32: first.enter_context(nc.sbuf_tensor(n, s, d))
            m["v_all"] = sb1("v_all", [P, NTILE * P])
            m["yT_all"] = sb1("yT_all", [P, NTILE * P])
            m["qs"] = sb1("qs", [P, 2, H, NTOK], BF16)
            m["ks"] = sb1("ks", [P, 2, H, NTOK], BF16)
            m["zero"] = sb1("zero", [2, NTOK], BF16)
            m["one"] = sb1("one", [2, NTOK], BF16)
            m["vw"] = sb1("vw", [P, 2, NT, H, VW])
            m["qk_parts"] = nc.dram_tensor("qk_parts", [NB, 2, H, PARTS, HD, NTOK], BF16, kind="Internal").ap()
            m["mx"] = sb1("mx1", [P, 2, OCT * NT])
            m["s_full"], m["s_free"] = (first.enter_context(nc.semaphore(n)) for n in ("s_full", "s_free"))
            m["stack_loaded"] = [[first.enter_context(nc.semaphore(f"stack_loaded{p}{o}")) for o in range(2)] for p in range(2)]
            with ExitStack() as c:
                prepare_and_mix(nc, c, m)
            with ExitStack() as c:
                attend(nc, c, m)
        with ExitStack() as c:
            second_layer(nc, c, m)


def _laid_out(a):
    import numpy as np

    tile = lambda v: np.ascontiguousarray(v)
    ups = np.concatenate([a["L1_ffn_w1"], a["L1_ffn_w1_s"]])
    downs = np.concatenate([a["L1_ffn_w2"], a["L1_ffn_w2_s"]])
    row = np.arange(P)[:, None]
    weight = np.arange(2 * L)[None, :]
    return {
        "x": tile(a["L0_attn_x"].reshape(NB, NT, P, P).transpose(0, 2, 1, 3)),
        "ident": np.eye(P, dtype=np.float32),
        "selcol": ((row % (2 * L) == weight) & (row < PARTS * 2 * L)).astype(np.float32),
        "blockm": (row // HD == np.arange(H)[None, :]).astype(np.float32),
        "wqkv0": tile(a["L0_attn_w_qkv"]),
        "PwT": tile(a["L0_ffn_P_w"].T),
        "UT": tile(np.concatenate([a["L0_ffn_U1"], a["L0_ffn_U2"], a["L0_ffn_U3"]]).T),
        "W1T": tile(a["L0_ffn_W1"].transpose(2, 0, 1)),
        "W2T": tile(a["L0_ffn_W2"].transpose(2, 0, 1)),
        "b2": tile(a["L0_ffn_b2"]),
        "wproj": tile(a["L0_attn_w_proj"]),
        "bproj": tile(a["L0_attn_b_proj"].reshape(P, 1)),
        "wqT": tile(a["L1_attn_Wq"].T),
        "bqc": tile(a["L1_attn_bq"].reshape(P, 1)),
        "pe_rows": tile(np.tile(a["L1_attn_pos_emb"][0, :, :NB + 1], (H, 1))),
        "wqkv1": tile(np.concatenate([a["L1_attn_Wq"], a["L1_attn_Wk"], a["L1_attn_Wv"]], axis=1)),
        "bqkv": tile(np.concatenate([a["L1_attn_bq"], a["L1_attn_bk"], a["L1_attn_bv"]]).reshape(1, 3 * P)),
        "wo": tile(a["L1_attn_Wo"]),
        "bo": tile(a["L1_attn_bo"].reshape(1, P)),
        "router": tile(a["L1_ffn_router_w"]),
        "rms": tile(np.concatenate([a["L1_ffn_rms_w"], a["L1_ffn_rms_w_s"]]).T),
        "w1": tile(ups.transpose(1, 0, 2).reshape(P, -1)),
        "w2": tile(downs.reshape(E1, 2, P, P).transpose(2, 0, 1, 3).reshape(P, -1)),
    }


def kernel(**inputs):
    import numpy as np
    import concourse.bacc as bacc
    from concourse.bass_utils import run_bass_kernel_spmd

    laid = _laid_out({k: np.asarray(v) for k, v in inputs.items()})
    nc = bacc.Bacc("TRN2", target_bir_lowering=False, num_devices=1)
    m = {}
    for name, a in laid.items():
        ap = nc.dram_tensor(f"in_{name}", a.shape, mybir.dt.from_np(a.dtype), kind="ExternalInput").ap()
        m["x" if name == "x" else name + "_d"] = ap
    m["out"] = nc.dram_tensor("out", [NB, P, NT, P], F32, kind="ExternalOutput").ap()
    build(nc, m)
    r = run_bass_kernel_spmd(nc, [{f"in_{k}": a for k, a in laid.items()}], core_ids=[0])
    return np.asarray(r.results[0]["out"]).transpose(0, 2, 1, 3).reshape(NB, NTOK, P)
```
